# Optimizing a Trainium2 kernel written in Bass

```python
import numpy as np
import jax
import jax.numpy as jnp

def _softmax(x, axis=-1):
    return jax.nn.softmax(x, axis=axis)

def _gelu(x):
    return jax.nn.gelu(x, approximate=True)

def _silu(x):
    return jax.nn.silu(x)

def _sigmoid(x):
    return jax.nn.sigmoid(x)

def _layernorm(x, axis=-1, eps=1e-05):
    m = jnp.mean(x, axis=axis, keepdims=True)
    v = jnp.var(x, axis=axis, keepdims=True)
    return (x - m) / jnp.sqrt(v + eps)

def _scatter_add(tgt, idx, src, axis=0):
    return tgt.at[idx].add(src)

def _segment_sum(src, seg, n):
    return jax.ops.segment_sum(src, seg, n)
kernel_name = 'mk_macaron_d2_jaxref_r8_2b2589'

def setup_inputs(seed: int=0):
    np.random.seed(seed)
    _w = jnp.asarray

    def _L0_attn_setup():
        import jax, jax.numpy as jnp
        import numpy as np
        DIM = 128
        HID = int(DIM * 1.5)
        GHID = int(DIM * 2)
        K = 4
        ALPHA_LOG_SCALE = -8.0

        def _rmsnorm(x, gamma):
            n = jnp.linalg.norm(x, axis=-1, keepdims=True)
            return gamma * jnp.sqrt(jnp.asarray(x.shape[-1], x.dtype)) * (x / n)

        def _causal_depthwise_conv(x, w, b):
            xc = jnp.transpose(x, (0, 2, 1))
            xc = jnp.pad(xc, ((0, 0), (0, 0), (K - 1, 0)))
            y = jax.lax.conv_general_dilated(xc, w, window_strides=(1,), padding='VALID', dimension_numbers=('NCH', 'OIH', 'NCH'), feature_group_count=w.shape[0])
            y = y + b[None, :, None]
            return jnp.transpose(y, (0, 2, 1))

        def _linear_scan(alpha, x):

            def combine(c1, c2):
                a1, b1 = c1
                a2, b2 = c2
                return (a1 * a2, a2 * b1 + b2)
            _, h = jax.lax.associative_scan(combine, (alpha, x), axis=1)
            return h
        key = jax.random.key(seed)
        ks = jax.random.split(key, 8)
        N, T = (4, 256)
        x = jax.random.normal(ks[0], (N, T, DIM), jnp.float32)
        W_in = jax.random.normal(ks[1], (2 * HID, DIM), jnp.float32) * DIM ** (-0.5)
        conv_w = jax.random.normal(ks[2], (HID, 1, K), jnp.float32) * 0.25
        conv_b = jnp.zeros((HID,), jnp.float32)
        W_gates = jax.random.normal(ks[3], (2 * HID, HID), jnp.float32) * HID ** (-0.5)
        b_gates = jnp.zeros((2 * HID,), jnp.float32)
        forget_base = jnp.linspace(-4.323, -9.0, HID, dtype=jnp.float32)
        W_out = jax.random.normal(ks[4], (DIM, HID), jnp.float32) * HID ** (-0.5)
        W_grow = jax.random.normal(ks[5], (2 * GHID, DIM), jnp.float32) * DIM ** (-0.5)
        W_shrink = jax.random.normal(ks[6], (DIM, GHID), jnp.float32) * GHID ** (-0.5)
        gamma1 = jnp.ones((DIM,), jnp.float32)
        gamma2 = jnp.ones((DIM,), jnp.float32)
        return {'x': x, 'gamma1': gamma1, 'W_in': W_in, 'conv_w': conv_w, 'conv_b': conv_b, 'W_gates': W_gates, 'b_gates': b_gates, 'forget_base': forget_base, 'W_out': W_out, 'gamma2': gamma2, 'W_grow': W_grow, 'W_shrink': W_shrink}
    _L0_attn_in = _L0_attn_setup()

    def _L0_ffn_setup():
        import jax, jax.numpy as jnp
        import numpy as np
        E = 8
        TOP_K = 2
        CAP_FACTOR = 1.25
        MIN_CAP = 4
        SCORE_SCALE = 1.0

        def _ffn(x, w1, b1, w2, b2):
            return jax.nn.gelu(x @ w1 + b1, approximate=False) @ w2 + b2
        key = jax.random.key(seed)
        ks = jax.random.split(key, 6)
        B, S, D, I = (4, 256, 128, 512)
        std = 0.02
        return {'x': jax.random.normal(ks[0], (B, S, D), jnp.float32), 'Wr': jax.random.normal(ks[1], (E, D), jnp.float32) * std, 'W1': jax.random.normal(ks[2], (E, D, I), jnp.float32) * std, 'b1': jnp.zeros((E, I), jnp.float32), 'W2': jax.random.normal(ks[3], (E, I, D), jnp.float32) * std, 'b2': jnp.zeros((E, D), jnp.float32), 'fw1': jax.random.normal(ks[4], (D, I), jnp.float32) * std, 'fb1': jnp.zeros((I,), jnp.float32), 'fw2': jax.random.normal(ks[5], (I, D), jnp.float32) * std, 'fb2': jnp.zeros((D,), jnp.float32)}
    _L0_ffn_in = _L0_ffn_setup()

    def _L1_attn_setup():
        import jax, jax.numpy as jnp
        import numpy as np
        D_MODEL = 128
        IDX_HEADS = 4
        IDX_DIM = 64
        TOP_K = 32

        def _rope(x):
            B, S, D = x.shape
            half = D // 2
            inv_freq = 1.0 / 10000.0 ** (jnp.arange(half, dtype=jnp.float32) / half)
            ang = jnp.arange(S, dtype=jnp.float32)[:, None] * inv_freq[None, :]
            cos, sin = (jnp.cos(ang), jnp.sin(ang))
            x1, x2 = (x[..., :half], x[..., half:])
            return jnp.concatenate([x1 * cos - x2 * sin, x1 * sin + x2 * cos], axis=-1)
        key = jax.random.key(seed)
        ks = jax.random.split(key, 11)
        B, S, D = (2, 512, D_MODEL)
        s = 0.02
        return {'x': jax.random.normal(ks[0], (B, S, D), dtype=jnp.float32), 'w_qkv': jax.random.normal(ks[1], (3 * D, D), dtype=jnp.float32) * s, 'b_qkv': jnp.zeros((3 * D,), dtype=jnp.float32), 'w_o': jax.random.normal(ks[2], (D, D), dtype=jnp.float32) * s, 'b_o': jnp.zeros((D,), dtype=jnp.float32), 'w_iq': jax.random.normal(ks[3], (IDX_HEADS * IDX_DIM, D), dtype=jnp.float32) * s, 'b_iq': jnp.zeros((IDX_HEADS * IDX_DIM,), dtype=jnp.float32), 'w_ik': jax.random.normal(ks[4], (IDX_DIM, D), dtype=jnp.float32) * s, 'b_ik': jnp.zeros((IDX_DIM,), dtype=jnp.float32), 'w_iw': jax.random.normal(ks[5], (IDX_HEADS, D), dtype=jnp.float32) * s, 'b_iw': jnp.zeros((IDX_HEADS,), dtype=jnp.float32)}
    _L1_attn_in = _L1_attn_setup()

    def _L1_ffn_setup():
        import jax, jax.numpy as jnp
        import numpy as np
        D = 128
        H = 4
        HD = D // H
        E = 8
        FF = 512
        CAP_FACTOR = 1.0

        def _ln(x, g, b, eps=1e-05):
            mu = jnp.mean(x, -1, keepdims=True)
            v = jnp.mean((x - mu) ** 2, -1, keepdims=True)
            return (x - mu) * jax.lax.rsqrt(v + eps) * g + b

        def _mha(x, w, b, ow, ob):
            L, N, _ = x.shape
            qkv = x @ w.T + b
            q, k, v = jnp.split(qkv, 3, axis=-1)
            rh = lambda t: t.reshape(L, N, H, HD).transpose(1, 2, 0, 3)
            q, k, v = (rh(q), rh(k), rh(v))
            scores = jnp.einsum('nhld,nhmd->nhlm', q, k) / np.float32(np.sqrt(HD))
            attn = jax.nn.softmax(scores, axis=-1)
            o = jnp.einsum('nhlm,nhmd->nhld', attn, v).transpose(2, 0, 1, 3).reshape(L, N, D)
            return o @ ow.T + ob

        def _moe(x, wg, w1, b1, w2, b2):
            L, N, _ = x.shape
            S = L * N
            cap = int(CAP_FACTOR * S) // E
            xf = x.reshape(S, D)
            gates = jax.nn.softmax(xf @ wg, axis=-1)
            idx = jnp.argmax(gates, axis=-1)
            mask1 = jax.nn.one_hot(idx, E, dtype=x.dtype)
            loc = jnp.sum((jnp.cumsum(mask1, 0) - 1.0) * mask1, -1).astype(jnp.int32)
            keep = loc < cap
            gate_val = jnp.take_along_axis(gates, idx[:, None], -1)[:, 0]
            slot = jnp.where(keep, idx.astype(jnp.int32) * cap + loc, E * cap)
            disp = jnp.zeros((E * cap, D), x.dtype).at[slot].set(xf, mode='drop')
            disp = disp.reshape(E, cap, D)
            h = jnp.einsum('ecd,edf->ecf', disp, w1) + b1[:, None, :]
            y = (jnp.einsum('ecf,efd->ecd', h, w2) + b2[:, None, :]).reshape(E * cap, D)
            out = jnp.where(keep[:, None], gate_val[:, None] * y[jnp.minimum(slot, E * cap - 1)], 0.0)
            return out.reshape(L, N, D)
        key = jax.random.key(seed)
        ks = jax.random.split(key, 8)
        L, N = (128, 16)
        s = 0.02
        return {'x': jax.random.normal(ks[0], (L, N, D), jnp.float32), 'in_proj_w': jax.random.normal(ks[1], (3 * D, D), jnp.float32) * s, 'in_proj_b': jnp.zeros((3 * D,), jnp.float32), 'out_proj_w': jax.random.normal(ks[2], (D, D), jnp.float32) * s, 'out_proj_b': jnp.zeros((D,), jnp.float32), 'ln1_g': jnp.ones((D,), jnp.float32), 'ln1_b': jnp.zeros((D,), jnp.float32), 'ln2_g': jnp.ones((D,), jnp.float32), 'ln2_b': jnp.zeros((D,), jnp.float32), 'wg': jax.random.normal(ks[3], (D, E), jnp.float32) * s, 'w1': jax.random.normal(ks[4], (E, D, FF), jnp.float32) * s, 'b1': jnp.zeros((E, FF), jnp.float32), 'w2': jax.random.normal(ks[5], (E, FF, D), jnp.float32) * s, 'b2': jnp.zeros((E, D), jnp.float32)}
    _L1_ffn_in = _L1_ffn_setup()
    _d = {'L0_attn_x': _L0_attn_in['x'], 'L0_attn_gamma1': _L0_attn_in['gamma1'], 'L0_attn_W_in': _L0_attn_in['W_in'], 'L0_attn_conv_w': _L0_attn_in['conv_w'], 'L0_attn_conv_b': _L0_attn_in['conv_b'], 'L0_attn_W_gates': _L0_attn_in['W_gates'], 'L0_attn_b_gates': _L0_attn_in['b_gates'], 'L0_attn_forget_base': _L0_attn_in['forget_base'], 'L0_attn_W_out': _L0_attn_in['W_out'], 'L0_attn_gamma2': _L0_attn_in['gamma2'], 'L0_attn_W_grow': _L0_attn_in['W_grow'], 'L0_attn_W_shrink': _L0_attn_in['W_shrink'], 'L0_ffn_Wr': _L0_ffn_in['Wr'], 'L0_ffn_W1': _L0_ffn_in['W1'], 'L0_ffn_b1': _L0_ffn_in['b1'], 'L0_ffn_W2': _L0_ffn_in['W2'], 'L0_ffn_b2': _L0_ffn_in['b2'], 'L0_ffn_fw1': _L0_ffn_in['fw1'], 'L0_ffn_fb1': _L0_ffn_in['fb1'], 'L0_ffn_fw2': _L0_ffn_in['fw2'], 'L0_ffn_fb2': _L0_ffn_in['fb2'], 'L1_attn_w_qkv': _L1_attn_in['w_qkv'], 'L1_attn_b_qkv': _L1_attn_in['b_qkv'], 'L1_attn_w_o': _L1_attn_in['w_o'], 'L1_attn_b_o': _L1_attn_in['b_o'], 'L1_attn_w_iq': _L1_attn_in['w_iq'], 'L1_attn_b_iq': _L1_attn_in['b_iq'], 'L1_attn_w_ik': _L1_attn_in['w_ik'], 'L1_attn_b_ik': _L1_attn_in['b_ik'], 'L1_attn_w_iw': _L1_attn_in['w_iw'], 'L1_attn_b_iw': _L1_attn_in['b_iw'], 'L1_ffn_in_proj_w': _L1_ffn_in['in_proj_w'], 'L1_ffn_in_proj_b': _L1_ffn_in['in_proj_b'], 'L1_ffn_out_proj_w': _L1_ffn_in['out_proj_w'], 'L1_ffn_out_proj_b': _L1_ffn_in['out_proj_b'], 'L1_ffn_ln1_g': _L1_ffn_in['ln1_g'], 'L1_ffn_ln1_b': _L1_ffn_in['ln1_b'], 'L1_ffn_ln2_g': _L1_ffn_in['ln2_g'], 'L1_ffn_ln2_b': _L1_ffn_in['ln2_b'], 'L1_ffn_wg': _L1_ffn_in['wg'], 'L1_ffn_w1': _L1_ffn_in['w1'], 'L1_ffn_b1': _L1_ffn_in['b1'], 'L1_ffn_w2': _L1_ffn_in['w2'], 'L1_ffn_b2': _L1_ffn_in['b2']}
    _x0 = _d['L0_attn_x']
    _d['L0_attn_x'] = jax.random.normal(jax.random.fold_in(jax.random.key(seed), 1), (2, 2048, 128), dtype=_x0.dtype)
    del _x0
    return _d

def reference(L0_attn_x, L0_attn_gamma1, L0_attn_W_in, L0_attn_conv_w, L0_attn_conv_b, L0_attn_W_gates, L0_attn_b_gates, L0_attn_forget_base, L0_attn_W_out, L0_attn_gamma2, L0_attn_W_grow, L0_attn_W_shrink, L0_ffn_Wr, L0_ffn_W1, L0_ffn_b1, L0_ffn_W2, L0_ffn_b2, L0_ffn_fw1, L0_ffn_fb1, L0_ffn_fw2, L0_ffn_fb2, L1_attn_w_qkv, L1_attn_b_qkv, L1_attn_w_o, L1_attn_b_o, L1_attn_w_iq, L1_attn_b_iq, L1_attn_w_ik, L1_attn_b_ik, L1_attn_w_iw, L1_attn_b_iw, L1_ffn_in_proj_w, L1_ffn_in_proj_b, L1_ffn_out_proj_w, L1_ffn_out_proj_b, L1_ffn_ln1_g, L1_ffn_ln1_b, L1_ffn_ln2_g, L1_ffn_ln2_b, L1_ffn_wg, L1_ffn_w1, L1_ffn_b1, L1_ffn_w2, L1_ffn_b2):

    def _L0_attn_ref(x, gamma1, W_in, conv_w, conv_b, W_gates, b_gates, forget_base, W_out, gamma2, W_grow, W_shrink):
        import jax, jax.numpy as jnp
        import numpy as np
        DIM = 128
        HID = int(DIM * 1.5)
        GHID = int(DIM * 2)
        K = 4
        ALPHA_LOG_SCALE = -8.0

        def _rmsnorm(x, gamma):
            n = jnp.linalg.norm(x, axis=-1, keepdims=True)
            return gamma * jnp.sqrt(jnp.asarray(x.shape[-1], x.dtype)) * (x / n)

        def _causal_depthwise_conv(x, w, b):
            xc = jnp.transpose(x, (0, 2, 1))
            xc = jnp.pad(xc, ((0, 0), (0, 0), (K - 1, 0)))
            y = jax.lax.conv_general_dilated(xc, w, window_strides=(1,), padding='VALID', dimension_numbers=('NCH', 'OIH', 'NCH'), feature_group_count=w.shape[0])
            y = y + b[None, :, None]
            return jnp.transpose(y, (0, 2, 1))

        def _linear_scan(alpha, x):

            def combine(c1, c2):
                a1, b1 = c1
                a2, b2 = c2
                return (a1 * a2, a2 * b1 + b2)
            _, h = jax.lax.associative_scan(combine, (alpha, x), axis=1)
            return h
        xn = _rmsnorm(x, gamma1)
        u = jnp.einsum('btd,hd->bth', xn, W_in)
        gate, v = jnp.split(u, 2, axis=-1)
        v = _causal_depthwise_conv(v, conv_w, conv_b)
        g = jnp.einsum('bth,gh->btg', v, W_gates) + b_gates
        forget, inp = jnp.split(g, 2, axis=-1)
        log_alpha = ALPHA_LOG_SCALE * jax.nn.softplus(forget_base) * jax.nn.sigmoid(forget)
        alpha = jnp.exp(log_alpha)
        beta = jnp.sqrt(1.0 - alpha ** 2 + 1e-06)
        xg = beta * jax.nn.sigmoid(inp) * v
        h = _linear_scan(alpha, xg)
        hawk_out = jnp.einsum('bth,dh->btd', jax.nn.gelu(gate, approximate=False) * h, W_out)
        x = x + hawk_out
        xn2 = _rmsnorm(x, gamma2)
        grow = jnp.einsum('btd,gd->btg', xn2, W_grow)
        gate2, v2 = jnp.split(grow, 2, axis=-1)
        mlp = jnp.einsum('btg,dg->btd', jax.nn.gelu(gate2, approximate=False) * v2, W_shrink)
        return x + mlp

    def _L0_ffn_ref(x, Wr, W1, b1, W2, b2, fw1, fb1, fw2, fb2):
        import jax, jax.numpy as jnp
        import numpy as np
        E = 8
        TOP_K = 2
        CAP_FACTOR = 1.25
        MIN_CAP = 4
        SCORE_SCALE = 1.0

        def _ffn(x, w1, b1, w2, b2):
            return jax.nn.gelu(x @ w1 + b1, approximate=False) @ w2 + b2
        B, S, D = x.shape
        T = B * S
        x_flat = x.reshape(T, D)
        logits = x_flat @ Wr.T * SCORE_SCALE
        probs = jax.nn.softmax(logits, axis=-1)
        topk_scores, topk_experts = jax.lax.top_k(probs, TOP_K)
        topk_scores = topk_scores / jnp.clip(topk_scores.sum(-1, keepdims=True), 1e-09, None)
        cap = max(int(CAP_FACTOR * (T * TOP_K / E)), MIN_CAP)
        y_fb = _ffn(x_flat, fw1, fb1, fw2, fb2)
        y_flat = jnp.zeros_like(x_flat)
        fallback = jnp.zeros((T,), bool)
        tok_ids = jnp.arange(T, dtype=jnp.int32)
        for e in range(E):
            match = topk_experts == e
            elig = match.any(-1) & ~fallback
            pos = jnp.cumsum(elig) - 1
            kept = elig & (pos < cap)
            overflow = elig & (pos >= cap)
            slot = jnp.where(kept, pos, cap)
            buf = jnp.zeros((cap + 1,), jnp.int32).at[slot].set(tok_ids)
            vmask = jnp.zeros((cap + 1,), bool).at[slot].set(kept)
            idx = buf[:cap]
            valid = vmask[:cap]
            x_e = x_flat[idx]
            y_e = _ffn(x_e, W1[e], b1[e], W2[e], b2[e])
            w_tok = (topk_scores * match).sum(-1)
            w = jnp.where(valid, w_tok[idx], 0.0)
            y_flat = y_flat.at[idx].add(y_e * w[:, None])
            y_flat = jnp.where(overflow[:, None], y_fb, y_flat)
            fallback = fallback | overflow
        return y_flat.reshape(B, S, D)

    def _L1_attn_ref(x, w_qkv, b_qkv, w_o, b_o, w_iq, b_iq, w_ik, b_ik, w_iw, b_iw):
        import jax, jax.numpy as jnp
        import numpy as np
        D_MODEL = 128
        IDX_HEADS = 4
        IDX_DIM = 64
        TOP_K = 32

        def _rope(x):
            B, S, D = x.shape
            half = D // 2
            inv_freq = 1.0 / 10000.0 ** (jnp.arange(half, dtype=jnp.float32) / half)
            ang = jnp.arange(S, dtype=jnp.float32)[:, None] * inv_freq[None, :]
            cos, sin = (jnp.cos(ang), jnp.sin(ang))
            x1, x2 = (x[..., :half], x[..., half:])
            return jnp.concatenate([x1 * cos - x2 * sin, x1 * sin + x2 * cos], axis=-1)
        B, S, D = x.shape
        qkv = x @ w_qkv.T + b_qkv
        Q, K, V = jnp.split(qkv, 3, axis=-1)
        Q, K = (_rope(Q), _rope(K))
        iq = (x @ w_iq.T + b_iq).reshape(B, S, IDX_HEADS, IDX_DIM)
        ik = x @ w_ik.T + b_ik
        iw = x @ w_iw.T + b_iw
        head_scores = jax.nn.relu(jnp.einsum('bqhd,bkd->bhqk', iq, ik))
        index_scores = jnp.einsum('bhqk,bqh->bqk', head_scores, iw)
        k = min(TOP_K, S)
        _, top_idx = jax.lax.top_k(index_scores, k)
        mask = jnp.zeros((B, S, S), dtype=bool)
        mask = mask.at[jnp.arange(B)[:, None, None], jnp.arange(S)[None, :, None], top_idx].set(True)
        attn_bias = jnp.where(mask, 0.0, -jnp.inf)
        scale = 1.0 / np.sqrt(D).astype(np.float32)
        logits = jnp.einsum('bqd,bkd->bqk', Q, K) * scale + attn_bias
        attn = jax.nn.softmax(logits, axis=-1)
        attn_out = jnp.einsum('bqk,bkd->bqd', attn, V)
        return attn_out @ w_o.T + b_o

    def _L1_ffn_ref(x, in_proj_w, in_proj_b, out_proj_w, out_proj_b, ln1_g, ln1_b, ln2_g, ln2_b, wg, w1, b1, w2, b2):
        import jax, jax.numpy as jnp
        import numpy as np
        D = 128
        H = 4
        HD = D // H
        E = 8
        FF = 512
        CAP_FACTOR = 1.0

        def _ln(x, g, b, eps=1e-05):
            mu = jnp.mean(x, -1, keepdims=True)
            v = jnp.mean((x - mu) ** 2, -1, keepdims=True)
            return (x - mu) * jax.lax.rsqrt(v + eps) * g + b

        def _mha(x, w, b, ow, ob):
            L, N, _ = x.shape
            qkv = x @ w.T + b
            q, k, v = jnp.split(qkv, 3, axis=-1)
            rh = lambda t: t.reshape(L, N, H, HD).transpose(1, 2, 0, 3)
            q, k, v = (rh(q), rh(k), rh(v))
            scores = jnp.einsum('nhld,nhmd->nhlm', q, k) / np.float32(np.sqrt(HD))
            attn = jax.nn.softmax(scores, axis=-1)
            o = jnp.einsum('nhlm,nhmd->nhld', attn, v).transpose(2, 0, 1, 3).reshape(L, N, D)
            return o @ ow.T + ob

        def _moe(x, wg, w1, b1, w2, b2):
            L, N, _ = x.shape
            S = L * N
            cap = int(CAP_FACTOR * S) // E
            xf = x.reshape(S, D)
            gates = jax.nn.softmax(xf @ wg, axis=-1)
            idx = jnp.argmax(gates, axis=-1)
            mask1 = jax.nn.one_hot(idx, E, dtype=x.dtype)
            loc = jnp.sum((jnp.cumsum(mask1, 0) - 1.0) * mask1, -1).astype(jnp.int32)
            keep = loc < cap
            gate_val = jnp.take_along_axis(gates, idx[:, None], -1)[:, 0]
            slot = jnp.where(keep, idx.astype(jnp.int32) * cap + loc, E * cap)
            disp = jnp.zeros((E * cap, D), x.dtype).at[slot].set(xf, mode='drop')
            disp = disp.reshape(E, cap, D)
            h = jnp.einsum('ecd,edf->ecf', disp, w1) + b1[:, None, :]
            y = (jnp.einsum('ecf,efd->ecd', h, w2) + b2[:, None, :]).reshape(E * cap, D)
            out = jnp.where(keep[:, None], gate_val[:, None] * y[jnp.minimum(slot, E * cap - 1)], 0.0)
            return out.reshape(L, N, D)
        y1 = _ln(x + _mha(x, in_proj_w, in_proj_b, out_proj_w, out_proj_b), ln1_g, ln1_b)
        y2 = _ln(y1 + _moe(y1, wg, w1, b1, w2, b2), ln2_g, ln2_b)
        return y2
    x = L0_attn_x
    x = x + 0.5 * _L0_ffn_ref(_layernorm(x, axis=-1), L0_ffn_Wr, L0_ffn_W1, L0_ffn_b1, L0_ffn_W2, L0_ffn_b2, L0_ffn_fw1, L0_ffn_fb1, L0_ffn_fw2, L0_ffn_fb2)
    x = x + _L0_attn_ref(_layernorm(x, axis=-1), L0_attn_gamma1, L0_attn_W_in, L0_attn_conv_w, L0_attn_conv_b, L0_attn_W_gates, L0_attn_b_gates, L0_attn_forget_base, L0_attn_W_out, L0_attn_gamma2, L0_attn_W_grow, L0_attn_W_shrink)
    x = x + 0.5 * _L0_ffn_ref(_layernorm(x, axis=-1), L0_ffn_Wr, L0_ffn_W1, L0_ffn_b1, L0_ffn_W2, L0_ffn_b2, L0_ffn_fw1, L0_ffn_fb1, L0_ffn_fw2, L0_ffn_fb2)
    x = x + 0.5 * _L1_ffn_ref(_layernorm(x, axis=-1), L1_ffn_in_proj_w, L1_ffn_in_proj_b, L1_ffn_out_proj_w, L1_ffn_out_proj_b, L1_ffn_ln1_g, L1_ffn_ln1_b, L1_ffn_ln2_g, L1_ffn_ln2_b, L1_ffn_wg, L1_ffn_w1, L1_ffn_b1, L1_ffn_w2, L1_ffn_b2)
    x = x + _L1_attn_ref(_layernorm(x, axis=-1), L1_attn_w_qkv, L1_attn_b_qkv, L1_attn_w_o, L1_attn_b_o, L1_attn_w_iq, L1_attn_b_iq, L1_attn_w_ik, L1_attn_b_ik, L1_attn_w_iw, L1_attn_b_iw)
    x = x + 0.5 * _L1_ffn_ref(_layernorm(x, axis=-1), L1_ffn_in_proj_w, L1_ffn_in_proj_b, L1_ffn_out_proj_w, L1_ffn_out_proj_b, L1_ffn_ln1_g, L1_ffn_ln1_b, L1_ffn_ln2_g, L1_ffn_ln2_b, L1_ffn_wg, L1_ffn_w1, L1_ffn_b1, L1_ffn_w2, L1_ffn_b2)
    return x

_drawn_inputs = setup_inputs


def setup_inputs(seed=0):
    import zlib

    import numpy as np

    out = dict(_drawn_inputs(seed))
    spreads = {'L0_attn_gamma1': (1.0, 0.2),
     'L0_attn_conv_b': (0.0, 0.1),
     'L0_attn_b_gates': (0.0, 0.449),
     'L0_attn_gamma2': (1.0, 0.2),
     'L0_ffn_b1': (0.0, 0.583),
     'L0_ffn_b2': (0.0, 0.1),
     'L0_ffn_fb1': (0.0, 0.8),
     'L0_ffn_fb2': (0.0, 0.8),
     'L1_attn_b_qkv': (0.0, 0.8),
     'L1_attn_b_o': (0.0, 0.1),
     'L1_attn_b_iq': (0.0, 0.8),
     'L1_attn_b_ik': (0.0, 0.8),
     'L1_attn_b_iw': (0.0, 0.8),
     'L1_ffn_in_proj_b': (0.0, 0.8),
     'L1_ffn_out_proj_b': (0.0, 0.1),
     'L1_ffn_ln1_g': (1.0, 0.2),
     'L1_ffn_ln1_b': (0.0, 0.1),
     'L1_ffn_ln2_g': (1.0, 0.2),
     'L1_ffn_ln2_b': (0.0, 0.1),
     'L1_ffn_b1': (0.0, 0.8),
     'L1_ffn_b2': (0.0, 0.8)}
    factors = {'L0_ffn_fw1': 8.0,
     'L0_ffn_fw2': 8.0,
     'L1_attn_w_qkv': 8.0,
     'L1_attn_w_o': 4.692,
     'L1_attn_w_iq': 8.0,
     'L1_attn_w_ik': 8.0,
     'L1_attn_w_iw': 8.0,
     'L1_ffn_in_proj_w': 4.419,
     'L1_ffn_out_proj_w': 3.628,
     'L1_ffn_wg': 7.173,
     'L1_ffn_w1': 8.0,
     'L1_ffn_w2': 8.0}
    for name, (base, spread) in spreads.items():
        noise = np.random.default_rng([zlib.crc32(name.encode()), seed]).standard_normal(out[name].shape)
        drawn = base * np.exp(spread * noise) if base else spread * noise
        out[name] = jnp.asarray(drawn.astype(out[name].dtype))
    for name, factor in factors.items():
        out[name] = (out[name] * factor).astype(out[name].dtype)
    return out
```

```python
from contextlib import ExitStack

import concourse.bass as bass
import numpy as np
from concourse import mybir

P = 128
F32 = mybir.dt.float32
BF16 = mybir.dt.bfloat16
U32 = mybir.dt.uint32
ALU = mybir.AluOpType
ACT = mybir.ActivationFunctionType
AX = mybir.AxisListType.X

BATCH, SEQ, D = 2, 2048, 128
TOK = BATCH * SEQ
TILES = TOK // P
TPG = 4
GROUP = TPG * P
GROUPS = TOK // GROUP
PAIRS = GROUPS // 2

E = 8
FF = 512
FC = FF // P
CAP0 = int(1.25 * (TOK * 2 / E))
ROWS0 = CAP0 // P
UNITS0 = [TPG] * (ROWS0 // TPG) + ([ROWS0 % TPG] if ROWS0 % TPG else [])
TRASH = E * CAP0
CAP1 = TOK // E
LN_EPS = 1e-5


class Scope:

    def __init__(self, nc, tag):
        self.nc, self.tag, self.stack, self.sems = nc, tag, ExitStack(), []

    def __enter__(self):
        self.stack.__enter__()
        return self

    def __exit__(self, *a):
        self.stack.__exit__(*a)
        for sem in self.sems:
            self.nc.gpsimd.sem_clear(sem)
            self.nc.release_semaphore(sem)

    def sb(self, name, shape, dt=F32):
        return self.stack.enter_context(self.nc.sbuf_tensor(f"{self.tag}_{name}", shape, dt))

    def ps(self, name, shape, dt=F32):
        return self.stack.enter_context(self.nc.psum_tensor(f"{self.tag}_{name}", shape, dt))

    def sem(self, name):
        self.sems.append(self.nc.alloc_semaphore(f"{self.tag}_{name}"))
        return self.sems[-1]

    def gather_sem(self, name):
        return self.nc.alloc_semaphore(f"{self.tag}_{name}")

    def counter(self, name, credit=0):
        return Signal(self.sem(name), credit)

    def block(self):
        return self.stack.enter_context(self.nc.Block())


class Signal:

    def __init__(self, sem, credit=0):
        self.sem, self.credit = sem, credit

    def ready(self, u):
        return self.credit + 1 + u

    def free(self, u, back=None):
        return self.credit + 1 - (self.credit if back is None else back) + u


class Chain:

    def __init__(self, eng, sem):
        self.eng, self.sem, self.n = eng, sem, 0

    def __call__(self, ins):
        self.n += 1
        ins.then_inc(self.sem, 1)
        self.eng.wait_ge(self.sem, self.n)


def tiles_of(buf, first, n):
    return buf[:, bass.ds(first, n), :]


def over(ap, n):
    return ap.unsqueeze(2).to_broadcast([ap.shape[0], ap.shape[1], n])




def row_stats(nc, tag, src, mean, factors):
    with Scope(nc, tag) as s:
        stats = s.sb("stats", [P, TILES, 6])
        diff = s.sb("diff", [P, TILES])
        var = s.sb("var", [P, TILES])
        sq = s.sb("sq", [P, TILES])
        arg = [s.sb(f"arg{k}", [P, TILES]) for k in range(len(factors))]
        root = [s.sb(f"root{k}", [P, TILES]) for k in range(len(factors))]
        counted, vdone, arg_ready, root_ready = (s.sem(n) for n in ("counted", "vdone", "arg_ready", "root_ready"))
        block = s.block()

        @block.vector
        def _(dve):
            with dve.Fori(0, TILES // TPG) as i:
                for t in range(TPG):
                    nc.vector.bn_stats(stats[:, bass.ds(TPG * i + t, 1), :], src[:, bass.ds(TPG * i + t, 1), :]).then_inc(counted, 1)
            dve.wait_ge(counted, TILES)
            link = Chain(dve, vdone)
            nc.vector.tensor_tensor(mean[:, :], stats[:, :, 1], stats[:, :, 4], ALU.add).then_inc(vdone, 1)
            nc.vector.tensor_tensor(diff[:, :], stats[:, :, 1], stats[:, :, 4], ALU.subtract).then_inc(vdone, 1)
            nc.vector.tensor_tensor(var[:, :], stats[:, :, 2], stats[:, :, 5], ALU.add).then_inc(vdone, 1)
            link.n = 3
            dve.wait_ge(vdone, 3)
            link(nc.vector.tensor_scalar(mean[:, :], mean[:, :], 0.5, None, ALU.mult))
            link(nc.vector.scalar_tensor_tensor(diff[:, :], diff[:, :], 0.25, diff[:, :], ALU.mult, ALU.mult))
            link(nc.vector.scalar_tensor_tensor(var[:, :], var[:, :], 1.0 / D, diff[:, :], ALU.mult, ALU.add))
            for k, (_, eps, about_mean) in enumerate(factors):
                base = var
                if not about_mean:
                    link(nc.vector.tensor_tensor(sq[:, :], mean[:, :], mean[:, :], ALU.mult))
                    link(nc.vector.tensor_tensor(sq[:, :], sq[:, :], var[:, :], ALU.add))
                    base = sq
                nc.vector.tensor_scalar(arg[k][:, :], base[:, :], eps, None, ALU.add).then_inc(arg_ready, 1)
            for k, (out, _, _) in enumerate(factors):
                dve.wait_ge(root_ready, k + 1)
                link(nc.vector.reciprocal(out[:, :], root[k][:, :]))
                link(nc.vector.tensor_tensor(root[k][:, :], out[:, :], out[:, :], ALU.mult))
                link(nc.vector.tensor_tensor(root[k][:, :], root[k][:, :], arg[k][:, :], ALU.mult))
                link(nc.vector.tensor_scalar(root[k][:, :], root[k][:, :], -0.5, 1.5, ALU.mult, ALU.add))
                link(nc.vector.tensor_tensor(out[:, :], out[:, :], root[k][:, :], ALU.mult))

        @block.scalar
        def _(act):
            for k in range(len(factors)):
                act.wait_ge(arg_ready, k + 1)
                nc.scalar.activation(root[k][:, :], arg[k][:, :], ACT.Sqrt).then_inc(root_ready, 1)




class FfnPipe:

    def __init__(self, s, ahead=2):
        self.ahead = ahead
        self.xg = s.sb("xg", [P, 2, GROUP])
        self.hid = s.sb("hid", [P, 2, FC, GROUP])
        self.yt = s.sb("yt", [P, 2, GROUP])
        self.p_x = s.ps("p_x", [P, 2, GROUP])
        self.p_h = s.ps("p_h", [P, 2, GROUP])
        self.p_y = s.ps("p_y", [P, GROUP])
        self.p_r = s.ps("p_r", [P, GROUP])
        self.x_transposed = s.counter("x_transposed", ahead)
        self.x_copied = s.counter("x_copied", 2)
        self.up_done = s.counter("up_done", 2 * FC)
        self.gelu_done = s.counter("gelu_done", 2)
        self.down_done = s.counter("down_done", ahead)
        self.y_copied = s.counter("y_copied", ahead)
        self.y_transposed = s.counter("y_transposed", 2)
        self.rows_taken = s.counter("rows_taken", 1)

    def pe_credits(self, pe):
        pe.sem_inc(self.x_transposed.sem, self.ahead)
        pe.sem_inc(self.up_done.sem, 2 * FC)
        pe.sem_inc(self.down_done.sem, self.ahead)
        pe.sem_inc(self.y_transposed.sem, 2)

    def act_credits(self, act):
        act.sem_inc(self.x_copied.sem, 2)
        act.sem_inc(self.gelu_done.sem, 2)
        act.sem_inc(self.y_copied.sem, self.ahead)

    def transpose_x(self, nc, pe, u, h, rows, ident):
        pe.wait_ge(self.x_copied.sem, self.x_copied.free(u))
        for t, row in enumerate(rows):
            last = nc.tensor.transpose(self.p_x[:, h, t * P:(t + 1) * P], row, ident)
        last.then_inc(self.x_transposed.sem, 1)

    def up(self, nc, pe, u, h, n, w1):
        for c in range(FC):
            pe.wait_ge(self.gelu_done.sem, self.gelu_done.free(FC * u + c))
            nc.tensor.matmul(self.p_h[:, c % 2, 0:n * P], w1[:, c * P:(c + 1) * P], self.xg[:, h, 0:n * P],
                             start=True, stop=True).then_inc(self.up_done.sem, 1)

    def down(self, nc, pe, u, h, n, w2):
        pe.wait_ge(self.y_copied.sem, self.y_copied.free(u, 1))
        for c in range(FC):
            pe.wait_ge(self.gelu_done.sem, self.gelu_done.ready(FC * u + c))
            last = nc.tensor.matmul(self.p_y[:, 0:n * P], w2[:, c, :], self.hid[:, h, c, 0:n * P],
                                    start=(c == 0), stop=(c == FC - 1))
        last.then_inc(self.down_done.sem, 1)

    def transpose_y(self, nc, pe, u, h, n, ident):
        pe.wait_ge(self.y_copied.sem, self.y_copied.ready(u))
        pe.wait_ge(self.rows_taken.sem, self.rows_taken.free(u))
        for t in range(n):
            last = nc.tensor.transpose(self.p_r[:, t * P:(t + 1) * P], self.yt[:, h, t * P:(t + 1) * P], ident)
        last.then_inc(self.y_transposed.sem, 1)

    def copy_x(self, nc, act, u, h, n):
        act.wait_ge(self.x_transposed.sem, self.x_transposed.ready(u))
        act.wait_ge(self.up_done.sem, self.up_done.free(FC * u + FC - 1))
        nc.scalar.activation(self.xg[:, h, 0:n * P], self.p_x[:, h, 0:n * P], ACT.Copy).then_inc(self.x_copied.sem, 1)

    def gelu(self, nc, act, u, h, n, b1):
        act.wait_ge(self.down_done.sem, self.down_done.free(u, 2))
        for c in range(FC):
            act.wait_ge(self.up_done.sem, self.up_done.ready(FC * u + c))
            nc.scalar.activation(self.hid[:, h, c, 0:n * P], self.p_h[:, c % 2, 0:n * P], ACT.Gelu,
                                 bias=b1[:, c:c + 1]).then_inc(self.gelu_done.sem, 1)

    def copy_y(self, nc, act, u, h, n, b2):
        act.wait_ge(self.down_done.sem, self.down_done.ready(u))
        act.wait_ge(self.y_transposed.sem, self.y_transposed.free(u))
        nc.scalar.activation(self.yt[:, h, 0:n * P], self.p_y[:, 0:n * P], ACT.Identity, bias=b2).then_inc(self.y_copied.sem, 1)

    def take_rows(self, nc, dve, u, n, out):
        dve.wait_ge(self.y_transposed.sem, self.y_transposed.ready(u))
        nc.vector.tensor_copy(out, self.p_r[:, 0:n * P].rearrange("p (t d) -> p t d", d=P)).then_inc(self.rows_taken.sem, 1)




def moe_top2(nc, tag, g, x):
    with Scope(nc, tag) as s:
        mean, rstd = s.sb("mean", [P, TILES]), s.sb("rstd", [P, TILES])
        xn = s.sb("xn", [P, TILES, D])
        yfb = s.sb("yfb", [P, TILES, D])
        logits = s.sb("logits", [P, TILES, E])
        slot = s.sb("slot", [P, 2, TILES], U32)
        wt = s.sb("wt", [P, 2, TILES])
        fallback = s.sb("fallback", [P, TILES])
        row_stats(nc, tag + "s", x, mean, [(rstd, LN_EPS, True)])
        fallback_ffn(nc, tag + "f", g, x, mean, rstd, xn, logits, yfb)
        route_top2(nc, tag + "r", g, logits, slot, wt, fallback)
        experts_top2(nc, tag + "e", g, xn, slot)
        combine_top2(nc, tag + "c", g, x, yfb, slot, wt, fallback)


def fallback_ffn(nc, tag, g, x, mean, rstd, xn, logits, yfb):
    with Scope(nc, tag) as s:
        pipe = FfnPipe(s)
        xs = s.sb("xs", [P, 2, TPG, D])
        p_l = s.ps("p_l", [P, 2, GROUP])
        normalized = s.counter("normalized")
        xs_kept = s.counter("xs_kept", 2)
        router_done = s.counter("router_done")
        logits_kept = s.counter("logits_kept", 2)
        block = s.block()
        w = g.w0

        @block.vector
        def _(dve):
            dve.sem_inc(pipe.rows_taken.sem, 1)
            dve.sem_inc(logits_kept.sem, 2)
            with dve.Fori(0, PAIRS) as i:
                for h in range(2):
                    u = 2 * i + h
                    dve.wait_ge(pipe.x_transposed.sem, pipe.x_transposed.free(u))
                    dve.wait_ge(xs_kept.sem, xs_kept.free(u))
                    for t in range(TPG):
                        k = TPG * u + t
                        last = nc.vector.tensor_scalar(xs[:, h, t:t + 1, :], x[:, bass.ds(k, 1), :],
                                                       mean[:, bass.ds(k, 1)], rstd[:, bass.ds(k, 1)],
                                                       ALU.subtract, ALU.mult)
                    last.then_inc(normalized.sem, 1)
                for h in range(2):
                    u = 2 * i + h
                    dve.wait_ge(router_done.sem, router_done.ready(u))
                    nc.vector.tensor_copy(tiles_of(logits, TPG * u, TPG),
                                          p_l[:, h, 0:TPG * E].rearrange("p (t e) -> p t e", e=E)).then_inc(logits_kept.sem, 1)
                for h in range(2):
                    u = 2 * i + h
                    pipe.take_rows(nc, dve, u, TPG, tiles_of(yfb, TPG * u, TPG))

        @block.gpsimd
        def _(pool):
            pool.sem_inc(xs_kept.sem, 2)
            with pool.Fori(0, PAIRS) as i:
                for h in range(2):
                    u = 2 * i + h
                    pool.wait_ge(normalized.sem, normalized.ready(u))
                    nc.gpsimd.tensor_copy(tiles_of(xn, TPG * u, TPG), xs[:, h, :, :]).then_inc(xs_kept.sem, 1)

        @block.tensor
        def _(pe):
            pipe.pe_credits(pe)
            with pe.Fori(0, PAIRS) as i:
                for h in range(2):
                    pe.wait_ge(normalized.sem, normalized.ready(2 * i + h))
                    pipe.transpose_x(nc, pe, 2 * i + h, h, [xs[:, h, t, :] for t in range(TPG)], g.ident)
                for h in range(2):
                    u = 2 * i + h
                    pe.wait_ge(pipe.x_copied.sem, pipe.x_copied.ready(u))
                    pe.wait_ge(logits_kept.sem, logits_kept.free(u))
                    for t in range(TPG):
                        last = nc.tensor.matmul(p_l[:, h, t * E:(t + 1) * E], pipe.xg[:, h, t * P:(t + 1) * P],
                                                w["wr"], start=True, stop=True)
                    last.then_inc(router_done.sem, 1)
                    pipe.up(nc, pe, u, h, TPG, w["fw1"])
                for h in range(2):
                    pipe.down(nc, pe, 2 * i + h, h, TPG, w["fw2"])
                for h in range(2):
                    pipe.transpose_y(nc, pe, 2 * i + h, h, TPG, g.ident)

        @block.scalar
        def _(act):
            pipe.act_credits(act)
            with act.Fori(0, PAIRS) as i:
                for h in range(2):
                    pipe.copy_x(nc, act, 2 * i + h, h, TPG)
                for h in range(2):
                    pipe.gelu(nc, act, 2 * i + h, h, TPG, w["fb1"])
                for h in range(2):
                    pipe.copy_y(nc, act, 2 * i + h, h, TPG, w["fb2"])


def probabilities(nc, tag, s, logits, probs, top):
    rest = s.sb("rest", [P, TILES, E])
    total = s.sb("total", [P, TILES])
    shifted, exps = s.sem("shifted"), s.sem("exps")

    def vector(link):
        link(nc.vector.tensor_reduce(total[:, :], logits[:, :, :], AX, ALU.max))
        link(nc.vector.tensor_tensor(rest[:, :, :], logits[:, :, :], over(total[:, :], E), ALU.subtract))
        link.eng.sem_inc(shifted, 1)
        link.eng.wait_ge(exps, 1)
        link(nc.vector.tensor_reduce(total[:, :], probs[:, :, :], AX, ALU.add))
        link(nc.vector.reciprocal(total[:, :], total[:, :]))
        link(nc.vector.tensor_tensor(probs[:, :, :], probs[:, :, :], over(total[:, :], E), ALU.mult))
        link(nc.vector.tensor_reduce(top, probs[:, :, :], AX, ALU.max))

    def scalar(act):
        act.wait_ge(shifted, 1)
        nc.scalar.activation(probs[:, :, :], rest[:, :, :], ACT.Exp).then_inc(exps, 1)

    return vector, scalar


def first_largest(nc, link, probs, top, rank, code, best, onehot):
    link(nc.vector.tensor_tensor(code[:, :, :], probs, over(top, E), ALU.is_equal))
    link(nc.vector.tensor_tensor(code[:, :, :], code[:, :, :], rank[:, :, :], ALU.mult))
    link(nc.vector.tensor_reduce(best[:, :], code[:, :, :], AX, ALU.max))
    link(nc.vector.tensor_tensor(onehot, rank[:, :, :], over(best[:, :], E), ALU.is_equal))


def route_top2(nc, tag, g, logits, slot, wt, fallback):
    with Scope(nc, tag) as s:
        probs = s.sb("probs", [P, TILES, E])
        top = s.sb("top", [P, 2, TILES])
        den = s.sb("den", [P, TILES])
        code = s.sb("code", [P, TILES, E])
        best = s.sb("best", [P, TILES])
        hot = s.sb("hot", [P, 2, TILES, E])
        match = s.sb("match", [P, TILES, E])
        second = s.sb("second", [P, TILES, E])
        pos = s.sb("pos", [P, TILES, E])
        elig = s.sb("elig", [P, TILES], BF16)
        before = s.sb("before", [P, TILES])
        over_cap = s.sb("over_cap", [P, TILES])
        valid = s.sb("valid", [P, TILES])
        slot_f = s.sb("slot_f", [P, 2, TILES])
        p_c = s.ps("p_c", [P, 2, TILES])
        vdone, counted, eligible = s.sem("vdone"), s.sem("counted"), s.sem("eligible")
        soft_v, soft_a = probabilities(nc, tag, s, logits, probs, top[:, 0, :])
        block = s.block()

        @block.scalar
        def _(act):
            soft_a(act)

        @block.tensor
        def _(pe):
            for e in range(E):
                pe.wait_ge(eligible, e + 1)
                nc.tensor.matmul(p_c[:, 0, :], g.upto[:, :], elig[:, :], start=True, stop=True)
                nc.tensor.matmul(p_c[:, 1, :], g.ones[:, :], elig[:, :], start=True, stop=True).then_inc(counted, 1)

        @block.vector
        def _(dve):
            link = Chain(dve, vdone)
            soft_v(link)
            first_largest(nc, link, probs[:, :, :], top[:, 0, :], g.rank, code, best, hot[:, 0, :, :])
            link(nc.vector.scalar_tensor_tensor(second[:, :, :], hot[:, 0, :, :], -2.0, probs[:, :, :], ALU.mult, ALU.add))
            link(nc.vector.tensor_reduce(top[:, 1, :], second[:, :, :], AX, ALU.max))
            first_largest(nc, link, second[:, :, :], top[:, 1, :], g.rank, code, best, hot[:, 1, :, :])
            link(nc.vector.tensor_tensor(den[:, :], top[:, 0, :], top[:, 1, :], ALU.add))
            link(nc.vector.tensor_scalar(den[:, :], den[:, :], 1e-9, None, ALU.max))
            link(nc.vector.reciprocal(den[:, :], den[:, :]))
            link(nc.vector.tensor_tensor(match[:, :, :], hot[:, 0, :, :], hot[:, 1, :, :], ALU.add))
            link(nc.vector.memset(fallback[:, :], 0.0))
            for e in range(E):
                nc.vector.scalar_tensor_tensor(elig[:, :], fallback[:, :], 0.5, match[:, :, e], ALU.is_lt, ALU.mult)\
                    .then_inc(eligible, 1)
                dve.wait_ge(counted, e + 1)
                link(nc.vector.tensor_tensor_scan(before[:, :], g.one32[:, :], p_c[:, 1, :], 0.0, ALU.mult, ALU.add))
                link(nc.vector.tensor_tensor(before[:, :], before[:, :], p_c[:, 1, :], ALU.subtract))
                link(nc.vector.scalar_tensor_tensor(before[:, :], p_c[:, 0, :], -1.0, before[:, :], ALU.add, ALU.add))
                nc.vector.tensor_scalar(pos[:, :, e], before[:, :], float(e * CAP0), None, ALU.add)
                link(nc.vector.scalar_tensor_tensor(over_cap[:, :], before[:, :], float(CAP0), elig[:, :], ALU.is_ge, ALU.mult))
                link(nc.vector.tensor_tensor(fallback[:, :], fallback[:, :], over_cap[:, :], ALU.max))
            link(nc.vector.tensor_scalar(valid[:, :], fallback[:, :], -1.0, 1.0, ALU.mult, ALU.add))
            for k in range(2):
                link(nc.vector.tensor_tensor(code[:, :, :], hot[:, k, :, :], pos[:, :, :], ALU.mult))
                link(nc.vector.tensor_reduce(slot_f[:, k, :], code[:, :, :], AX, ALU.add))
                link(nc.vector.scalar_tensor_tensor(slot_f[:, k, :], slot_f[:, k, :], g.trash[:, :], valid[:, :],
                                                    ALU.subtract, ALU.mult))
                link(nc.vector.tensor_scalar(slot_f[:, k, :], slot_f[:, k, :], g.trash[:, :], None, ALU.add))
                link(nc.vector.tensor_copy(slot[:, k, :], slot_f[:, k, :]))
                link(nc.vector.tensor_tensor(wt[:, k, :], top[:, k, :], den[:, :], ALU.mult))
                link(nc.vector.tensor_tensor(wt[:, k, :], wt[:, k, :], valid[:, :], ALU.mult))


def experts_top2(nc, tag, g, xn, slot):
    w = g.w0
    with Scope(nc, tag) as s:
        NU = len(UNITS0)
        pipe = FfnPipe(s, ahead=2 * NU)
        rows = s.sb("rows", [P, 2, ROWS0, D])
        outs = s.sb("outs", [P, E * ROWS0, D])
        w1 = s.sb("w1", [P, 2, FF])
        w2 = s.sb("w2", [P, 2, FC, D])
        bias = s.sb("bias", [P, 2, FC + 1])
        scattered = s.gather_sem("scattered")
        rows_in = [s.sem(f"rows_in{h}") for h in range(2)]
        weights_in = [s.sem(f"weights_in{h}") for h in range(2)]
        stored = [s.gather_sem(f"stored{h}") for h in range(2)]
        outs_ready = s.counter("outs_ready")
        block = s.block()
        first = [sum(UNITS0[:k]) for k in range(NU)]
        turn = [(h, k, UNITS0[k]) for h in range(2) for k in range(NU)]

        @block.gpsimd
        def _(pool):
            for k in range(2):
                for t in range(TILES):
                    pool.indirect_dma_start(g.x_slots, bass.IndirectOffsetOnAxis(ap=slot[:, k, t:t + 1], axis=0),
                                            xn[:, t, :], None).then_inc(scattered, 16)
            with pool.Fori(0, E // 2) as i:
                for h in range(2):
                    pool.wait_ge(outs_ready.sem, outs_ready.ready(2 * i + h))
                    pool.dma_start(g.y_slots[bass.ds((2 * i + h) * CAP0, CAP0), :].rearrange("(p j) d -> p j d", p=P),
                                   tiles_of(outs, (2 * i + h) * ROWS0, ROWS0)).then_inc(stored[h], 16)
            for h in range(2):
                pool.wait_ge(stored[h], 16 * (E // 2))

        @block.sync
        def _(sp):
            with sp.Fori(0, E // 2) as i:
                for h in range(2):
                    e = 2 * i + h
                    sp.wait_ge(pipe.y_copied.sem, pipe.y_copied.free(NU * e + NU - 1))
                    sp.dma_start(w1[:, h, :], w["w1"][bass.ds(e * D, D), :]).then_inc(weights_in[h], 16)
                    sp.dma_start(w2[:, h, :, :], w["w2"][bass.ds(e * P, P), :].rearrange("p (c d) -> p c d", c=FC))\
                        .then_inc(weights_in[h], 16)
                    sp.dma_start(bias[:, h, :], w["b12"][bass.ds(e * P, P), :]).then_inc(weights_in[h], 16)
                    sp.wait_ge(scattered, 16 * 2 * TILES)
                    sp.wait_ge(pipe.x_transposed.sem, pipe.x_transposed.free(NU * e + NU - 1))
                    sp.dma_start(rows[:, h, :, :], g.x_slots[bass.ds(e * CAP0, CAP0), :]
                                 .rearrange("(p j) d -> p j d", p=P)).then_inc(rows_in[h], 16)

        @block.tensor
        def _(pe):
            pipe.pe_credits(pe)
            with pe.Fori(0, E // 2) as i:
                def into(n):
                    h, k, m = turn[n]
                    if k == 0:
                        pe.wait_ge(rows_in[h], 16 * i + 16)
                    pipe.transpose_x(nc, pe, 2 * NU * i + n, n % 2,
                                     [rows[:, h, first[k] + t, :] for t in range(m)], g.ident)

                def up(n):
                    h, k, m = turn[n]
                    u = 2 * NU * i + n
                    if k == 0:
                        pe.wait_ge(weights_in[h], 48 * i + 48)
                    pe.wait_ge(pipe.x_copied.sem, pipe.x_copied.ready(u))
                    pipe.up(nc, pe, u, n % 2, m, w1[:, h, :])

                def down(n):
                    h, k, m = turn[n]
                    pipe.down(nc, pe, 2 * NU * i + n, n % 2, m, w2[:, h, :, :])

                def out(n):
                    pipe.transpose_y(nc, pe, 2 * NU * i + n, n % 2, turn[n][2], g.ident)

                into(0)
                for n in range(2 * NU):
                    if n + 1 < 2 * NU:
                        into(n + 1)
                    up(n)
                    if n:
                        down(n - 1)
                    if n > 1:
                        out(n - 2)
                down(2 * NU - 1)
                out(2 * NU - 2)
                out(2 * NU - 1)

        @block.scalar
        def _(act):
            pipe.act_credits(act)
            with act.Fori(0, E // 2) as i:
                pipe.copy_x(nc, act, 2 * NU * i, 0, turn[0][2])
                for n in range(2 * NU):
                    u = 2 * NU * i + n
                    if n + 1 < 2 * NU:
                        pipe.copy_x(nc, act, u + 1, (n + 1) % 2, turn[n + 1][2])
                    h, _, m = turn[n]
                    pipe.gelu(nc, act, u, n % 2, m, bias[:, h, 0:FC])
                    if n:
                        pipe.copy_y(nc, act, u - 1, (n - 1) % 2, turn[n - 1][2], bias[:, turn[n - 1][0], FC:FC + 1])
                n = 2 * NU - 1
                pipe.copy_y(nc, act, 2 * NU * i + n, n % 2, turn[n][2], bias[:, 1, FC:FC + 1])

        @block.vector
        def _(dve):
            dve.sem_inc(pipe.rows_taken.sem, 1)
            with dve.Fori(0, E // 2) as i:
                for n, (h, k, m) in enumerate(turn):
                    pipe.take_rows(nc, dve, 2 * NU * i + n, m, tiles_of(outs, (2 * i + h) * ROWS0 + first[k], m))
                    if k == NU - 1:
                        dve.wait_ge(pipe.rows_taken.sem, pipe.rows_taken.ready(2 * NU * i + n))
                        dve.sem_inc(outs_ready.sem, 1)


def combine_top2(nc, tag, g, x, yfb, slot, wt, fallback):
    PART = 8
    with Scope(nc, tag) as s:
        got = s.sb("got", [P, 2, TILES, D])
        gathered = [s.gather_sem(f"gathered{q}") for q in range(TILES // PART)]
        vdone = s.sem("vdone")
        block = s.block()

        @block.gpsimd
        def _(pool):
            for t in range(TILES):
                for k in range(2):
                    pool.indirect_dma_start(got[:, k, t, :], None, g.y_slots,
                                            bass.IndirectOffsetOnAxis(ap=slot[:, k, t:t + 1], axis=0))\
                        .then_inc(gathered[t // PART], 16)

        @block.vector
        def _(dve):
            link = Chain(dve, vdone)
            for q in range(TILES // PART):
                part = slice(q * PART, (q + 1) * PART)
                a, b, f = got[:, 0, part, :], got[:, 1, part, :], yfb[:, part, :]
                link(nc.vector.tensor_tensor(f, f, over(fallback[:, part], D), ALU.mult))
                dve.wait_ge(gathered[q], 16 * 2 * PART)
                nc.vector.tensor_tensor(a, a, over(wt[:, 0, part], D), ALU.mult).then_inc(vdone, 1)
                link.n += 1
                link(nc.vector.tensor_tensor(b, b, over(wt[:, 1, part], D), ALU.mult))
                link(nc.vector.tensor_tensor(a, a, b, ALU.add))
                link(nc.vector.tensor_tensor(a, a, f, ALU.add))
                link(nc.vector.scalar_tensor_tensor(x[:, part, :], a, 0.5, x[:, part, :], ALU.mult, ALU.add))



HID = 192
REST = HID - P
SEGS = 3
QUARTERS = SEQ // GROUP
BTILES = SEQ // P


def seg(buf, j, i):
    return buf[:, bass.ds(j * SEQ + i * GROUP, GROUP)]


def whole(buf, j):
    return buf[:, j * SEQ:(j + 1) * SEQ]


def btiles(buf, b, i, t=0, n=TPG):
    return buf[:, bass.ds(TPG * i + (BTILES * b + t), n), :]


def bcol(buf, b, i, t):
    return buf[:, bass.ds(TPG * i + (BTILES * b + t), 1)]


def hawk(nc, tag, g, x):
    with Scope(nc, tag) as s:
        mean, r_ln, r_rms = (s.sb(n, [P, TILES]) for n in ("mean", "r_ln", "r_rms"))
        z = s.sb("z", [P, TILES, D])
        row_stats(nc, tag + "s", x, mean, [(r_ln, LN_EPS, True), (r_rms, 0.0, True)])
        with Scope(nc, tag + "w") as s2:
            gate = s2.sb("gate", [P, SEGS * SEQ])
            conv = s2.sb("conv", [P, SEGS * SEQ])
            inp = s2.sb("inp", [P, SEGS * SEQ])
            with Scope(nc, tag + "v") as s3:
                v = s3.sb("v", [P, SEGS * SEQ])
                hawk_project(nc, tag + "p", g, x, mean, r_ln, r_rms, z, gate, v)
                hawk_conv(nc, tag + "c", g, v, conv)
            with Scope(nc, tag + "f") as s3:
                forget = s3.sb("forget", [P, SEGS * SEQ])
                hawk_gates(nc, tag + "g", g, conv, forget, inp)
                hawk_scan(nc, tag + "r", g, forget, inp, conv, gate)
            hawk_out(nc, tag + "o", g, gate, z)
        row_stats(nc, tag + "t", z, mean, [(r_rms, 0.0, False)])
        hawk_mlp(nc, tag + "m", g, x, z, r_rms)


def hawk_project(nc, tag, g, x, mean, r_ln, r_rms, z, gate, v):
    w = g.w1
    with Scope(nc, tag) as s:
        zs = s.sb("zs", [P, 2, TPG, D])
        zg = s.sb("zg", [P, 2, GROUP])
        p_x = s.ps("p_x", [P, 2, GROUP])
        p_g = s.ps("p_g", [P, SEGS, GROUP])
        p_v = s.ps("p_v", [P, SEGS, GROUP])
        normalized = s.counter("normalized")
        transposed = s.counter("transposed", 2)
        copied = s.counter("copied", 2)
        gate_done = s.counter("gate_done")
        v_done = s.counter("v_done", SEGS)
        gate_kept = s.counter("gate_kept", SEGS)
        v_kept = s.counter("v_kept", SEGS)
        block = s.block()

        @block.vector
        def _(dve):
            dve.sem_inc(v_kept.sem, SEGS)
            with dve.Fori(0, QUARTERS) as i:
                for b in range(2):
                    dve.wait_ge(transposed.sem, transposed.free(2 * i + b))
                    for t in range(TPG):
                        last = nc.vector.tensor_scalar(zs[:, b, t:t + 1, :], btiles(x, b, i, t, 1), bcol(mean, b, i, t),
                                                       bcol(r_rms, b, i, t), ALU.subtract, ALU.mult)
                    last.then_inc(normalized.sem, 1)
                for b in range(2):
                    for t in range(TPG):
                        nc.vector.tensor_scalar(btiles(z, b, i, t, 1), btiles(x, b, i, t, 1), bcol(mean, b, i, t),
                                                bcol(r_ln, b, i, t), ALU.subtract, ALU.mult)
                for j in range(SEGS):
                    dve.wait_ge(v_done.sem, v_done.ready(SEGS * i + j))
                    nc.vector.tensor_copy(seg(v, j, i), p_v[:, j, :]).then_inc(v_kept.sem, 1)

        @block.tensor
        def _(pe):
            pe.sem_inc(transposed.sem, 2)
            pe.sem_inc(v_done.sem, SEGS)
            with pe.Fori(0, QUARTERS) as i:
                for b in range(2):
                    pe.wait_ge(normalized.sem, normalized.ready(2 * i + b))
                    pe.wait_ge(copied.sem, copied.free(2 * i + b))
                    for t in range(TPG):
                        last = nc.tensor.transpose(p_x[:, b, t * P:(t + 1) * P], zs[:, b, t, :], g.ident)
                    last.then_inc(transposed.sem, 1)
                pe.wait_ge(copied.sem, copied.ready(2 * i + 1))
                for bank, kept, done, w_a, w_r in ((p_g, gate_kept, gate_done, w["in_ga"], w["in_gr"]),
                                                   (p_v, v_kept, v_done, w["in_va"], w["in_vr"])):
                    for b in range(2):
                        pe.wait_ge(kept.sem, kept.free(SEGS * i + b))
                        nc.tensor.matmul(bank[:, b, :], w_a, zg[:, b, :], start=True, stop=True).then_inc(done.sem, 1)
                    pe.wait_ge(kept.sem, kept.free(SEGS * i + 2))
                    nc.tensor.matmul(bank[:, 2, :], w_r[:, 0, :], zg[:, 0, :], start=True, stop=False)
                    nc.tensor.matmul(bank[:, 2, :], w_r[:, 1, :], zg[:, 1, :], start=False, stop=True).then_inc(done.sem, 1)

        @block.scalar
        def _(act):
            act.sem_inc(copied.sem, 2)
            act.sem_inc(gate_kept.sem, SEGS)
            with act.Fori(0, QUARTERS) as i:
                act.wait_ge(v_done.sem, v_done.free(SEGS * i + 2))
                for b in range(2):
                    act.wait_ge(transposed.sem, transposed.ready(2 * i + b))
                    nc.scalar.activation(zg[:, b, :], p_x[:, b, :], ACT.Copy).then_inc(copied.sem, 1)
                for j in range(SEGS):
                    act.wait_ge(gate_done.sem, gate_done.ready(SEGS * i + j))
                    nc.scalar.activation(seg(gate, j, i), p_g[:, j, :], ACT.Gelu).then_inc(gate_kept.sem, 1)


def hawk_conv(nc, tag, g, v, conv):
    w = g.w1
    TAPS = 4
    with Scope(nc, tag) as s:
        first_tap, vdone = s.sem("first_tap"), s.sem("vdone")
        block = s.block()

        @block.scalar
        def _(act):
            for j in range(SEGS):
                c = j // 2
                nc.scalar.activation(whole(conv, j), whole(v, j), ACT.Identity, bias=w["conv_b"][:, c:c + 1],
                                     scale=w["conv_w"][:, TAPS * c + TAPS - 1:TAPS * c + TAPS]).then_inc(first_tap, 1)

        @block.vector
        def _(dve):
            link = Chain(dve, vdone)
            for j in range(SEGS):
                dve.wait_ge(first_tap, j + 1)
                for k in range(1, TAPS):
                    col = TAPS * (j // 2) + TAPS - 1 - k
                    out = conv[:, j * SEQ + k:(j + 1) * SEQ]
                    link(nc.vector.scalar_tensor_tensor(out, v[:, j * SEQ:(j + 1) * SEQ - k], w["conv_w"][:, col:col + 1], out,
                                                        ALU.mult, ALU.add))


def hawk_gates(nc, tag, g, conv, forget, inp):
    w = g.w1
    with Scope(nc, tag) as s:
        p_f = s.ps("p_f", [P, SEGS, GROUP])
        p_i = s.ps("p_i", [P, SEGS, GROUP])
        done = s.counter("done")
        kept = s.counter("kept", 2 * SEGS)
        block = s.block()

        @block.tensor
        def _(pe):
            with pe.Fori(0, QUARTERS) as i:
                for n, (bank, aa, ra, ar, rr) in enumerate(((p_f, w["f_aa"], w["f_ra"], w["f_ar"], w["f_rr"]),
                                                            (p_i, w["i_aa"], w["i_ra"], w["i_ar"], w["i_rr"]))):
                    for b in range(2):
                        pe.wait_ge(kept.sem, kept.free(2 * SEGS * i + SEGS * n + b))
                        nc.tensor.matmul(bank[:, b, :], aa, seg(conv, b, i), start=True, stop=False)
                        nc.tensor.matmul(bank[:, b, :], ra[:, b, :], seg(conv, 2, i), start=False, stop=True).then_inc(done.sem, 1)
                    pe.wait_ge(kept.sem, kept.free(2 * SEGS * i + SEGS * n + 2))
                    for b in range(2):
                        nc.tensor.matmul(bank[:, 2, :], ar[:, b, :], seg(conv, b, i), start=(b == 0), stop=False)
                    nc.tensor.matmul(bank[:, 2, :], rr, seg(conv, 2, i), start=False, stop=True).then_inc(done.sem, 1)

        @block.scalar
        def _(act):
            act.sem_inc(kept.sem, 2 * SEGS)
            with act.Fori(0, QUARTERS) as i:
                for n, (bank, out) in enumerate(((p_f, forget), (p_i, inp))):
                    for j in range(SEGS):
                        act.wait_ge(done.sem, done.ready(2 * SEGS * i + SEGS * n + j))
                        nc.scalar.activation(seg(out, j, i), bank[:, j, :], ACT.Sigmoid,
                                             bias=w["b_gates"][:, 2 * n + j // 2:2 * n + j // 2 + 1]).then_inc(kept.sem, 1)


def hawk_scan(nc, tag, g, forget, inp, conv, gate):
    with Scope(nc, tag) as s:
        beta = s.sb("beta", [P, SEGS * SEQ])
        alpha_done, square_done, beta_done, vdone, one_minus = (s.sem(n) for n in ("alpha", "square", "beta_done", "vdone", "one_minus"))
        block = s.block()

        @block.scalar
        def _(act):
            for j in range(SEGS):
                nc.scalar.activation(whole(forget, j), whole(forget, j), ACT.Exp, scale=g.decay[:, j // 2:j // 2 + 1])\
                    .then_inc(alpha_done, 1)
            for j in range(SEGS):
                act.wait_ge(alpha_done, j + 1)
                nc.scalar.activation(whole(beta, j), whole(forget, j), ACT.Square).then_inc(square_done, 1)
            for j in range(SEGS):
                act.wait_ge(one_minus, j + 1)
                nc.scalar.activation(whole(beta, j), whole(beta, j), ACT.Sqrt, bias=g.tiny[:, :]).then_inc(beta_done, 1)

        @block.vector
        def _(dve):
            link = Chain(dve, vdone)
            for j in range(SEGS):
                link(nc.vector.tensor_tensor(whole(inp, j), whole(inp, j), whole(conv, j), ALU.mult))
            for j in range(SEGS):
                dve.wait_ge(square_done, j + 1)
                nc.vector.tensor_scalar(whole(beta, j), whole(beta, j), -1.0, 1.0, ALU.mult, ALU.add).then_inc(one_minus, 1)
            for j in range(SEGS):
                dve.wait_ge(beta_done, j + 1)
                link(nc.vector.tensor_tensor(whole(inp, j), whole(inp, j), whole(beta, j), ALU.mult))
                link(nc.vector.tensor_tensor_scan(whole(conv, j), whole(forget, j), whole(inp, j), 0.0, ALU.mult, ALU.add))
                link(nc.vector.tensor_tensor(whole(gate, j), whole(gate, j), whole(conv, j), ALU.mult))


def hawk_out(nc, tag, g, gate, z):
    w = g.w1
    with Scope(nc, tag) as s:
        yt = s.sb("yt", [P, 2, GROUP])
        p_y = s.ps("p_y", [P, 2, GROUP])
        p_r = s.ps("p_r", [P, 2, GROUP])
        projected = s.counter("projected")
        copied = s.counter("copied", 2)
        transposed = s.counter("transposed", 2)
        added = s.counter("added", 2)
        block = s.block()

        @block.tensor
        def _(pe):
            pe.sem_inc(transposed.sem, 2)
            with pe.Fori(0, QUARTERS) as i:
                for b in range(2):
                    pe.wait_ge(copied.sem, copied.free(2 * i + b))
                    nc.tensor.matmul(p_y[:, b, :], w["out_a"], seg(gate, b, i), start=True, stop=False)
                    nc.tensor.matmul(p_y[:, b, :], w["out_r"][:, b, :], seg(gate, 2, i), start=False, stop=True)\
                        .then_inc(projected.sem, 1)
                for b in range(2):
                    pe.wait_ge(copied.sem, copied.ready(2 * i + b))
                    pe.wait_ge(added.sem, added.free(2 * i + b))
                    for t in range(TPG):
                        last = nc.tensor.transpose(p_r[:, b, t * P:(t + 1) * P], yt[:, b, t * P:(t + 1) * P], g.ident)
                    last.then_inc(transposed.sem, 1)

        @block.scalar
        def _(act):
            act.sem_inc(copied.sem, 2)
            with act.Fori(0, QUARTERS) as i:
                for b in range(2):
                    act.wait_ge(projected.sem, projected.ready(2 * i + b))
                    act.wait_ge(transposed.sem, transposed.free(2 * i + b))
                    nc.scalar.activation(yt[:, b, :], p_y[:, b, :], ACT.Copy).then_inc(copied.sem, 1)

        @block.vector
        def _(dve):
            dve.sem_inc(added.sem, 2)
            with dve.Fori(0, QUARTERS) as i:
                for b in range(2):
                    dve.wait_ge(transposed.sem, transposed.ready(2 * i + b))
                    nc.vector.tensor_tensor(btiles(z, b, i), p_r[:, b, :].rearrange("p (t d) -> p t d", d=D), btiles(z, b, i),
                                            ALU.add).then_inc(added.sem, 1)


def hawk_mlp(nc, tag, g, x, z, r_rms):
    w = g.w1
    GC = 2
    with Scope(nc, tag) as s:
        zs = s.sb("zs", [P, 2, TPG, D])
        zg = s.sb("zg", [P, 2, GROUP])
        hid = s.sb("hid", [P, 2, GC, GROUP])
        yt = s.sb("yt", [P, 2, GROUP])
        p_x = s.ps("p_x", [P, 2, GROUP])
        p_g = s.ps("p_g", [P, GC, GROUP])
        p_v = s.ps("p_v", [P, GC, GROUP])
        p_y = s.ps("p_y", [P, GROUP])
        p_r = s.ps("p_r", [P, GROUP])
        normalized = s.counter("normalized")
        transposed = s.counter("transposed", 2)
        copied = s.counter("copied", 2)
        gate_done = s.counter("gate_done")
        value_done = s.counter("value_done", 2 * GC)
        gelu_done = s.counter("gelu_done", GC)
        product_done = s.counter("product_done", GC)
        shrunk = s.counter("shrunk", 2)
        y_copied = s.counter("y_copied", 1)
        y_transposed = s.counter("y_transposed", 2)
        added = s.counter("added", 1)
        block = s.block()

        @block.vector
        def _(dve):
            dve.sem_inc(product_done.sem, GC)
            dve.sem_inc(added.sem, 1)
            with dve.Fori(0, QUARTERS) as i:
                for b in range(2):
                    dve.wait_ge(transposed.sem, transposed.free(2 * i + b))
                    for t in range(TPG):
                        last = nc.vector.tensor_scalar(zs[:, b, t:t + 1, :], btiles(z, b, i, t, 1), bcol(r_rms, b, i, t),
                                                       None, ALU.mult)
                    last.then_inc(normalized.sem, 1)
                for b in range(2):
                    for c in range(GC):
                        k = GC * (2 * i + b) + c
                        dve.wait_ge(value_done.sem, value_done.ready(k))
                        dve.wait_ge(gelu_done.sem, gelu_done.ready(k))
                        nc.vector.tensor_tensor(hid[:, b, c, :], hid[:, b, c, :], p_v[:, c, :], ALU.mult)\
                            .then_inc(product_done.sem, 1)
                for b in range(2):
                    dve.wait_ge(y_transposed.sem, y_transposed.ready(2 * i + b))
                    nc.vector.tensor_tensor(btiles(z, b, i), p_r[:, :].rearrange("p (t d) -> p t d", d=D), btiles(z, b, i),
                                            ALU.add).then_inc(added.sem, 1)
                for b in range(2):
                    dve.wait_ge(added.sem, added.ready(2 * i + b))
                    nc.vector.tensor_tensor(btiles(x, b, i), btiles(x, b, i), btiles(z, b, i), ALU.add)

        @block.tensor
        def _(pe):
            pe.sem_inc(transposed.sem, 2)
            pe.sem_inc(value_done.sem, 2 * GC)
            pe.sem_inc(shrunk.sem, 2)
            pe.sem_inc(y_transposed.sem, 2)
            with pe.Fori(0, QUARTERS) as i:
                for b in range(2):
                    pe.wait_ge(normalized.sem, normalized.ready(2 * i + b))
                    pe.wait_ge(copied.sem, copied.free(2 * i + b))
                    for t in range(TPG):
                        last = nc.tensor.transpose(p_x[:, b, t * P:(t + 1) * P], zs[:, b, t, :], g.ident)
                    last.then_inc(transposed.sem, 1)
                for b in range(2):
                    pe.wait_ge(copied.sem, copied.ready(2 * i + b))
                    for c in range(GC):
                        k = GC * (2 * i + b) + c
                        pe.wait_ge(gelu_done.sem, gelu_done.free(k))
                        nc.tensor.matmul(p_g[:, c, :], w["grow"][:, c * P:(c + 1) * P], zg[:, b, :], start=True, stop=True)\
                            .then_inc(gate_done.sem, 1)
                        pe.wait_ge(product_done.sem, product_done.free(k))
                        nc.tensor.matmul(p_v[:, c, :], w["grow"][:, (GC + c) * P:(GC + c + 1) * P], zg[:, b, :],
                                         start=True, stop=True).then_inc(value_done.sem, 1)
                for b in range(2):
                    pe.wait_ge(product_done.sem, product_done.ready(GC * (2 * i + b) + GC - 1))
                    pe.wait_ge(y_copied.sem, y_copied.free(2 * i + b))
                    for c in range(GC):
                        last = nc.tensor.matmul(p_y[:, :], w["shrink"][:, c, :], hid[:, b, c, :], start=(c == 0), stop=(c == GC - 1))
                    last.then_inc(shrunk.sem, 1)
                for b in range(2):
                    pe.wait_ge(y_copied.sem, y_copied.ready(2 * i + b))
                    pe.wait_ge(added.sem, added.free(2 * i + b))
                    for t in range(TPG):
                        last = nc.tensor.transpose(p_r[:, t * P:(t + 1) * P], yt[:, b, t * P:(t + 1) * P], g.ident)
                    last.then_inc(y_transposed.sem, 1)

        @block.scalar
        def _(act):
            act.sem_inc(copied.sem, 2)
            act.sem_inc(gelu_done.sem, GC)
            act.sem_inc(y_copied.sem, 1)
            with act.Fori(0, QUARTERS) as i:
                for b in range(2):
                    act.wait_ge(transposed.sem, transposed.ready(2 * i + b))
                    act.wait_ge(value_done.sem, value_done.free(GC * (2 * i + b) + GC - 1))
                    nc.scalar.activation(zg[:, b, :], p_x[:, b, :], ACT.Copy).then_inc(copied.sem, 1)
                for b in range(2):
                    act.wait_ge(shrunk.sem, shrunk.free(2 * i + b))
                    for c in range(GC):
                        act.wait_ge(gate_done.sem, gate_done.ready(GC * (2 * i + b) + c))
                        nc.scalar.activation(hid[:, b, c, :], p_g[:, c, :], ACT.Gelu).then_inc(gelu_done.sem, 1)
                for b in range(2):
                    act.wait_ge(shrunk.sem, shrunk.ready(2 * i + b))
                    act.wait_ge(y_transposed.sem, y_transposed.free(2 * i + b))
                    nc.scalar.activation(yt[:, b, :], p_y[:, :], ACT.Copy).then_inc(y_copied.sem, 1)


def hawk_constants(nc, tag, g):
    w = g.w1
    with Scope(nc, tag) as s:
        a, e, d, y, y2, acc = (s.sb(n, [P, 2]) for n in ("a", "e", "d", "y", "y2", "acc"))
        vdone, negated, exps = s.sem("vdone"), s.sem("negated"), s.sem("exps")
        block = s.block()

        @block.scalar
        def _(act):
            act.wait_ge(negated, 1)
            nc.scalar.activation(e[:, :], a[:, :], ACT.Exp).then_inc(exps, 1)

        @block.vector
        def _(dve):
            link = Chain(dve, vdone)
            for m in (w["in_all"], w["grow"]):
                link(nc.vector.tensor_scalar(m, m, w["gamma1"] if m is w["in_all"] else w["gamma2"], None, ALU.mult))
            link(nc.vector.memset(g.tiny[:, :], 1e-6))
            link(nc.vector.tensor_scalar(d[:, :], w["forget_base"], -1.0, None, ALU.mult))
            nc.vector.tensor_tensor(a[:, :], w["forget_base"], d[:, :], ALU.min).then_inc(negated, 1)
            dve.wait_ge(exps, 1)
            link(nc.vector.tensor_scalar(d[:, :], e[:, :], 2.0, None, ALU.add))
            link(nc.vector.reciprocal(d[:, :], d[:, :]))
            link(nc.vector.tensor_tensor(y[:, :], e[:, :], d[:, :], ALU.mult))
            link(nc.vector.tensor_tensor(y2[:, :], y[:, :], y[:, :], ALU.mult))
            link(nc.vector.memset(acc[:, :], 1.0 / 17))
            for k in range(15, 0, -2):
                link(nc.vector.tensor_tensor(acc[:, :], acc[:, :], y2[:, :], ALU.mult))
                link(nc.vector.tensor_scalar(acc[:, :], acc[:, :], 1.0 / k, None, ALU.add))
            link(nc.vector.tensor_tensor(acc[:, :], acc[:, :], y[:, :], ALU.mult))
            link(nc.vector.tensor_scalar(d[:, :], w["forget_base"], 0.0, None, ALU.max))
            link(nc.vector.scalar_tensor_tensor(acc[:, :], acc[:, :], 2.0, d[:, :], ALU.mult, ALU.add))
            link(nc.vector.tensor_scalar(g.decay[:, :], acc[:, :], -8.0, None, ALU.mult))



HEADS, HD = 4, 32
SC = 2 * 2 * HEADS


def fuse_experts(nc, tag, g, io):
    w = g.w2
    with Scope(nc, tag) as s:
        w1t = s.sb("w1t", [P, E * FC, D])
        w2 = s.sb("w2", [P, E * FC, D])
        b12t = s.sb("b12t", [P, TPG, 32])
        p_w = s.ps("p_w", [P, E, D])
        p_b = s.ps("p_b", [P, E])
        p_t = s.ps("p_t", [P, P])
        w1_in, w2_in, cleared, done, copied, transposed = (
            s.sem(n) for n in ("w1_in", "w2_in", "cleared", "done", "copied", "transposed"))
        block = s.block()

        @block.sync
        def _(sp):
            sp.dma_start(w1t[:, :, :], io["w1t_top1"].rearrange("p (n d) -> p n d", d=D)).then_inc(w1_in, 16)
            sp.dma_start(w2[:, :, :], io["w2_top1"].rearrange("p (n d) -> p n d", d=D)).then_inc(w2_in, 16)

        @block.tensor
        def _(pe):
            pe.wait_ge(w1_in, 16)
            pe.wait_ge(w2_in, 16)
            for e in range(E):
                for c in range(FC):
                    nc.tensor.matmul(p_b[:, e:e + 1], w2[:, e * FC + c, :], w["b1"][:, e * FC + c:e * FC + c + 1],
                                     start=(c == 0), stop=(c == FC - 1))
            for e in range(E):
                for c in range(FC):
                    last = nc.tensor.matmul(p_w[:, e, :], w1t[:, e * FC + c, :], w2[:, e * FC + c, :],
                                            start=(c == 0), stop=(c == FC - 1))
            last.then_inc(done, 1)
            pe.wait_ge(copied, 1)
            nc.tensor.transpose(p_t[:, :], b12t[:, :, :].rearrange("p t e -> p (t e)"), g.ident).then_inc(transposed, 1)

        @block.vector
        def _(dve):
            link = Chain(dve, cleared)
            link(nc.vector.memset(g.b12[:, :, :], 0.0))
            link(nc.vector.memset(b12t[:, :, :], 0.0))
            dve.wait_ge(done, 1)
            for t in range(TPG):
                last = nc.vector.tensor_tensor(b12t[:, t, 0:E], p_b[:, :], w["b2"], ALU.add)
            last.then_inc(copied, 1)
            nc.vector.tensor_copy(g.w12[:, :, :], p_w[:, :, :])
            dve.wait_ge(transposed, 1)
            for t in range(TPG):
                nc.vector.tensor_copy(g.b12[t * 32:(t + 1) * 32, t, :], p_t[t * 32:(t + 1) * 32, :])


def pair_moe(nc, tag, g, x):
    with Scope(nc, tag) as s:
        mean, rstd = s.sb("mean", [P, TILES]), s.sb("rstd", [P, TILES])
        z = s.sb("z", [P, TILES, D])
        row_stats(nc, tag + "s", x, mean, [(rstd, LN_EPS, True)])
        with Scope(nc, tag + "A") as s2:
            v = s2.sb("v", [P, BTILES, 2, D])
            scores = s2.sb("scores", [P, BTILES, SC])
            pair_scores(nc, tag + "q", g, x, mean, rstd, z, v, scores)
            pair_softmax(nc, tag + "m", g, scores)
            pair_attend(nc, tag + "a", g, scores, v, z)
        row_stats(nc, tag + "t", z, mean, [(rstd, LN_EPS, True)])
        with Scope(nc, tag + "B") as s2:
            yt = s2.sb("yt", [P, TOK])
            logits = s2.sb("logits", [P, TILES, E])
            wt = s2.sb("wt", [P, TILES, 32])
            wtt = s2.sb("wtt", [P, GROUPS, P])
            top1_logits(nc, tag + "g", g, z, mean, rstd, yt, logits)
            route_top1(nc, tag + "r", g, logits, wt, wtt)
            experts_top1(nc, tag + "e", g, yt, wt, wtt, z)
        row_stats(nc, tag + "u", z, mean, [(rstd, LN_EPS, True)])
        add_normed(nc, tag + "f", g, z, mean, rstd, x)


def pair_scores(nc, tag, g, x, mean, rstd, z, v, scores):
    w = g.w2
    with Scope(nc, tag) as s:
        zs = s.sb("zs", [P, 2, TPG, D])
        zg = s.sb("zg", [P, 2, GROUP])
        qk = s.sb("qk", [P, 2, 2, 2 * D])
        prod = s.sb("prod", [P, 2, 2, 2, D])
        p_x = s.ps("p_x", [P, 2, GROUP])
        p_q = s.ps("p_q", [P, 2, 2, GROUP])
        normalized = s.counter("normalized")
        z_kept = s.counter("z_kept", 2)
        transposed = s.counter("transposed", 2)
        copied = s.counter("copied", 2)
        projected = s.counter("projected", TPG)
        biased = s.counter("biased", 2)
        multiplied = s.counter("multiplied")
        reduced = s.counter("reduced", 1)
        block = s.block()

        @block.vector
        def _(dve):
            dve.sem_inc(biased.sem, 2)
            with dve.Fori(0, QUARTERS) as i:
                for b in range(2):
                    dve.wait_ge(transposed.sem, transposed.free(2 * i + b))
                    dve.wait_ge(z_kept.sem, z_kept.free(2 * i + b))
                    for t in range(TPG):
                        last = nc.vector.tensor_scalar(zs[:, b, t:t + 1, :], btiles(x, b, i, t, 1), bcol(mean, b, i, t),
                                                       bcol(rstd, b, i, t), ALU.subtract, ALU.mult)
                    last.then_inc(normalized.sem, 1)
                for t in range(TPG):
                    k = TPG * i + t
                    h = t % 2
                    dve.wait_ge(projected.sem, projected.ready(k))
                    nc.vector.tensor_tensor(qk[:, h, :, :], p_q[:, h, :, 0:2 * D],
                                            w["qkv_b"][:, 0:2 * D].unsqueeze(1).to_broadcast([P, 2, 2 * D]), ALU.add)
                    nc.vector.tensor_tensor(v[:, bass.ds(k, 1), :, :].rearrange("p a m d -> p (a m) d"), p_q[:, h, :, 2 * D:3 * D],
                                            w["qkv_b"][:, 2 * D:3 * D].unsqueeze(1).to_broadcast([P, 2, D]), ALU.add)\
                        .then_inc(biased.sem, 1)
                    dve.wait_ge(biased.sem, biased.ready(k))
                    nc.vector.tensor_tensor(prod[:, h, :, :, :], qk[:, h, :, 0:D].unsqueeze(2).to_broadcast([P, 2, 2, D]),
                                            qk[:, h, :, D:2 * D].unsqueeze(1).to_broadcast([P, 2, 2, D]), ALU.mult)\
                        .then_inc(multiplied.sem, 1)
                    dve.wait_ge(multiplied.sem, multiplied.ready(k))
                    nc.vector.tensor_reduce(scores[:, bass.ds(k, 1), :],
                                            prod[:, h, :, :, :].rearrange("p l m (h c) -> p (l m h) c", c=HD), AX, ALU.add)

        @block.gpsimd
        def _(pool):
            pool.sem_inc(z_kept.sem, 2)
            with pool.Fori(0, QUARTERS) as i:
                for b in range(2):
                    pool.wait_ge(normalized.sem, normalized.ready(2 * i + b))
                    nc.gpsimd.tensor_tensor(btiles(z, b, i), zs[:, b, :, :],
                                            w["out_b"].unsqueeze(1).to_broadcast([P, TPG, D]), ALU.add).then_inc(z_kept.sem, 1)

        @block.tensor
        def _(pe):
            pe.sem_inc(transposed.sem, 2)
            pe.sem_inc(projected.sem, TPG)
            with pe.Fori(0, QUARTERS) as i:
                for b in range(2):
                    pe.wait_ge(normalized.sem, normalized.ready(2 * i + b))
                    pe.wait_ge(copied.sem, copied.free(2 * i + b))
                    for t in range(TPG):
                        last = nc.tensor.transpose(p_x[:, b, t * P:(t + 1) * P], zs[:, b, t, :], g.ident)
                    last.then_inc(transposed.sem, 1)
                pe.wait_ge(copied.sem, copied.ready(2 * i + 1))
                for t in range(TPG):
                    pe.wait_ge(biased.sem, biased.free(TPG * i + t))
                    for b in range(2):
                        last = nc.tensor.matmul(p_q[:, t % 2, b, 0:3 * D], zg[:, b, t * P:(t + 1) * P], w["qkv"],
                                                start=True, stop=True)
                    last.then_inc(projected.sem, 1)

        @block.scalar
        def _(act):
            act.sem_inc(copied.sem, 2)
            with act.Fori(0, QUARTERS) as i:
                act.wait_ge(projected.sem, projected.free(TPG * i + TPG - 1))
                for b in range(2):
                    act.wait_ge(transposed.sem, transposed.ready(2 * i + b))
                    nc.scalar.activation(zg[:, b, :], p_x[:, b, :], ACT.Copy).then_inc(copied.sem, 1)


def pair_softmax(nc, tag, g, scores):
    with Scope(nc, tag) as s:
        most = s.sb("most", [P, BTILES * 2, HEADS])
        shifted, exps, vdone = s.sem("shifted"), s.sem("exps"), s.sem("vdone")
        block = s.block()
        by = scores[:, :, :].rearrange("p a (l m h) -> p (a l) m h", l=2, m=2)
        wide = most[:, :, :].unsqueeze(2).to_broadcast([P, BTILES * 2, 2, HEADS])

        @block.scalar
        def _(act):
            act.wait_ge(shifted, 1)
            nc.scalar.activation(scores[:, :, :], scores[:, :, :], ACT.Exp, scale=float(1 / np.float32(np.sqrt(HD))))\
                .then_inc(exps, 1)

        @block.vector
        def _(dve):
            link = Chain(dve, vdone)
            link(nc.vector.tensor_tensor(most[:, :, :], by[:, :, 0, :], by[:, :, 1, :], ALU.max))
            nc.vector.tensor_tensor(by, by, wide, ALU.subtract).then_inc(shifted, 1)
            dve.wait_ge(exps, 1)
            link(nc.vector.tensor_tensor(most[:, :, :], by[:, :, 0, :], by[:, :, 1, :], ALU.add))
            link(nc.vector.reciprocal(most[:, :, :], most[:, :, :]))
            link(nc.vector.tensor_tensor(by, by, wide, ALU.mult))


def pair_attend(nc, tag, g, scores, v, z):
    w = g.w2
    with Scope(nc, tag) as s:
        prod = s.sb("prod", [P, 2, 2, 2, D])
        o = s.sb("o", [P, TPG, 2, D])
        og = s.sb("og", [P, 2, GROUP])
        p_x = s.ps("p_x", [P, 2, GROUP])
        p_r = s.ps("p_r", [P, 2, GROUP])
        multiplied = s.counter("multiplied")
        summed = s.counter("summed", 2)
        transposed = s.counter("transposed", 1)
        copied = s.counter("copied", 2)
        projected = s.counter("projected", 2)
        added = s.counter("added", 2)
        block = s.block()

        @block.vector
        def _(dve):
            dve.sem_inc(added.sem, 2)
            dve.sem_inc(summed.sem, 2)
            with dve.Fori(0, QUARTERS) as i:
                dve.wait_ge(transposed.sem, transposed.free(i))
                for t in range(TPG):
                    k = TPG * i + t
                    h = t % 2
                    dve.wait_ge(summed.sem, summed.free(k))
                    nc.vector.tensor_tensor(prod[:, h, :, :, :].rearrange("p l m (h c) -> p l (m h) c", c=HD),
                                            scores[:, bass.ds(k, 1), :].rearrange("p a (l n) -> p (a l) n", l=2)
                                            .unsqueeze(3).to_broadcast([P, 2, 2 * HEADS, HD]),
                                            v[:, bass.ds(k, 1), :, :].rearrange("p a m (h c) -> p a (m h) c", c=HD)
                                            .to_broadcast([P, 2, 2 * HEADS, HD]), ALU.mult).then_inc(multiplied.sem, 1)
                    dve.wait_ge(multiplied.sem, multiplied.ready(k))
                    nc.vector.tensor_tensor(o[:, t, :, :], prod[:, h, :, 0, :], prod[:, h, :, 1, :], ALU.add)\
                        .then_inc(summed.sem, 1)
                for b in range(2):
                    dve.wait_ge(projected.sem, projected.ready(2 * i + b))
                    nc.vector.tensor_tensor(btiles(z, b, i), p_r[:, b, :].rearrange("p (t d) -> p t d", d=D), btiles(z, b, i),
                                            ALU.add).then_inc(added.sem, 1)

        @block.tensor
        def _(pe):
            pe.sem_inc(transposed.sem, 1)
            pe.sem_inc(projected.sem, 2)
            with pe.Fori(0, QUARTERS) as i:
                for b in range(2):
                    pe.wait_ge(copied.sem, copied.free(2 * i + b))
                for t in range(TPG):
                    pe.wait_ge(summed.sem, summed.ready(TPG * i + t))
                    for b in range(2):
                        last = nc.tensor.transpose(p_x[:, b, t * P:(t + 1) * P], o[:, t, b, :], g.ident)
                last.then_inc(transposed.sem, 1)
                for b in range(2):
                    pe.wait_ge(copied.sem, copied.ready(2 * i + b))
                    pe.wait_ge(added.sem, added.free(2 * i + b))
                    for t in range(TPG):
                        last = nc.tensor.matmul(p_r[:, b, t * P:(t + 1) * P], og[:, b, t * P:(t + 1) * P], w["out"],
                                                start=True, stop=True)
                    last.then_inc(projected.sem, 1)

        @block.scalar
        def _(act):
            act.sem_inc(copied.sem, 2)
            with act.Fori(0, QUARTERS) as i:
                for b in range(2):
                    act.wait_ge(transposed.sem, transposed.ready(i))
                    act.wait_ge(projected.sem, projected.free(2 * i + b))
                    nc.scalar.activation(og[:, b, :], p_x[:, b, :], ACT.Copy).then_inc(copied.sem, 1)


def top1_logits(nc, tag, g, z, mean, rstd, yt, logits):
    w = g.w2
    with Scope(nc, tag) as s:
        ys = s.sb("ys", [P, 2, TPG, D])
        yg = s.sb("yg", [P, 2, GROUP])
        p_x = s.ps("p_x", [P, 2, GROUP])
        p_l = s.ps("p_l", [P, 2, GROUP])
        centred = s.counter("centred")
        scaled = s.counter("scaled")
        normalized = s.counter("normalized")
        kept = s.counter("kept", 2)
        yt_kept = s.counter("yt_kept", 2)
        transposed = s.counter("transposed", 2)
        copied = s.counter("copied", 2)
        routed = s.counter("routed", 2)
        logits_kept = s.counter("logits_kept", 2)
        block = s.block()
        wide = lambda r: r.unsqueeze(1).to_broadcast([P, TPG, D])

        @block.vector
        def _(dve):
            dve.sem_inc(logits_kept.sem, 2)
            with dve.Fori(0, QUARTERS) as i:
                for b in range(2):
                    u = 2 * i + b
                    dve.wait_ge(transposed.sem, transposed.free(u))
                    dve.wait_ge(kept.sem, kept.free(u))
                    for t in range(TPG):
                        last = nc.vector.tensor_scalar(ys[:, b, t:t + 1, :], btiles(z, b, i, t, 1), bcol(mean, b, i, t),
                                                       bcol(rstd, b, i, t), ALU.subtract, ALU.mult)
                    last.then_inc(centred.sem, 1)
                    dve.wait_ge(centred.sem, centred.ready(u))
                    nc.vector.tensor_tensor(ys[:, b, :, :], ys[:, b, :, :], wide(w["ln1_g"]), ALU.mult).then_inc(scaled.sem, 1)
                    dve.wait_ge(scaled.sem, scaled.ready(u))
                    nc.vector.tensor_tensor(ys[:, b, :, :], ys[:, b, :, :], wide(w["ln1_b"]), ALU.add).then_inc(normalized.sem, 1)
                for b in range(2):
                    u = 2 * i + b
                    dve.wait_ge(routed.sem, routed.ready(u))
                    nc.vector.tensor_copy(btiles(logits, b, i), p_l[:, b, 0:TPG * E].rearrange("p (t e) -> p t e", e=E))\
                        .then_inc(logits_kept.sem, 1)

        @block.gpsimd
        def _(pool):
            pool.sem_inc(kept.sem, 2)
            pool.sem_inc(yt_kept.sem, 2)
            with pool.Fori(0, QUARTERS) as i:
                for b in range(2):
                    pool.wait_ge(normalized.sem, normalized.ready(2 * i + b))
                    nc.gpsimd.tensor_copy(btiles(z, b, i), ys[:, b, :, :]).then_inc(kept.sem, 1)
                for b in range(2):
                    pool.wait_ge(copied.sem, copied.ready(2 * i + b))
                    nc.gpsimd.tensor_copy(yt[:, bass.ds(GROUP * i + SEQ * b, GROUP)], yg[:, b, :]).then_inc(yt_kept.sem, 1)

        @block.tensor
        def _(pe):
            pe.sem_inc(transposed.sem, 2)
            pe.sem_inc(routed.sem, 2)
            with pe.Fori(0, QUARTERS) as i:
                for b in range(2):
                    pe.wait_ge(normalized.sem, normalized.ready(2 * i + b))
                    pe.wait_ge(copied.sem, copied.free(2 * i + b))
                    for t in range(TPG):
                        last = nc.tensor.transpose(p_x[:, b, t * P:(t + 1) * P], ys[:, b, t, :], g.ident)
                    last.then_inc(transposed.sem, 1)
                for b in range(2):
                    pe.wait_ge(copied.sem, copied.ready(2 * i + b))
                    pe.wait_ge(logits_kept.sem, logits_kept.free(2 * i + b))
                    for t in range(TPG):
                        last = nc.tensor.matmul(p_l[:, b, t * E:(t + 1) * E], yg[:, b, t * P:(t + 1) * P], w["wg"],
                                                start=True, stop=True)
                    last.then_inc(routed.sem, 1)

        @block.scalar
        def _(act):
            act.sem_inc(copied.sem, 2)
            with act.Fori(0, QUARTERS) as i:
                for b in range(2):
                    act.wait_ge(transposed.sem, transposed.ready(2 * i + b))
                    act.wait_ge(routed.sem, routed.free(2 * i + b))
                    act.wait_ge(yt_kept.sem, yt_kept.free(2 * i + b))
                    nc.scalar.activation(yg[:, b, :], p_x[:, b, :], ACT.Copy).then_inc(copied.sem, 1)


def route_top1(nc, tag, g, logits, wt, wtt):
    with Scope(nc, tag) as s:
        probs = s.sb("probs", [P, TILES, E])
        top = s.sb("top", [P, TILES])
        code = s.sb("code", [P, TILES, E])
        best = s.sb("best", [P, TILES])
        hot = s.sb("hot", [P, TILES, E])
        mask = s.sb("mask", [P, E, TILES], BF16)
        before = s.sb("before", [P, E, TILES])
        p_c = s.ps("p_c", [P, 2, GROUP])
        p_t = s.ps("p_t", [P, GROUPS, P])
        vdone, masked, counted, weighted, transposed = (
            s.sem(n) for n in ("vdone", "masked", "counted", "weighted", "transposed"))
        soft_v, soft_a = probabilities(nc, tag, s, logits, probs, top[:, :])
        block = s.block()
        N = E * TILES
        view = lambda ap: ap.rearrange("p (e t) -> p e t", e=E)

        @block.scalar
        def _(act):
            soft_a(act)

        @block.tensor
        def _(pe):
            pe.wait_ge(masked, 1)
            flat = mask[:, :, :].rearrange("p e t -> p (e t)")
            nc.tensor.matmul(p_c[:, 0, 0:N], g.upto[:, :], flat, start=True, stop=True)
            nc.tensor.matmul(p_c[:, 1, 0:N], g.ones[:, :], flat, start=True, stop=True).then_inc(counted, 1)
            pe.wait_ge(weighted, 1)
            for q in range(GROUPS):
                last = nc.tensor.transpose(p_t[:, q, :], wt[:, q * TPG:(q + 1) * TPG, :].rearrange("p t e -> p (t e)"), g.ident)
            last.then_inc(transposed, 1)

        @block.vector
        def _(dve):
            link = Chain(dve, vdone)
            soft_v(link)
            first_largest(nc, link, probs[:, :, :], top[:, :], g.rank, code, best, hot[:, :, :])
            link(nc.vector.memset(wt[:, :, :], 0.0))
            nc.vector.tensor_copy(mask[:, :, :].rearrange("p e t -> p t e"), hot[:, :, :]).then_inc(masked, 1)
            dve.wait_ge(counted, 1)
            link(nc.vector.tensor_tensor_scan(before[:, :, :].rearrange("p e t -> p (e t)"), g.carry[:, :], p_c[:, 1, 0:N],
                                              0.0, ALU.mult, ALU.add))
            link(nc.vector.tensor_tensor(before[:, :, :], before[:, :, :], view(p_c[:, 1, 0:N]), ALU.subtract))
            link(nc.vector.tensor_tensor(before[:, :, :], view(p_c[:, 0, 0:N]), before[:, :, :], ALU.add))
            link(nc.vector.tensor_scalar(before[:, :, :], before[:, :, :], float(CAP1), None, ALU.is_le))
            link(nc.vector.tensor_tensor(hot[:, :, :], hot[:, :, :], before[:, :, :].rearrange("p e t -> p t e"), ALU.mult))
            nc.vector.tensor_tensor(wt[:, :, 0:E], hot[:, :, :], over(top[:, :], E), ALU.mult).then_inc(weighted, 1)
            dve.wait_ge(transposed, 1)
            nc.vector.tensor_copy(wtt[:, :, :], p_t[:, :, :])


def experts_top1(nc, tag, g, yt, wt, wtt, z):
    H = E // 2
    with Scope(nc, tag) as s:
        yg = s.sb("yg", [P, 2, GROUP])
        wg = s.sb("wg", [P, 2, P])
        low = s.sb("low", [P, 2, TPG, D])
        high = s.sb("high", [P, 2, TPG, D])
        p_b = s.ps("p_b", [P, 2, GROUP])
        p_e = s.ps("p_e", [P, 2, E, D])
        copied = s.counter("copied")
        biases = s.counter("biases")
        products = s.counter("products", 2 * TPG)
        started = s.counter("started", 2)
        chained = s.counter("chained", 2 * H)
        summed = s.counter("summed", 2)
        block = s.block()

        @block.scalar
        def _(act):
            with act.Fori(0, QUARTERS) as i:
                for b in range(2):
                    act.wait_ge(products.sem, products.free(TPG * (2 * i + b) + TPG - 1))
                    nc.scalar.activation(wg[:, b, :], wtt[:, bass.ds(i + QUARTERS * b, 1), :].rearrange("p a n -> p (a n)"), ACT.Copy)
                    nc.scalar.activation(yg[:, b, :], yt[:, bass.ds(GROUP * i + SEQ * b, GROUP)], ACT.Copy)\
                        .then_inc(copied.sem, 1)

        @block.tensor
        def _(pe):
            pe.sem_inc(products.sem, 2 * TPG)
            with pe.Fori(0, QUARTERS) as i:
                for b in range(2):
                    u = 2 * i + b
                    pe.wait_ge(copied.sem, copied.ready(u))
                    pe.wait_ge(started.sem, started.free(u))
                    nc.tensor.matmul(p_b[:, b, :], wg[:, b, :], g.b12[:, :, :].rearrange("p t d -> p (t d)"),
                                     start=True, stop=True).then_inc(biases.sem, 1)
                    for t in range(TPG):
                        k = TPG * u + t
                        pe.wait_ge(chained.sem, chained.free(H * k + H - 1))
                        for half in range(2):
                            last = nc.tensor.matmul(p_e[:, t % 2, half * H:(half + 1) * H, :].rearrange("p e d -> p (e d)"),
                                                    yg[:, b, t * P:(t + 1) * P],
                                                    g.w12[:, half * H:(half + 1) * H, :].rearrange("p e d -> p (e d)"),
                                                    start=True, stop=True)
                        last.then_inc(products.sem, 1)

        @block.vector
        def _(dve):
            dve.sem_inc(started.sem, 2)
            dve.sem_inc(summed.sem, 2)
            dve.sem_inc(chained.sem, 2 * H)
            with dve.Fori(0, QUARTERS) as i:
                for b in range(2):
                    u = 2 * i + b
                    dve.wait_ge(biases.sem, biases.ready(u))
                    dve.wait_ge(summed.sem, summed.free(u))
                    nc.vector.tensor_tensor(low[:, b, :, :], p_b[:, b, :].rearrange("p (t d) -> p t d", d=D), btiles(z, b, i),
                                            ALU.add).then_inc(started.sem, 1)
                    dve.wait_ge(started.sem, started.ready(u))
                    for t in range(TPG):
                        k = TPG * u + t
                        dve.wait_ge(products.sem, products.ready(k))
                        gate = lambda e: wt[:, bass.ds(TPG * i + (BTILES * b + t), 1), e]
                        for e in range(H):
                            if e:
                                dve.wait_ge(chained.sem, chained.ready(H * k + e - 1))
                            nc.vector.scalar_tensor_tensor(low[:, b, t, :], p_e[:, t % 2, e, :], gate(e), low[:, b, t, :],
                                                           ALU.mult, ALU.add)
                            if e:
                                last = nc.vector.scalar_tensor_tensor(high[:, b, t, :], p_e[:, t % 2, H + e, :], gate(H + e),
                                                                      high[:, b, t, :], ALU.mult, ALU.add)
                            else:
                                last = nc.vector.tensor_scalar(high[:, b, t, :], p_e[:, t % 2, H, :], gate(H), None, ALU.mult)
                            last.then_inc(chained.sem, 1)
                    dve.wait_ge(chained.sem, chained.ready(H * (TPG * u + TPG - 1) + H - 1))
                    nc.vector.tensor_tensor(btiles(z, b, i), low[:, b, :, :], high[:, b, :, :], ALU.add)\
                        .then_inc(summed.sem, 1)


def add_normed(nc, tag, g, z, mean, rstd, x):
    w = g.w2
    PART = 8
    with Scope(nc, tag) as s:
        vdone, centred = s.sem("vdone"), s.sem("centred")
        block = s.block()
        wide = lambda r: r.unsqueeze(1).to_broadcast([P, PART, D])

        @block.vector
        def _(dve):
            with dve.Fori(0, TILES // TPG) as i:
                for t in range(TPG):
                    k = TPG * i + t
                    nc.vector.tensor_scalar(z[:, bass.ds(k, 1), :], z[:, bass.ds(k, 1), :], mean[:, bass.ds(k, 1)],
                                            rstd[:, bass.ds(k, 1)], ALU.subtract, ALU.mult).then_inc(centred, 1)
            dve.wait_ge(centred, TILES)
            link = Chain(dve, vdone)
            for q in range(TILES // PART):
                part = z[:, q * PART:(q + 1) * PART, :]
                xp = x[:, q * PART:(q + 1) * PART, :]
                link(nc.vector.tensor_tensor(part, part, wide(w["ln2_g"]), ALU.mult))
                link(nc.vector.tensor_tensor(part, part, wide(w["ln2_b"]), ALU.add))
                link(nc.vector.scalar_tensor_tensor(xp, part, 0.5, xp, ALU.mult, ALU.add))



IH, ID = 4, 64
TOPK = 32
NONE = -3.0e38
MASKED = -1.0e30
HALF = SEQ // 2
SCALE = float(1 / np.sqrt(np.float32(D)))


def sparse_attention(nc, tag, g, x):
    with Scope(nc, tag) as s:
        qt, kt = s.sb("qt", [P, TOK]), s.sb("kt", [P, TOK])
        v = s.sb("v", [P, TILES, D])
        iqt = s.sb("iqt", [P, IH // 2, TOK])
        ikt = s.sb("ikt", [P, TOK])
        iw = s.sb("iw", [P, TILES, IH])
        with Scope(nc, tag + "1") as s2:
            mean, rstd = s2.sb("mean", [P, TILES]), s2.sb("rstd", [P, TILES])
            row_stats(nc, tag + "s", x, mean, [(rstd, LN_EPS, True)])
            attention_project(nc, tag + "p", g, x, mean, rstd, qt, kt, v, iqt, ikt, iw)
        attention_select(nc, tag + "a", g, x, qt, kt, v, iqt, ikt, iw)


def attention_project(nc, tag, g, x, mean, rstd, qt, kt, v, iqt, ikt, iw):
    w = g.w3
    with Scope(nc, tag) as s:
        cos, sin = s.sb("cos", [P, SEQ]), s.sb("sin", [P, SEQ])
        zs = s.sb("zs", [P, 2, TPG, D])
        zg = s.sb("zg", [P, 2, GROUP])
        rot = s.sb("rot", [P, 2, 2, GROUP])
        p_x = s.ps("p_x", [P, GROUP])
        p_qk = s.ps("p_qk", [P, 4, GROUP])
        p_i = s.ps("p_i", [P, GROUP])
        p_v = s.ps("p_v", [P, GROUP])
        p_w = s.ps("p_w", [P, TPG * IH])
        tables = s.sem("tables")
        normalized = s.counter("normalized")
        transposed = s.counter("transposed", 2)
        copied = s.counter("copied", 1)
        turned = s.counter("turned")
        rotated = s.counter("rotated", 4)
        summed = s.counter("summed", 2)
        indexed = s.counter("indexed")
        index_kept = s.counter("index_kept", 1)
        valued = s.counter("valued")
        value_kept = s.counter("value_kept", 1)
        weighed = s.counter("weighed", 2)
        weight_kept = s.counter("weight_kept", 1)
        block = s.block()

        @block.sync
        def _(sp):
            sp.dma_start(cos[:, :], g.cos).then_inc(tables, 16)
            sp.dma_start(sin[:, :], g.sin).then_inc(tables, 16)

        @block.vector
        def _(dve):
            dve.sem_inc(rotated.sem, 4)
            dve.sem_inc(summed.sem, 2)
            dve.sem_inc(value_kept.sem, 1)
            dve.sem_inc(weight_kept.sem, 1)
            dve.wait_ge(tables, 32)
            with dve.Fori(0, QUARTERS) as i:
                for b in range(2):
                    u = 2 * i + b
                    dve.wait_ge(transposed.sem, transposed.free(u))
                    for t in range(TPG):
                        last = nc.vector.tensor_scalar(zs[:, b, t:t + 1, :], btiles(x, b, i, t, 1), bcol(mean, b, i, t),
                                                       bcol(rstd, b, i, t), ALU.subtract, ALU.mult)
                    last.then_inc(normalized.sem, 1)
                for b in range(2):
                    u = 2 * i + b
                    for m, out in enumerate((qt, kt)):
                        dve.wait_ge(summed.sem, summed.free(2 * u + m))
                        for part, table in enumerate((cos, sin)):
                            n = 2 * m + part
                            dve.wait_ge(turned.sem, turned.ready(4 * u + n))
                            nc.vector.scalar_tensor_tensor(rot[:, m, part, :], p_qk[:, n, :], w["qk_b"][:, n:n + 1],
                                                           table[:, bass.ds(GROUP * i, GROUP)], ALU.add, ALU.mult)\
                                .then_inc(rotated.sem, 1)
                        dve.wait_ge(rotated.sem, rotated.ready(4 * u + 2 * m + 1))
                        nc.vector.tensor_tensor(out[:, bass.ds(GROUP * i + SEQ * b, GROUP)], rot[:, m, 0, :], rot[:, m, 1, :],
                                                ALU.add).then_inc(summed.sem, 1)
                    dve.wait_ge(valued.sem, valued.ready(u))
                    nc.vector.tensor_tensor(btiles(v, b, i), p_v[:, :].rearrange("p (t d) -> p t d", d=D),
                                            w["v_b"].unsqueeze(1).to_broadcast([P, TPG, D]), ALU.add).then_inc(value_kept.sem, 1)
                    dve.wait_ge(weighed.sem, weighed.ready(u))
                    nc.vector.tensor_tensor(btiles(iw, b, i), p_w[:, :].rearrange("p (t h) -> p t h", h=IH),
                                            w["iw_b"].unsqueeze(1).to_broadcast([P, TPG, IH]), ALU.add).then_inc(weight_kept.sem, 1)

        @block.gpsimd
        def _(pool):
            with pool.Fori(0, QUARTERS) as i:
                for b in range(2):
                    pool.wait_ge(normalized.sem, normalized.ready(2 * i + b))
                    nc.gpsimd.tensor_tensor(btiles(x, b, i), btiles(x, b, i), w["o_b"].unsqueeze(1).to_broadcast([P, TPG, D]), ALU.add)

        @block.tensor
        def _(pe):
            pe.sem_inc(transposed.sem, 2)
            pe.sem_inc(weighed.sem, 2)
            with pe.Fori(0, QUARTERS) as i:
                for b in range(2):
                    u = 2 * i + b
                    pe.wait_ge(normalized.sem, normalized.ready(u))
                    pe.wait_ge(copied.sem, copied.free(u))
                    for t in range(TPG):
                        last = nc.tensor.transpose(p_x[:, t * P:(t + 1) * P], zs[:, b, t, :], g.ident)
                    last.then_inc(transposed.sem, 1)
                    pe.wait_ge(copied.sem, copied.ready(u))
                    for n in range(4):
                        pe.wait_ge(rotated.sem, rotated.free(4 * u + n))
                        nc.tensor.matmul(p_qk[:, n, :], w["qk"][:, n * D:(n + 1) * D], zg[:, b, :], start=True, stop=True)\
                            .then_inc(turned.sem, 1)
                        if n < 3:
                            pe.wait_ge(index_kept.sem, index_kept.free(3 * u + n))
                            nc.tensor.matmul(p_i[:, :], w["iqk"][:, n * P:(n + 1) * P], zg[:, b, :], start=True, stop=True)\
                                .then_inc(indexed.sem, 1)
                    pe.wait_ge(value_kept.sem, value_kept.free(u))
                    for t in range(TPG):
                        last = nc.tensor.matmul(p_v[:, t * D:(t + 1) * D], zg[:, b, t * P:(t + 1) * P], w["v"], start=True, stop=True)
                    last.then_inc(valued.sem, 1)
                    pe.wait_ge(weight_kept.sem, weight_kept.free(u))
                    for t in range(TPG):
                        last = nc.tensor.matmul(p_w[:, t * IH:(t + 1) * IH], zg[:, b, t * P:(t + 1) * P], w["iw"], start=True, stop=True)
                    last.then_inc(weighed.sem, 1)

        @block.scalar
        def _(act):
            act.sem_inc(copied.sem, 1)
            act.sem_inc(index_kept.sem, 1)
            with act.Fori(0, QUARTERS) as i:
                for b in range(2):
                    u = 2 * i + b
                    act.wait_ge(transposed.sem, transposed.ready(u))
                    act.wait_ge(weighed.sem, weighed.free(u))
                    nc.scalar.activation(zg[:, b, :], p_x[:, :], ACT.Copy).then_inc(copied.sem, 1)
                    for n in range(3):
                        out = ikt[:, bass.ds(GROUP * i + SEQ * b, GROUP)] if n == 2 else iqt[:, n, bass.ds(GROUP * i + SEQ * b, GROUP)]
                        act.wait_ge(indexed.sem, indexed.ready(3 * u + n))
                        nc.scalar.activation(out, p_i[:, :], ACT.Identity, bias=w["iqk_b"][:, n:n + 1]).then_inc(index_kept.sem, 1)


def attention_select(nc, tag, g, x, qt, kt, v, iqt, ikt, iw):
    w = g.w3
    UNITS = 2 * IH
    RING = 4
    with Scope(nc, tag) as s:
        iqs = s.sb("iqs", [P, IH, P])
        qs = s.sb("qs", [P, P])
        relu = s.sb("relu", [P, RING, HALF])
        score = s.sb("score", [P, SEQ])
        best = s.sb("best", [P, 8])
        prob = s.sb("prob", [P, SEQ])
        probt = s.sb("probt", [P, SEQ])
        most, bias, total, inv = (s.sb(n, [P, 1]) for n in ("most", "bias", "total", "inv"))
        ot = s.sb("ot", [P, P])
        p_s = s.ps("p_s", [P, 2, HALF])
        p_l = s.ps("p_l", [P, SEQ])
        queries = s.counter("queries")
        scored = s.counter("scored")
        logits = s.counter("logits", 1)
        rectified = s.counter("rectified", 2)
        added = s.counter("added", RING)
        vdone = s.sem("vdone")
        masked = s.counter("masked")
        exped = s.counter("exped")
        prob_t = s.counter("prob_t")
        prob_t_kept = s.counter("prob_t_kept", 2)
        attended = s.counter("attended", 1)
        inverted = s.counter("inverted")
        o_kept = s.counter("o_kept")
        projected = s.counter("projected")
        finished = s.counter("finished", 1)
        block = s.block()
        N = BTILES

        def in_turn(eng, first, second):
            for b in range(2):
                first(b, 0, N * b, second if b else None)
                with eng.Fori(1, N) as t:
                    first(b, t, t + N * b, second)
            second(1, N - 1, 2 * N - 1)

        def behind(b, t):
            return (0, N - 1) if isinstance(t, int) and t == 0 else (b, t - 1)

        @block.gpsimd
        def _(pool):
            for b in range(2):
                with pool.Fori(0, N) as t:
                    n = t + N * b
                    pool.wait_ge(logits.sem, logits.free(n))
                    nc.gpsimd.tensor_tensor(iqs[:, :, :].rearrange("p (m h) q -> p m h q", h=2),
                                            iqt[:, :, bass.ds(P * t + SEQ * b, P)].unsqueeze(2).to_broadcast([P, IH // 2, 2, P]),
                                            g.halves[:, :].unsqueeze(1).unsqueeze(3).to_broadcast([P, IH // 2, 2, P]), ALU.mult)
                    nc.gpsimd.tensor_copy(qs[:, :], qt[:, bass.ds(P * t + SEQ * b, P)]).then_inc(queries.sem, 1)

        @block.tensor
        def _(pe):
            pe.sem_inc(logits.sem, 1)
            pe.sem_inc(attended.sem, 1)

            def select(b, t, n, then):
                pe.wait_ge(queries.sem, queries.ready(n))
                for half in range(2):
                    for pair in range(IH // 2):
                        for c in range(HALF // GROUP):
                            for h in range(2):
                                unit = UNITS * n + IH * half + 2 * pair + h
                                at = SEQ * b + half * HALF + c * GROUP
                                if c == 0:
                                    pe.wait_ge(rectified.sem, rectified.free(unit))
                                last = nc.tensor.matmul(p_s[:, h, c * GROUP:(c + 1) * GROUP], iqs[:, 2 * pair + h, :],
                                                        ikt[:, at:at + GROUP], start=True, stop=True)
                                if c == HALF // GROUP - 1:
                                    last.then_inc(scored.sem, 1)
                if then is not None:
                    then(*behind(b, t), n - 1)
                pe.wait_ge(finished.sem, finished.free(n))
                for c in range(SEQ // GROUP):
                    last = nc.tensor.matmul(p_l[:, c * GROUP:(c + 1) * GROUP], qs[:, :],
                                            kt[:, SEQ * b + c * GROUP:SEQ * b + (c + 1) * GROUP], start=True, stop=True)
                last.then_inc(logits.sem, 1)

            def attend(b, t, n):
                pe.wait_ge(exped.sem, exped.ready(n))
                for half in range(2):
                    for k in range(half * N // 2, (half + 1) * N // 2):
                        last = nc.tensor.transpose(p_l[:, k * P:(k + 1) * P], prob[:, k * P:(k + 1) * P], g.ident)
                    last.then_inc(prob_t.sem, 1)
                pe.wait_ge(prob_t_kept.sem, prob_t_kept.ready(2 * n + 1))
                for k in range(N):
                    last = nc.tensor.matmul(p_l[:, 0:P], v[:, N * b + k, :], probt[:, k * P:(k + 1) * P],
                                            start=(k == 0), stop=(k == N - 1))
                last.then_inc(attended.sem, 1)
                pe.wait_ge(o_kept.sem, o_kept.ready(n))
                nc.tensor.matmul(p_l[:, GROUP:GROUP + D], ot[:, :], w["o"], start=True, stop=True).then_inc(projected.sem, 1)

            in_turn(pe, select, attend)

        @block.scalar
        def _(act):
            act.sem_inc(rectified.sem, 2)
            act.sem_inc(prob_t_kept.sem, 2)

            def rectify(n, units):
                for k in units:
                    unit = UNITS * n + k
                    act.wait_ge(scored.sem, scored.ready(unit))
                    act.wait_ge(added.sem, added.free(unit))
                    nc.scalar.activation(relu[:, k % RING, :], p_s[:, k % 2, :], ACT.Relu).then_inc(rectified.sem, 1)

            def exponentials(n):
                act.wait_ge(masked.sem, masked.ready(n))
                nc.scalar.activation(prob[:, :], prob[:, :], ACT.Exp, bias=bias[:, :], accum_out=total[:, :]).then_inc(exped.sem, 1)

            def copies(n):
                act.wait_ge(attended.sem, attended.free(n))
                for half in range(2):
                    act.wait_ge(prob_t.sem, prob_t.ready(2 * n + half))
                    part = slice(half * HALF, (half + 1) * HALF)
                    nc.scalar.activation(probt[:, part], p_l[:, part], ACT.Copy).then_inc(prob_t_kept.sem, 1)
                act.wait_ge(attended.sem, attended.ready(n))
                nc.scalar.activation(ot[:, :], p_l[:, 0:P], ACT.Copy).then_inc(o_kept.sem, 1)

            def select(b, t, n, then):
                rectify(n, range(RING))
                if then is not None:
                    exponentials(n - 1)
                rectify(n, range(RING, UNITS))
                if then is not None:
                    copies(n - 1)

            def attend(b, t, n):
                exponentials(n)
                copies(n)

            in_turn(act, select, attend)

        @block.vector
        def _(dve):
            dve.sem_inc(added.sem, RING)
            dve.sem_inc(finished.sem, 1)

            def select(b, t, n, then):
                steps = [0]

                def link(ins):
                    steps[0] += 1
                    ins.then_inc(vdone, 1)
                    dve.wait_ge(vdone, steps[0])

                def wanted(h):
                    return iw[:, bass.ds(t + N * b, 1), h]

                for half in range(2):
                    part = score[:, half * HALF:(half + 1) * HALF]
                    for h in range(IH):
                        k = IH * half + h
                        unit = UNITS * n + k
                        dve.wait_ge(rectified.sem, rectified.ready(unit))
                        if h == 0:
                            nc.vector.tensor_scalar(part, relu[:, k % RING, :], wanted(0), None, ALU.mult).then_inc(added.sem, 1)
                        else:
                            dve.wait_ge(added.sem, added.ready(unit - 1))
                            nc.vector.scalar_tensor_tensor(part, relu[:, k % RING, :], wanted(h), part, ALU.mult, ALU.add)\
                                .then_inc(added.sem, 1)
                dve.wait_ge(added.sem, added.ready(UNITS * n + UNITS - 1))
                dve.sem_inc(vdone, 1)
                dve.sem_clear(vdone)
                for r in range(TOPK // 8):
                    link(nc.vector.max(best[:, :], score[:, :]))
                    link(nc.vector.match_replace(score[:, :], best[:, :], score[:, :], NONE))
                    if r == 1 and then is not None:
                        finish_rows(*behind(b, t), n - 1)
                dve.wait_ge(logits.sem, logits.ready(n))
                if then is not None:
                    dve.wait_ge(prob_t.sem, prob_t.ready(2 * n - 1))
                link(nc.vector.tensor_scalar(prob[:, :], score[:, :], NONE / 2, MASKED, ALU.is_gt, ALU.mult))
                link(nc.vector.tensor_tensor_reduce(out=prob[:, :], in0=prob[:, :], in1=p_l[:, :], scale=SCALE, scalar=NONE,
                                                    op0=ALU.add, op1=ALU.max, accum_out=most[:, :]))
                nc.vector.tensor_scalar(bias[:, :], most[:, :], -1.0, None, ALU.mult).then_inc(masked.sem, 1)

            def finish_rows(b, t, n):
                dve.wait_ge(exped.sem, exped.ready(n))
                nc.vector.reciprocal(inv[:, :], total[:, :]).then_inc(inverted.sem, 1)
                dve.wait_ge(inverted.sem, inverted.ready(n))
                dve.wait_ge(projected.sem, projected.ready(n))
                rows = x[:, bass.ds(t + N * b, 1), :].rearrange("p a d -> p (a d)")
                nc.vector.scalar_tensor_tensor(rows, p_l[:, GROUP:GROUP + D], inv[:, :], rows, ALU.mult, ALU.add)\
                    .then_inc(finished.sem, 1)

            in_turn(dve, select, finish_rows)



PACK0 = dict(wr=E, fw1=FF, fw2=FC * D, fb1=FC, fb2=1)
PACK1 = dict(in_ga=P, in_va=P, in_gr=2 * P, in_vr=2 * P, grow=FF, shrink=2 * P,
             f_aa=P, f_ra=2 * P, f_ar=2 * P, f_rr=P, i_aa=P, i_ra=2 * P, i_ar=2 * P, i_rr=P,
             out_a=P, out_r=2 * P, gamma1=1, gamma2=1, conv_w=8, conv_b=2, b_gates=4, forget_base=2)
PACK2 = dict(qkv=3 * D, out=D, wg=E, b1=E * FC, b2=E, qkv_b=3 * D, out_b=D, ln1_g=D, ln1_b=D, ln2_g=D, ln2_b=D)
PACK3 = dict(qk=4 * D, iqk=3 * P, v=D, iw=IH, o=D, qk_b=4, iqk_b=3, v_b=D, iw_b=IH, o_b=D)


def pack_views(buf, widths, split={}):
    at, views = 0, {}
    for name, n in widths.items():
        view = buf[:, at:at + n]
        if name in split:
            view = view.rearrange("p (c d) -> p c d", c=split[name])
        views[name] = view
        at += n
    return views


def build(nc, io, out, stages=range(6)):
    with Scope(nc, "g") as g:
        x = g.sb("x", [P, TILES, D])
        pack0 = g.sb("pack0", [P, sum(PACK0.values())])
        g.w0 = pack_views(pack0, PACK0, {"fw2": FC})
        g.w0["w1"], g.w0["w2"], g.w0["b12"] = io["w1_top2"], io["w2_top2"], io["b12_top2"]
        pack1 = g.sb("pack1", [P, sum(PACK1.values())])
        g.w1 = pack_views(pack1, PACK1, {n: 2 for n in ("in_gr", "in_vr", "shrink", "f_ra", "f_ar", "i_ra", "i_ar", "out_r")})
        g.w1["in_all"] = pack1[:, 0:6 * P]
        g.decay = g.sb("decay", [P, 2])
        g.tiny = g.sb("tiny", [P, 1])
        pack3 = g.sb("pack3", [P, sum(PACK3.values())])
        g.w3 = pack_views(pack3, PACK3)
        g.cos, g.sin = io["cos"], io["sin"]
        pack2 = g.sb("pack2", [P, sum(PACK2.values())])
        g.w2 = pack_views(pack2, PACK2)
        g.w12 = g.sb("w12", [P, E, D])
        g.b12 = g.sb("b12", [P, TPG, D])
        g.carry = g.sb("carry", [P, E * TILES])
        g.halves = g.sb("halves", [P, 2])
        ident = g.sb("ident", [P, P])
        g.ident = ident[:, :]
        g.upto = g.sb("upto", [P, P], BF16)
        g.ones = g.sb("ones", [P, P], BF16)
        g.one32 = g.sb("one32", [P, TILES])
        g.rank = g.sb("rank", [P, TILES, E])
        g.trash = g.sb("trash", [P, 1])
        g.x_slots = nc.dram_tensor("x_slots", (TRASH + P, D), F32, kind="Internal").ap()
        g.y_slots = nc.dram_tensor("y_slots", (TRASH + P, D), F32, kind="Internal").ap()
        setup(nc, g, io, x, (pack0, pack1, pack2, pack3), ident)
        if 1 in stages:
            hawk_constants(nc, "hc", g)
        if 3 in stages or 5 in stages:
            fuse_experts(nc, "fe", g, io)
        if 0 in stages:
            moe_top2(nc, "a", g, x)
        if 1 in stages:
            hawk(nc, "b", g, x)
        if 2 in stages:
            moe_top2(nc, "c", g, x)
        if 3 in stages:
            pair_moe(nc, "d", g, x)
        if 4 in stages:
            sparse_attention(nc, "e", g, x)
        if 5 in stages:
            pair_moe(nc, "k", g, x)
        finish(nc, out, x)


def setup(nc, g, io, x, packs, ident):
    with Scope(nc, "setup") as s:
        zeros = s.sb("zeros", [P, ROWS0, D])
        loaded, made, cleared, zeroed = (s.sem(n) for n in ("loaded", "made", "cleared", "zeroed"))
        block = s.block()

        @block.sync
        def _(sp):
            sp.dma_start(x[:, :, :], io["x"].rearrange("b (t p) d -> p (b t) d", p=P)).then_inc(loaded, 16)
            for k, pack in enumerate(packs):
                sp.dma_start(pack[:, :], io[f"pack{k}"]).then_inc(loaded, 16)
            sp.wait_ge(loaded, 16 * (1 + len(packs)))

        @block.scalar
        def _(act):
            act.wait_ge(zeroed, 1)
            for e in range(E):
                act.dma_start(g.x_slots[e * CAP0:(e + 1) * CAP0, :].rearrange("(p j) d -> p j d", p=P),
                              zeros[:, :, :]).then_inc(cleared, 16)
            act.dma_start(g.x_slots[TRASH:TRASH + P, :], zeros[:, 0, :]).then_inc(cleared, 16)
            act.dma_start(g.y_slots[TRASH:TRASH + P, :], zeros[:, 0, :]).then_inc(cleared, 16)
            act.wait_ge(cleared, 16 * (E + 2))

        @block.vector
        def _(dve):
            nc.vector.memset(zeros[:, :, :], 0.0).then_inc(zeroed, 1)
            for h in range(2):
                for k in range(2):
                    nc.vector.memset(g.halves[k * ID:(k + 1) * ID, h:h + 1], float(h == k))

        @block.gpsimd
        def _(pool):
            link = Chain(pool, made)
            link(nc.gpsimd.memset(ident[:, :], 0.0))
            link(nc.gpsimd.affine_select(out=ident[:, :], in_=ident[:, :], compare_op=ALU.not_equal, fill=1.0,
                                         base=0, pattern=[[-1, P]], channel_multiplier=1))
            link(nc.gpsimd.memset(g.ones[:, :], 1.0))
            link(nc.gpsimd.memset(g.one32[:, :], 1.0))
            link(nc.gpsimd.affine_select(out=g.upto[:, :], in_=g.ones[:, :], compare_op=ALU.is_ge, fill=0.0,
                                         base=0, pattern=[[1, P]], channel_multiplier=-1))
            link(nc.gpsimd.iota(g.rank[:, :, :], pattern=[[0, TILES], [-1, E]], base=E, channel_multiplier=0,
                                allow_small_or_imprecise_dtypes=True))
            link(nc.gpsimd.memset(g.carry[:, :], 1.0))
            link(nc.gpsimd.memset(g.carry[:, :].rearrange("p (e t) -> p e t", t=TILES)[:, :, 0], 0.0))
            link(nc.gpsimd.iota(g.trash[:, :], pattern=[[0, 1]], base=TRASH, channel_multiplier=1,
                                allow_small_or_imprecise_dtypes=True))


def finish(nc, out, x):
    with Scope(nc, "finish") as s:
        stored = s.sem("stored")
        block = s.block()

        @block.sync
        def _(sp):
            sp.dma_start(out.rearrange("b (t p) d -> p (b t) d", p=P), x[:, :, :]).then_inc(stored, 16)
            sp.wait_ge(stored, 16)


def chunks(a, rows=P):
    return np.concatenate([a[k:k + rows] for k in range(0, a.shape[0], rows)], axis=1)


def lay_out(i):
    cols = lambda v: np.ascontiguousarray(v.reshape(-1, P).T)
    f = {k: np.asarray(v) for k, v in i.items()}
    pack0 = np.concatenate([
        f["L0_ffn_Wr"].T, f["L0_ffn_fw1"], chunks(f["L0_ffn_fw2"]), cols(f["L0_ffn_fb1"]), cols(f["L0_ffn_fb2"])], axis=1)
    rest = lambda a, axis: [np.pad(a, [(0, REST) if k == axis else (0, 0) for k in range(2)]),
                            np.pad(a, [(REST, 0) if k == axis else (0, 0) for k in range(2)])]
    w_in, w_g = f["L0_attn_W_in"].T, f["L0_attn_W_gates"].T
    gate, value = w_in[:, :HID], w_in[:, HID:]
    both = lambda v: np.concatenate([v[:P], v[P:], v[P:]], axis=0).reshape(2, P, -1)
    pair = lambda v: np.concatenate(list(both(v.reshape(HID, -1))), axis=1)
    gates = []
    for m in (w_g[:, :HID], w_g[:, HID:]):
        gates += [m[:P, :P], *rest(m[P:, :P], 0), *rest(m[:P, P:], 1),
                  np.concatenate(rest(m[P:, P:], 1), axis=0)]
    w_out = f["L0_attn_W_out"].T
    pack1 = np.concatenate([
        gate[:, :P], value[:, :P], *rest(gate[:, P:], 1), *rest(value[:, P:], 1), f["L0_attn_W_grow"].T,
        chunks(f["L0_attn_W_shrink"].T), *gates, w_out[:P], *rest(w_out[P:], 0),
        f["L0_attn_gamma1"][:, None], f["L0_attn_gamma2"][:, None], pair(f["L0_attn_conv_w"][:, 0, :]),
        pair(f["L0_attn_conv_b"]), pair(f["L0_attn_b_gates"][:HID]), pair(f["L0_attn_b_gates"][HID:]),
        pair(f["L0_attn_forget_base"])], axis=1)
    rows = lambda v: np.broadcast_to(v[None, :], (P, v.size))
    w1 = f["L1_ffn_w1"]
    pack2 = np.concatenate([
        f["L1_ffn_in_proj_w"].T, f["L1_ffn_out_proj_w"].T, f["L1_ffn_wg"], cols(f["L1_ffn_b1"].reshape(-1)),
        cols(f["L1_ffn_b2"].reshape(-1)), rows(f["L1_ffn_in_proj_b"]), rows(f["L1_ffn_out_proj_b"]),
        rows(f["L1_ffn_ln1_g"]), rows(f["L1_ffn_ln1_b"]), rows(f["L1_ffn_ln2_g"]), rows(f["L1_ffn_ln2_b"])], axis=1)
    q, k, v = np.split(f["L1_attn_w_qkv"], 3)
    q_b, k_b, v_b = np.split(f["L1_attn_b_qkv"], 3)
    swap = lambda a: np.concatenate([a[D // 2:], a[:D // 2]], axis=0)
    twice = lambda a: np.concatenate([a, a], axis=0)
    pack3 = np.concatenate([
        q.T, swap(q).T, k.T, swap(k).T, f["L1_attn_w_iq"].T, twice(f["L1_attn_w_ik"]).T, v.T, f["L1_attn_w_iw"].T,
        f["L1_attn_w_o"].T, cols(q_b), cols(swap(q_b)), cols(k_b), cols(swap(k_b)), cols(f["L1_attn_b_iq"]),
        cols(twice(f["L1_attn_b_ik"])), rows(v_b), rows(f["L1_attn_b_iw"]), rows(f["L1_attn_b_o"])], axis=1)
    half = D // 2
    freq = (1.0 / np.float32(10000.0) ** (np.arange(half, dtype=np.float32) / np.float32(half))).astype(np.float32)
    angle = freq[:, None] * np.arange(SEQ, dtype=np.float32)[None, :]
    return {
        "pack3": pack3,
        "cos": twice(np.cos(angle)),
        "sin": np.concatenate([-np.sin(angle), np.sin(angle)], axis=0),
        "pack2": pack2,
        "w1t_top1": chunks(w1.transpose(0, 2, 1).reshape(E * FF, D)),
        "w2_top1": chunks(f["L1_ffn_w2"].reshape(E * FF, D)),
        "pack1": pack1,
        "x": f["L0_attn_x"],
        "pack0": pack0,
        "w1_top2": f["L0_ffn_W1"].reshape(E * D, FF),
        "b12_top2": np.concatenate([np.concatenate([cols(f["L0_ffn_b1"][e]), cols(f["L0_ffn_b2"][e])], axis=1)
                                    for e in range(E)], axis=0),
        "w2_top2": np.concatenate([chunks(f["L0_ffn_W2"][e]) for e in range(E)], axis=0),
    }


def kernel(**inputs):
    import concourse.bacc as bacc
    from concourse.bass_utils import run_bass_kernel_spmd

    nc = bacc.Bacc("TRN2", target_bir_lowering=False, num_devices=1)
    arrays, io = {}, {}
    for name, a in lay_out(inputs).items():
        arrays[name] = np.ascontiguousarray(a)
        io[name] = nc.dram_tensor(name, a.shape, mybir.dt.from_np(a.dtype), kind="ExternalInput").ap()
    out = nc.dram_tensor("out", (BATCH, SEQ, D), F32, kind="ExternalOutput").ap()
    build(nc, io, out)
    r = run_bass_kernel_spmd(nc, [arrays], core_ids=[0])
    return r.results[0]["out"]
```

```python
from contextlib import ExitStack

import concourse.bass as bass
import numpy as np
from concourse import mybir

P = 128
F32 = mybir.dt.float32
F32R = mybir.dt.float32r
BF16 = mybir.dt.bfloat16
U32 = mybir.dt.uint32
ALU = mybir.AluOpType
ACT = mybir.ActivationFunctionType
AX = mybir.AxisListType.X

BATCH, SEQ, D = 2, 2048, 128
TOK = BATCH * SEQ
TILES = TOK // P
TPG = 4
GROUP = TPG * P
GROUPS = TOK // GROUP
PAIRS = GROUPS // 2

E = 8
FF = 512
FC = FF // P
CAP0 = int(1.25 * (TOK * 2 / E))
ROWS0 = CAP0 // P
UNITS0 = [TPG] * (ROWS0 // TPG) + ([ROWS0 % TPG] if ROWS0 % TPG else [])
TRASH = E * CAP0
CAP1 = TOK // E
LN_EPS = 1e-5


class Scope:

    def __init__(self, nc, tag):
        self.nc, self.tag, self.stack, self.sems = nc, tag, ExitStack(), []

    def __enter__(self):
        self.stack.__enter__()
        return self

    def __exit__(self, *a):
        self.stack.__exit__(*a)
        for sem in self.sems:
            self.nc.gpsimd.sem_clear(sem)
            self.nc.release_semaphore(sem)

    def sb(self, name, shape, dt=F32):
        return self.stack.enter_context(self.nc.sbuf_tensor(f"{self.tag}_{name}", shape, dt))

    def ps(self, name, shape, dt=F32):
        return self.stack.enter_context(self.nc.psum_tensor(f"{self.tag}_{name}", shape, dt))

    def sem(self, name):
        self.sems.append(self.nc.alloc_semaphore(f"{self.tag}_{name}"))
        return self.sems[-1]

    def gather_sem(self, name):
        return self.nc.alloc_semaphore(f"{self.tag}_{name}")

    def counter(self, name, credit=0):
        return Signal(self.sem(name), credit)

    def block(self):
        return self.stack.enter_context(self.nc.Block())


class Signal:

    def __init__(self, sem, credit=0):
        self.sem, self.credit = sem, credit

    def ready(self, u):
        return self.credit + 1 + u

    def free(self, u, back=None):
        return self.credit + 1 - (self.credit if back is None else back) + u


class Chain:

    def __init__(self, eng, sem):
        self.eng, self.sem, self.n = eng, sem, 0

    def __call__(self, ins):
        self.n += 1
        ins.then_inc(self.sem, 1)
        self.eng.wait_ge(self.sem, self.n)


def tiles_of(buf, first, n):
    return buf[:, bass.ds(first, n), :]


def over(ap, n):
    return ap.unsqueeze(2).to_broadcast([ap.shape[0], ap.shape[1], n])




def row_stats(nc, tag, stats, mean, factors, src=None):
    with Scope(nc, tag) as s:
        diff = s.sb("diff", [P, TILES])
        var = s.sb("var", [P, TILES])
        sq = s.sb("sq", [P, TILES])
        arg = [s.sb(f"arg{k}", [P, TILES]) for k in range(len(factors))]
        root = [s.sb(f"root{k}", [P, TILES]) for k in range(len(factors))]
        counted, vdone, arg_ready, root_ready = (s.sem(n) for n in ("counted", "vdone", "arg_ready", "root_ready"))
        block = s.block()

        @block.vector
        def _(dve):
            if src is not None:
                for t in range(TILES):
                    last = nc.vector.bn_stats(stats[:, t, :], src[:, t, :])
                last.then_inc(counted, 1)
                dve.wait_ge(counted, 1)
            link = Chain(dve, vdone)
            nc.vector.tensor_tensor(mean[:, :], stats[:, :, 1], stats[:, :, 4], ALU.add).then_inc(vdone, 1)
            nc.vector.tensor_tensor(diff[:, :], stats[:, :, 1], stats[:, :, 4], ALU.subtract).then_inc(vdone, 1)
            nc.vector.tensor_tensor(var[:, :], stats[:, :, 2], stats[:, :, 5], ALU.add).then_inc(vdone, 1)
            link.n = 3
            dve.wait_ge(vdone, 3)
            link(nc.vector.tensor_scalar(mean[:, :], mean[:, :], 0.5, None, ALU.mult))
            link(nc.vector.scalar_tensor_tensor(diff[:, :], diff[:, :], 0.25, diff[:, :], ALU.mult, ALU.mult))
            link(nc.vector.scalar_tensor_tensor(var[:, :], var[:, :], 1.0 / D, diff[:, :], ALU.mult, ALU.add))
            for k, (_, eps, about_mean) in enumerate(factors):
                base = var
                if not about_mean:
                    link(nc.vector.tensor_tensor(sq[:, :], mean[:, :], mean[:, :], ALU.mult))
                    link(nc.vector.tensor_tensor(sq[:, :], sq[:, :], var[:, :], ALU.add))
                    base = sq
                nc.vector.tensor_scalar(arg[k][:, :], base[:, :], eps, None, ALU.add).then_inc(arg_ready, 1)
            for k, (out, _, _) in enumerate(factors):
                dve.wait_ge(root_ready, k + 1)
                link(nc.vector.reciprocal(out[:, :], root[k][:, :]))
                link(nc.vector.tensor_tensor(root[k][:, :], out[:, :], out[:, :], ALU.mult))
                link(nc.vector.tensor_tensor(root[k][:, :], root[k][:, :], arg[k][:, :], ALU.mult))
                link(nc.vector.tensor_scalar(root[k][:, :], root[k][:, :], -0.5, 1.5, ALU.mult, ALU.add))
                link(nc.vector.tensor_tensor(out[:, :], out[:, :], root[k][:, :], ALU.mult))

        @block.scalar
        def _(act):
            for k in range(len(factors)):
                act.wait_ge(arg_ready, k + 1)
                nc.scalar.activation(root[k][:, :], arg[k][:, :], ACT.Sqrt).then_inc(root_ready, 1)


def in_pairs(eng, first, second):
    for h in range(2):
        first(0, h)
    with eng.Fori(1, PAIRS) as i:
        for h in range(2):
            first(i, h)
        for h in range(2):
            second(i - 1, h)
    for h in range(2):
        second(PAIRS - 1, h)




class FfnPipe:

    def __init__(self, s, ahead=2):
        self.ahead = ahead
        self.xg = s.sb("xg", [P, 2, GROUP])
        self.hid = s.sb("hid", [P, 2, FC, GROUP])
        self.yt = s.sb("yt", [P, 2, GROUP])
        self.p_x = s.ps("p_x", [P, 2, GROUP])
        self.p_h = s.ps("p_h", [P, 2, GROUP])
        self.p_y = s.ps("p_y", [P, GROUP])
        self.p_r = s.ps("p_r", [P, GROUP])
        self.x_transposed = s.counter("x_transposed", ahead)
        self.x_copied = s.counter("x_copied", 2)
        self.up_done = s.counter("up_done", 2 * FC)
        self.gelu_done = s.counter("gelu_done", 2)
        self.down_done = s.counter("down_done", ahead)
        self.y_copied = s.counter("y_copied", ahead)
        self.y_transposed = s.counter("y_transposed", 2)
        self.rows_taken = s.counter("rows_taken", 1)

    def pe_credits(self, pe):
        pe.sem_inc(self.x_transposed.sem, self.ahead)
        pe.sem_inc(self.up_done.sem, 2 * FC)
        pe.sem_inc(self.down_done.sem, self.ahead)
        pe.sem_inc(self.y_transposed.sem, 2)

    def act_credits(self, act):
        act.sem_inc(self.x_copied.sem, 2)
        act.sem_inc(self.gelu_done.sem, 2)
        act.sem_inc(self.y_copied.sem, self.ahead)

    def transpose_x(self, nc, pe, u, h, rows, ident):
        pe.wait_ge(self.x_copied.sem, self.x_copied.free(u))
        for t, row in enumerate(rows):
            last = nc.tensor.transpose(self.p_x[:, h, t * P:(t + 1) * P], row, ident)
        last.then_inc(self.x_transposed.sem, 1)

    def up(self, nc, pe, u, xg, w1):
        for c in range(FC):
            pe.wait_ge(self.gelu_done.sem, self.gelu_done.free(FC * u + c))
            nc.tensor.matmul(self.p_h[:, c % 2, 0:xg.shape[1]], w1[:, c * P:(c + 1) * P], xg,
                             start=True, stop=True).then_inc(self.up_done.sem, 1)

    def down(self, nc, pe, u, h, n, w2):
        pe.wait_ge(self.y_copied.sem, self.y_copied.free(u, 1))
        for c in range(FC):
            pe.wait_ge(self.gelu_done.sem, self.gelu_done.ready(FC * u + c))
            last = nc.tensor.matmul(self.p_y[:, 0:n * P], w2[:, c, :], self.hid[:, h, c, 0:n * P],
                                    start=(c == 0), stop=(c == FC - 1))
        last.then_inc(self.down_done.sem, 1)

    def transpose_y(self, nc, pe, u, h, n, ident):
        pe.wait_ge(self.y_copied.sem, self.y_copied.ready(u))
        pe.wait_ge(self.rows_taken.sem, self.rows_taken.free(u))
        for t in range(n):
            last = nc.tensor.transpose(self.p_r[:, t * P:(t + 1) * P], self.yt[:, h, t * P:(t + 1) * P], ident)
        last.then_inc(self.y_transposed.sem, 1)

    def copy_x(self, nc, act, u, h, n):
        act.wait_ge(self.x_transposed.sem, self.x_transposed.ready(u))
        act.wait_ge(self.up_done.sem, self.up_done.free(FC * u + FC - 1))
        nc.scalar.activation(self.xg[:, h, 0:n * P], self.p_x[:, h, 0:n * P], ACT.Copy).then_inc(self.x_copied.sem, 1)

    def gelu(self, nc, act, u, h, n, b1):
        act.wait_ge(self.down_done.sem, self.down_done.free(u, 2))
        for c in range(FC):
            act.wait_ge(self.up_done.sem, self.up_done.ready(FC * u + c))
            nc.scalar.activation(self.hid[:, h, c, 0:n * P], self.p_h[:, c % 2, 0:n * P], ACT.Gelu,
                                 bias=b1[:, c:c + 1]).then_inc(self.gelu_done.sem, 1)

    def copy_y(self, nc, act, u, h, n, b2):
        act.wait_ge(self.down_done.sem, self.down_done.ready(u))
        act.wait_ge(self.y_transposed.sem, self.y_transposed.free(u))
        nc.scalar.activation(self.yt[:, h, 0:n * P], self.p_y[:, 0:n * P], ACT.Identity, bias=b2).then_inc(self.y_copied.sem, 1)

    def take_rows(self, nc, dve, u, n, out):
        dve.wait_ge(self.y_transposed.sem, self.y_transposed.ready(u))
        nc.vector.tensor_copy(out, self.p_r[:, 0:n * P].rearrange("p (t d) -> p t d", d=P)).then_inc(self.rows_taken.sem, 1)




def moe_top2(nc, tag, g, x, first, io=None):
    with Scope(nc, tag) as s:
        mean, rstd = s.sb("mean", [P, TILES]), s.sb("rstd", [P, TILES])
        xn = s.sb("xn", [P, TILES, D])
        yfb = s.sb("yfb", [P, TILES, D])
        logits = s.sb("logits", [P, TILES, E])
        slot = s.sb("slot", [P, 2, TILES], U32)
        wt = s.sb("wt", [P, 2, TILES])
        fallback = s.sb("fallback", [P, TILES])
        row_stats(nc, tag + "s", g.stats, mean, [(rstd, LN_EPS, True)], x if first else None)
        with Scope(nc, tag + "x") as s2:
            xt = s2.sb("xt", [P, TOK])
            router(nc, tag + "l", g, x, mean, rstd, xn, xt, logits)
            route_top2(nc, tag + "r", g, logits, slot, wt, fallback)
            fallback_ffn(nc, tag + "f", g, xn, xt, slot, yfb)
        experts_top2(nc, tag + "e", g)
        combine_top2(nc, tag + "c", g, x, yfb, slot, wt, fallback, io)


def router(nc, tag, g, x, mean, rstd, xn, xt, logits):
    with Scope(nc, tag) as s:
        xs = s.sb("xs", [P, 2, TPG, D])
        xg = s.sb("xg", [P, 2, GROUP])
        p_x = s.ps("p_x", [P, 2, GROUP])
        p_l = s.ps("p_l", [P, 2, GROUP])
        normalized = s.counter("normalized")
        xs_kept = s.counter("xs_kept", 2)
        transposed = s.counter("transposed", 2)
        copied = s.counter("copied", 2)
        x_kept = s.counter("x_kept", 2)
        routed = s.counter("routed", 2)
        logits_kept = s.counter("logits_kept", 2)
        block = s.block()
        w = g.w0

        @block.vector
        def _(dve):
            dve.sem_inc(logits_kept.sem, 2)

            def keep(i, h):
                u = 2 * i + h
                dve.wait_ge(routed.sem, routed.ready(u))
                nc.vector.tensor_copy(tiles_of(logits, TPG * u, TPG),
                                      p_l[:, h, 0:TPG * E].rearrange("p (t e) -> p t e", e=E)).then_inc(logits_kept.sem, 1)

            def normalize(i, h):
                u = 2 * i + h
                dve.wait_ge(transposed.sem, transposed.free(u))
                dve.wait_ge(xs_kept.sem, xs_kept.free(u))
                for t in range(TPG):
                    k = TPG * u + t
                    last = nc.vector.tensor_scalar(xs[:, h, t:t + 1, :], x[:, bass.ds(k, 1), :],
                                                   mean[:, bass.ds(k, 1)], rstd[:, bass.ds(k, 1)],
                                                   ALU.subtract, ALU.mult)
                last.then_inc(normalized.sem, 1)

            in_pairs(dve, normalize, keep)

        @block.gpsimd
        def _(pool):
            pool.sem_inc(xs_kept.sem, 2)
            with pool.Fori(0, PAIRS) as i:
                for h in range(2):
                    u = 2 * i + h
                    pool.wait_ge(normalized.sem, normalized.ready(u))
                    nc.gpsimd.tensor_copy(tiles_of(xn, TPG * u, TPG), xs[:, h, :, :]).then_inc(xs_kept.sem, 1)

        @block.tensor
        def _(pe):
            pe.sem_inc(transposed.sem, 2)
            pe.sem_inc(routed.sem, 2)

            def transpose(i, h):
                u = 2 * i + h
                pe.wait_ge(normalized.sem, normalized.ready(u))
                pe.wait_ge(x_kept.sem, x_kept.free(u))
                for t in range(TPG):
                    last = nc.tensor.transpose(p_x[:, h, t * P:(t + 1) * P], xs[:, h, t, :], g.ident)
                last.then_inc(transposed.sem, 1)

            def route(i, h):
                u = 2 * i + h
                pe.wait_ge(copied.sem, copied.ready(u))
                pe.wait_ge(logits_kept.sem, logits_kept.free(u))
                for t in range(TPG):
                    last = nc.tensor.matmul(p_l[:, h, t * E:(t + 1) * E], xg[:, h, t * P:(t + 1) * P],
                                            w["wr"], start=True, stop=True)
                last.then_inc(routed.sem, 1)

            in_pairs(pe, transpose, route)

        @block.scalar
        def _(act):
            act.sem_inc(copied.sem, 2)
            act.sem_inc(x_kept.sem, 2)
            with act.Fori(0, PAIRS) as i:
                for h in range(2):
                    u = 2 * i + h
                    act.wait_ge(transposed.sem, transposed.ready(u))
                    act.wait_ge(routed.sem, routed.free(u))
                    nc.scalar.activation(xg[:, h, :], p_x[:, h, :], ACT.Copy).then_inc(copied.sem, 1)
                    nc.scalar.activation(xt[:, bass.ds(GROUP * u, GROUP)], p_x[:, h, :], ACT.Copy).then_inc(x_kept.sem, 1)


def fallback_ffn(nc, tag, g, xn, xt, slot, yfb):
    with Scope(nc, tag) as s:
        pipe = FfnPipe(s)
        scattered = s.gather_sem("scattered")
        block = s.block()
        w = g.w0

        @block.vector
        def _(dve):
            dve.sem_inc(pipe.rows_taken.sem, 1)
            with dve.Fori(0, PAIRS) as i:
                for h in range(2):
                    u = 2 * i + h
                    pipe.take_rows(nc, dve, u, TPG, tiles_of(yfb, TPG * u, TPG))

        @block.gpsimd
        def _(pool):
            pool.wait_ge(g.cleared, 16 * (E + 2))
            for k in range(2):
                for t in range(TILES):
                    pool.indirect_dma_start(g.x_slots, bass.IndirectOffsetOnAxis(ap=slot[:, k, t:t + 1], axis=0),
                                            xn[:, t, :], None).then_inc(scattered, 16)
            pool.wait_ge(scattered, 16 * 2 * TILES)

        @block.tensor
        def _(pe):
            pipe.pe_credits(pe)

            def turn(i, first):
                for h in range(2):
                    u = 2 * i + h
                    pipe.up(nc, pe, u, xt[:, bass.ds(GROUP * u, GROUP)], w["fw1"])
                    if not (first and h == 0):
                        pipe.down(nc, pe, u - 1, 1 - h, TPG, w["fw2"])
                    if not first:
                        pipe.transpose_y(nc, pe, u - 2, h, TPG, g.ident)

            turn(0, True)
            with pe.Fori(1, PAIRS) as i:
                turn(i, False)
            pipe.down(nc, pe, GROUPS - 1, 1, TPG, w["fw2"])
            for h in range(2):
                pipe.transpose_y(nc, pe, GROUPS - 2 + h, h, TPG, g.ident)

        @block.scalar
        def _(act):
            pipe.act_credits(act)

            def turn(i, first):
                for h in range(2):
                    u = 2 * i + h
                    pipe.gelu(nc, act, u, h, TPG, w["fb1"])
                    if not (first and h == 0):
                        pipe.copy_y(nc, act, u - 1, 1 - h, TPG, w["fb2"])

            turn(0, True)
            with act.Fori(1, PAIRS) as i:
                turn(i, False)
            pipe.copy_y(nc, act, GROUPS - 1, 1, TPG, w["fb2"])


def probabilities(nc, tag, s, logits, probs, top):
    rest = s.sb("rest", [P, TILES, E])
    total = s.sb("total", [P, TILES])
    shifted, exps = s.sem("shifted"), s.sem("exps")

    def vector(link):
        link(nc.vector.tensor_reduce(total[:, :], logits[:, :, :], AX, ALU.max))
        link(nc.vector.tensor_tensor(rest[:, :, :], logits[:, :, :], over(total[:, :], E), ALU.subtract))
        link.eng.sem_inc(shifted, 1)
        link.eng.wait_ge(exps, 1)
        link(nc.vector.tensor_reduce(total[:, :], probs[:, :, :], AX, ALU.add))
        link(nc.vector.reciprocal(total[:, :], total[:, :]))
        link(nc.vector.tensor_tensor(probs[:, :, :], probs[:, :, :], over(total[:, :], E), ALU.mult))
        link(nc.vector.tensor_reduce(top, probs[:, :, :], AX, ALU.max))

    def scalar(act):
        act.wait_ge(shifted, 1)
        nc.scalar.activation(probs[:, :, :], rest[:, :, :], ACT.Exp).then_inc(exps, 1)

    return vector, scalar


def first_largest(nc, link, probs, top, rank, code, best, onehot):
    link(nc.vector.tensor_tensor(code[:, :, :], probs, over(top, E), ALU.is_equal))
    link(nc.vector.tensor_tensor(code[:, :, :], code[:, :, :], rank[:, :, :], ALU.mult))
    link(nc.vector.tensor_reduce(best[:, :], code[:, :, :], AX, ALU.max))
    link(nc.vector.tensor_tensor(onehot, rank[:, :, :], over(best[:, :], E), ALU.is_equal))


def route_top2(nc, tag, g, logits, slot, wt, fallback):
    with Scope(nc, tag) as s:
        probs = s.sb("probs", [P, TILES, E])
        top = s.sb("top", [P, 2, TILES])
        den = s.sb("den", [P, TILES])
        code = s.sb("code", [P, TILES, E])
        best = s.sb("best", [P, TILES])
        hot = s.sb("hot", [P, 2, TILES, E])
        match = s.sb("match", [P, TILES, E])
        second = s.sb("second", [P, TILES, E])
        pos = s.sb("pos", [P, TILES, E])
        elig = s.sb("elig", [P, TILES], BF16)
        before = s.sb("before", [P, TILES])
        over_cap = s.sb("over_cap", [P, TILES])
        valid = s.sb("valid", [P, TILES])
        slot_f = s.sb("slot_f", [P, 2, TILES])
        p_c = s.ps("p_c", [P, 2, TILES])
        vdone, counted, eligible = s.sem("vdone"), s.sem("counted"), s.sem("eligible")
        soft_v, soft_a = probabilities(nc, tag, s, logits, probs, top[:, 0, :])
        block = s.block()

        @block.scalar
        def _(act):
            soft_a(act)

        @block.tensor
        def _(pe):
            for e in range(E):
                pe.wait_ge(eligible, e + 1)
                nc.tensor.matmul(p_c[:, 0, :], g.upto[:, :], elig[:, :], start=True, stop=True)
                nc.tensor.matmul(p_c[:, 1, :], g.ones[:, :], elig[:, :], start=True, stop=True).then_inc(counted, 1)

        @block.vector
        def _(dve):
            link = Chain(dve, vdone)
            soft_v(link)
            first_largest(nc, link, probs[:, :, :], top[:, 0, :], g.rank, code, best, hot[:, 0, :, :])
            link(nc.vector.scalar_tensor_tensor(second[:, :, :], hot[:, 0, :, :], -2.0, probs[:, :, :], ALU.mult, ALU.add))
            link(nc.vector.tensor_reduce(top[:, 1, :], second[:, :, :], AX, ALU.max))
            first_largest(nc, link, second[:, :, :], top[:, 1, :], g.rank, code, best, hot[:, 1, :, :])
            link(nc.vector.tensor_tensor(den[:, :], top[:, 0, :], top[:, 1, :], ALU.add))
            link(nc.vector.tensor_scalar(den[:, :], den[:, :], 1e-9, None, ALU.max))
            link(nc.vector.reciprocal(den[:, :], den[:, :]))
            link(nc.vector.tensor_tensor(match[:, :, :], hot[:, 0, :, :], hot[:, 1, :, :], ALU.add))
            link(nc.vector.memset(fallback[:, :], 0.0))
            for e in range(E):
                nc.vector.scalar_tensor_tensor(elig[:, :], fallback[:, :], 0.5, match[:, :, e], ALU.is_lt, ALU.mult)\
                    .then_inc(eligible, 1)
                dve.wait_ge(counted, e + 1)
                link(nc.vector.tensor_tensor_scan(before[:, :], g.one32[:, :], p_c[:, 1, :], 0.0, ALU.mult, ALU.add))
                link(nc.vector.tensor_tensor(before[:, :], before[:, :], p_c[:, 1, :], ALU.subtract))
                link(nc.vector.scalar_tensor_tensor(before[:, :], p_c[:, 0, :], -1.0, before[:, :], ALU.add, ALU.add))
                nc.vector.tensor_scalar(pos[:, :, e], before[:, :], float(e * CAP0), None, ALU.add)
                link(nc.vector.scalar_tensor_tensor(over_cap[:, :], before[:, :], float(CAP0), elig[:, :], ALU.is_ge, ALU.mult))
                link(nc.vector.tensor_tensor(fallback[:, :], fallback[:, :], over_cap[:, :], ALU.max))
            link(nc.vector.tensor_scalar(valid[:, :], fallback[:, :], -1.0, 1.0, ALU.mult, ALU.add))
            for k in range(2):
                link(nc.vector.tensor_tensor(code[:, :, :], hot[:, k, :, :], pos[:, :, :], ALU.mult))
                link(nc.vector.tensor_reduce(slot_f[:, k, :], code[:, :, :], AX, ALU.add))
                link(nc.vector.scalar_tensor_tensor(slot_f[:, k, :], slot_f[:, k, :], g.trash[:, :], valid[:, :],
                                                    ALU.subtract, ALU.mult))
                link(nc.vector.tensor_scalar(slot_f[:, k, :], slot_f[:, k, :], g.trash[:, :], None, ALU.add))
                link(nc.vector.tensor_copy(slot[:, k, :], slot_f[:, k, :]))
                link(nc.vector.tensor_tensor(wt[:, k, :], top[:, k, :], den[:, :], ALU.mult))
                link(nc.vector.tensor_tensor(wt[:, k, :], wt[:, k, :], valid[:, :], ALU.mult))


def experts_top2(nc, tag, g):
    w = g.w0
    with Scope(nc, tag) as s:
        NU = len(UNITS0)
        pipe = FfnPipe(s, ahead=2 * NU)
        rows = s.sb("rows", [P, 2, ROWS0, D])
        outs = s.sb("outs", [P, E * ROWS0, D])
        w1 = s.sb("w1", [P, 2, FF])
        w2 = s.sb("w2", [P, 2, FC, D])
        bias = s.sb("bias", [P, 2, FC + 1])
        rows_in = [s.sem(f"rows_in{h}") for h in range(2)]
        weights_in = [s.sem(f"weights_in{h}") for h in range(2)]
        stored = [s.gather_sem(f"stored{h}") for h in range(2)]
        outs_ready = s.counter("outs_ready")
        block = s.block()
        first = [sum(UNITS0[:k]) for k in range(NU)]
        turn = [(h, k, UNITS0[k]) for h in range(2) for k in range(NU)]
        U = 2 * NU
        TURNS = E // 2

        def in_turns(eng, body):
            body(0, at_first=True)
            with eng.Fori(1, TURNS - 1) as i:
                body(i)
            body(TURNS - 1, at_last=True)

        @block.gpsimd
        def _(pool):
            with pool.Fori(0, E // 2) as i:
                for h in range(2):
                    pool.wait_ge(outs_ready.sem, outs_ready.ready(2 * i + h))
                    pool.dma_start(g.y_slots[bass.ds((2 * i + h) * CAP0, CAP0), :].rearrange("(p j) d -> p j d", p=P),
                                   tiles_of(outs, (2 * i + h) * ROWS0, ROWS0)).then_inc(stored[h], 16)
            for h in range(2):
                pool.wait_ge(stored[h], 16 * (E // 2))

        @block.sync
        def _(sp):
            with sp.Fori(0, E // 2) as i:
                for h in range(2):
                    e = 2 * i + h
                    sp.wait_ge(pipe.y_copied.sem, pipe.y_copied.free(NU * e + NU - 1))
                    sp.dma_start(w1[:, h, :], w["w1"][bass.ds(e * D, D), :]).then_inc(weights_in[h], 16)
                    sp.dma_start(w2[:, h, :, :], w["w2"][bass.ds(e * P, P), :].rearrange("p (c d) -> p c d", c=FC))\
                        .then_inc(weights_in[h], 16)
                    sp.dma_start(bias[:, h, :], w["b12"][bass.ds(e * P, P), :]).then_inc(weights_in[h], 16)
                    sp.wait_ge(pipe.x_transposed.sem, pipe.x_transposed.free(NU * e + NU - 1))
                    sp.dma_start(rows[:, h, :, :], g.x_slots[bass.ds(e * CAP0, CAP0), :]
                                 .rearrange("(p j) d -> p j d", p=P)).then_inc(rows_in[h], 16)

        @block.tensor
        def _(pe):
            pipe.pe_credits(pe)

            def into(i, n):
                h, k, m = turn[n % U]
                if k == 0:
                    pe.wait_ge(rows_in[h], 16 * (i + n // U) + 16)
                pipe.transpose_x(nc, pe, U * i + n, n % 2, [rows[:, h, first[k] + t, :] for t in range(m)], g.ident)

            def up(i, n):
                h, k, m = turn[n]
                if k == 0:
                    pe.wait_ge(weights_in[h], 48 * i + 48)
                pe.wait_ge(pipe.x_copied.sem, pipe.x_copied.ready(U * i + n))
                pipe.up(nc, pe, U * i + n, pipe.xg[:, n % 2, 0:m * P], w1[:, h, :])

            def down(i, n):
                h, k, m = turn[n % U]
                pipe.down(nc, pe, U * i + n, n % 2, m, w2[:, h, :, :])

            def out(i, n):
                pipe.transpose_y(nc, pe, U * i + n, n % 2, turn[n % U][2], g.ident)

            def two_experts(i, at_first=False, at_last=False):
                for n in range(U):
                    if not (at_last and n == U - 1):
                        into(i, n + 1)
                    up(i, n)
                    if not (at_first and n < 1):
                        down(i, n - 1)
                    if not (at_first and n < 2):
                        out(i, n - 2)

            into(0, 0)
            in_turns(pe, two_experts)
            down(TURNS - 1, U - 1)
            out(TURNS - 1, U - 2)
            out(TURNS - 1, U - 1)

        @block.scalar
        def _(act):
            pipe.act_credits(act)

            def copy_y(i, n):
                h, k, m = turn[n % U]
                pipe.copy_y(nc, act, U * i + n, n % 2, m, bias[:, h, FC:FC + 1])

            def two_experts(i, at_first=False, at_last=False):
                for n in range(U):
                    h, _, m = turn[n]
                    if not (at_last and n == U - 1):
                        pipe.copy_x(nc, act, U * i + n + 1, (n + 1) % 2, turn[(n + 1) % U][2])
                    pipe.gelu(nc, act, U * i + n, n % 2, m, bias[:, h, 0:FC])
                    if not (at_first and n < 1):
                        copy_y(i, n - 1)

            pipe.copy_x(nc, act, 0, 0, turn[0][2])
            in_turns(act, two_experts)
            copy_y(TURNS - 1, U - 1)

        @block.vector
        def _(dve):
            dve.sem_inc(pipe.rows_taken.sem, 1)
            with dve.Fori(0, E // 2) as i:
                for n, (h, k, m) in enumerate(turn):
                    pipe.take_rows(nc, dve, 2 * NU * i + n, m, tiles_of(outs, (2 * i + h) * ROWS0 + first[k], m))
                    if k == NU - 1:
                        dve.wait_ge(pipe.rows_taken.sem, pipe.rows_taken.ready(2 * NU * i + n))
                        dve.sem_inc(outs_ready.sem, 1)


def later_constants(nc, s, g, io):
    hawk_vector, hawk_scalar = hawk_constants(nc, s, g)
    fuse_sync, fuse_tensor, fuse_vector = fuse_experts(nc, s, g, io)

    def vector(dve):
        hawk_vector(dve)
        fuse_vector(dve)

    return fuse_sync, fuse_tensor, vector, hawk_scalar


def combine_top2(nc, tag, g, x, yfb, slot, wt, fallback, io):
    PART = 8
    with Scope(nc, tag) as s:
        got = s.sb("got", [P, 2, TILES, D])
        gathered = [s.gather_sem(f"gathered{q}") for q in range(TILES // PART)]
        vdone = s.sem("vdone")
        beside = later_constants(nc, s, g, io) if io else None
        block = s.block()
        if beside:
            sync, tensor, vector, scalar = beside
            block.sync(sync)
            block.tensor(tensor)
            block.scalar(scalar)

        @block.gpsimd
        def _(pool):
            for t in range(TILES):
                for k in range(2):
                    pool.indirect_dma_start(got[:, k, t, :], None, g.y_slots,
                                            bass.IndirectOffsetOnAxis(ap=slot[:, k, t:t + 1], axis=0))\
                        .then_inc(gathered[t // PART], 16)

        @block.vector
        def _(dve):
            if beside:
                vector(dve)
            link = Chain(dve, vdone)
            for q in range(TILES // PART):
                part = slice(q * PART, (q + 1) * PART)
                a, b, f = got[:, 0, part, :], got[:, 1, part, :], yfb[:, part, :]
                link(nc.vector.tensor_tensor(f, f, over(fallback[:, part], D), ALU.mult))
                dve.wait_ge(gathered[q], 16 * 2 * PART)
                nc.vector.tensor_tensor(a, a, over(wt[:, 0, part], D), ALU.mult).then_inc(vdone, 1)
                link.n += 1
                link(nc.vector.tensor_tensor(b, b, over(wt[:, 1, part], D), ALU.mult))
                link(nc.vector.tensor_tensor(a, a, b, ALU.add))
                link(nc.vector.tensor_tensor(a, a, f, ALU.add))
                link(nc.vector.scalar_tensor_tensor(x[:, part, :], a, 0.5, x[:, part, :], ALU.mult, ALU.add))
                for t in range(q * PART, (q + 1) * PART):
                    nc.vector.bn_stats(g.stats[:, t, :], x[:, t, :])



HID = 192
REST = HID - P
SEGS = 3
QUARTERS = SEQ // GROUP
BTILES = SEQ // P


def seg(buf, j, i):
    return buf[:, bass.ds(j * SEQ + i * GROUP, GROUP)]


def whole(buf, j):
    return buf[:, j * SEQ:(j + 1) * SEQ]


def btiles(buf, b, i, t=0, n=TPG):
    return buf[:, bass.ds(TPG * i + (BTILES * b + t), n), :]


def bcol(buf, b, i, t):
    return buf[:, bass.ds(TPG * i + (BTILES * b + t), 1)]


def hawk(nc, tag, g, x, src=None):
    with Scope(nc, tag) as s:
        mean, r_ln, r_rms = (s.sb(n, [P, TILES]) for n in ("mean", "r_ln", "r_rms"))
        z = s.sb("z", [P, TILES, D])
        row_stats(nc, tag + "s", g.stats, mean, [(r_ln, LN_EPS, True), (r_rms, 0.0, True)], src)
        with Scope(nc, tag + "w") as s2:
            gate = s2.sb("gate", [P, SEGS * SEQ])
            conv = s2.sb("conv", [P, SEGS * SEQ])
            inp = s2.sb("inp", [P, SEGS * SEQ])
            with Scope(nc, tag + "v") as s3:
                v = s3.sb("v", [P, SEGS * SEQ])
                hawk_project(nc, tag + "p", g, x, mean, r_ln, r_rms, z, gate, v)
                hawk_conv(nc, tag + "c", g, v, conv)
            with Scope(nc, tag + "f") as s3:
                forget = s3.sb("forget", [P, SEGS * SEQ])
                hawk_gates(nc, tag + "g", g, conv, forget, inp)
                hawk_scan(nc, tag + "r", g, forget, inp, conv, gate)
            hawk_out(nc, tag + "o", g, gate, z)
        row_stats(nc, tag + "t", g.stats, mean, [(r_rms, 0.0, False)])
        hawk_mlp(nc, tag + "m", g, x, z, r_rms)


def hawk_project(nc, tag, g, x, mean, r_ln, r_rms, z, gate, v):
    w = g.w1
    with Scope(nc, tag) as s:
        zs = s.sb("zs", [P, 2, TPG, D])
        zg = s.sb("zg", [P, 2, GROUP])
        p_x = s.ps("p_x", [P, 2, GROUP])
        p_g = s.ps("p_g", [P, SEGS, GROUP])
        p_v = s.ps("p_v", [P, SEGS, GROUP])
        normalized = s.counter("normalized")
        transposed = s.counter("transposed", 2)
        copied = s.counter("copied", 2)
        gate_done = s.counter("gate_done")
        v_done = s.counter("v_done", SEGS)
        gate_kept = s.counter("gate_kept", SEGS)
        v_kept = s.counter("v_kept", SEGS)
        block = s.block()

        @block.vector
        def _(dve):
            dve.sem_inc(v_kept.sem, SEGS)
            with dve.Fori(0, QUARTERS) as i:
                for b in range(2):
                    dve.wait_ge(transposed.sem, transposed.free(2 * i + b))
                    for t in range(TPG):
                        last = nc.vector.tensor_scalar(zs[:, b, t:t + 1, :], btiles(x, b, i, t, 1), bcol(mean, b, i, t),
                                                       bcol(r_rms, b, i, t), ALU.subtract, ALU.mult)
                    last.then_inc(normalized.sem, 1)
                for b in range(2):
                    for t in range(TPG):
                        nc.vector.tensor_scalar(btiles(z, b, i, t, 1), btiles(x, b, i, t, 1), bcol(mean, b, i, t),
                                                bcol(r_ln, b, i, t), ALU.subtract, ALU.mult)
                for j in range(SEGS):
                    dve.wait_ge(v_done.sem, v_done.ready(SEGS * i + j))
                    nc.vector.tensor_copy(seg(v, j, i), p_v[:, j, :]).then_inc(v_kept.sem, 1)

        @block.tensor
        def _(pe):
            pe.sem_inc(transposed.sem, 2)
            pe.sem_inc(v_done.sem, SEGS)
            with pe.Fori(0, QUARTERS) as i:
                for b in range(2):
                    pe.wait_ge(normalized.sem, normalized.ready(2 * i + b))
                    pe.wait_ge(copied.sem, copied.free(2 * i + b))
                    for t in range(TPG):
                        last = nc.tensor.transpose(p_x[:, b, t * P:(t + 1) * P], zs[:, b, t, :], g.ident)
                    last.then_inc(transposed.sem, 1)
                pe.wait_ge(copied.sem, copied.ready(2 * i + 1))
                for bank, kept, done, w_a, w_r in ((p_g, gate_kept, gate_done, w["in_ga"], w["in_gr"]),
                                                   (p_v, v_kept, v_done, w["in_va"], w["in_vr"])):
                    for b in range(2):
                        pe.wait_ge(kept.sem, kept.free(SEGS * i + b))
                        nc.tensor.matmul(bank[:, b, :], w_a, zg[:, b, :], start=True, stop=True).then_inc(done.sem, 1)
                    pe.wait_ge(kept.sem, kept.free(SEGS * i + 2))
                    nc.tensor.matmul(bank[:, 2, :], w_r[:, 0, :], zg[:, 0, :], start=True, stop=False)
                    nc.tensor.matmul(bank[:, 2, :], w_r[:, 1, :], zg[:, 1, :], start=False, stop=True).then_inc(done.sem, 1)

        @block.scalar
        def _(act):
            act.sem_inc(copied.sem, 2)
            act.sem_inc(gate_kept.sem, SEGS)
            with act.Fori(0, QUARTERS) as i:
                act.wait_ge(v_done.sem, v_done.free(SEGS * i + 2))
                for b in range(2):
                    act.wait_ge(transposed.sem, transposed.ready(2 * i + b))
                    nc.scalar.activation(zg[:, b, :], p_x[:, b, :], ACT.Copy).then_inc(copied.sem, 1)
                for j in range(SEGS):
                    act.wait_ge(gate_done.sem, gate_done.ready(SEGS * i + j))
                    nc.scalar.activation(seg(gate, j, i), p_g[:, j, :], ACT.Gelu).then_inc(gate_kept.sem, 1)


def hawk_conv(nc, tag, g, v, conv):
    w = g.w1
    TAPS = 4
    with Scope(nc, tag) as s:
        first_tap, vdone = s.sem("first_tap"), s.sem("vdone")
        block = s.block()

        @block.scalar
        def _(act):
            for j in range(SEGS):
                c = j // 2
                nc.scalar.activation(whole(conv, j), whole(v, j), ACT.Identity, bias=w["conv_b"][:, c:c + 1],
                                     scale=w["conv_w"][:, TAPS * c + TAPS - 1:TAPS * c + TAPS]).then_inc(first_tap, 1)

        @block.vector
        def _(dve):
            link = Chain(dve, vdone)
            for j in range(SEGS):
                dve.wait_ge(first_tap, j + 1)
                for k in range(1, TAPS):
                    col = TAPS * (j // 2) + TAPS - 1 - k
                    out = conv[:, j * SEQ + k:(j + 1) * SEQ]
                    link(nc.vector.scalar_tensor_tensor(out, v[:, j * SEQ:(j + 1) * SEQ - k], w["conv_w"][:, col:col + 1], out,
                                                        ALU.mult, ALU.add))


def hawk_gates(nc, tag, g, conv, forget, inp):
    w = g.w1
    with Scope(nc, tag) as s:
        p_f = s.ps("p_f", [P, SEGS, GROUP])
        p_i = s.ps("p_i", [P, SEGS, GROUP])
        done = s.counter("done")
        kept = s.counter("kept", 2 * SEGS)
        block = s.block()

        @block.tensor
        def _(pe):
            with pe.Fori(0, QUARTERS) as i:
                for n, (bank, aa, ra, ar, rr) in enumerate(((p_f, w["f_aa"], w["f_ra"], w["f_ar"], w["f_rr"]),
                                                            (p_i, w["i_aa"], w["i_ra"], w["i_ar"], w["i_rr"]))):
                    for b in range(2):
                        pe.wait_ge(kept.sem, kept.free(2 * SEGS * i + SEGS * n + b))
                        nc.tensor.matmul(bank[:, b, :], aa, seg(conv, b, i), start=True, stop=False)
                        nc.tensor.matmul(bank[:, b, :], ra[:, b, :], seg(conv, 2, i), start=False, stop=True).then_inc(done.sem, 1)
                    pe.wait_ge(kept.sem, kept.free(2 * SEGS * i + SEGS * n + 2))
                    for b in range(2):
                        nc.tensor.matmul(bank[:, 2, :], ar[:, b, :], seg(conv, b, i), start=(b == 0), stop=False)
                    nc.tensor.matmul(bank[:, 2, :], rr, seg(conv, 2, i), start=False, stop=True).then_inc(done.sem, 1)

        @block.scalar
        def _(act):
            act.sem_inc(kept.sem, 2 * SEGS)
            with act.Fori(0, QUARTERS) as i:
                for n, (bank, out) in enumerate(((p_f, forget), (p_i, inp))):
                    for j in range(SEGS):
                        act.wait_ge(done.sem, done.ready(2 * SEGS * i + SEGS * n + j))
                        nc.scalar.activation(seg(out, j, i), bank[:, j, :], ACT.Sigmoid,
                                             bias=w["b_gates"][:, 2 * n + j // 2:2 * n + j // 2 + 1]).then_inc(kept.sem, 1)


def hawk_scan(nc, tag, g, forget, inp, conv, gate):
    with Scope(nc, tag) as s:
        beta = s.sb("beta", [P, SEGS * SEQ])
        alpha_done, square_done, beta_done, vdone, one_minus = (s.sem(n) for n in ("alpha", "square", "beta_done", "vdone", "one_minus"))
        block = s.block()

        @block.scalar
        def _(act):
            for j in range(SEGS):
                nc.scalar.activation(whole(forget, j), whole(forget, j), ACT.Exp, scale=g.decay[:, j // 2:j // 2 + 1])\
                    .then_inc(alpha_done, 1)
            for j in range(SEGS):
                act.wait_ge(alpha_done, j + 1)
                nc.scalar.activation(whole(beta, j), whole(forget, j), ACT.Square).then_inc(square_done, 1)
            for j in range(SEGS):
                act.wait_ge(one_minus, j + 1)
                nc.scalar.activation(whole(beta, j), whole(beta, j), ACT.Sqrt, bias=g.tiny[:, :]).then_inc(beta_done, 1)

        @block.vector
        def _(dve):
            link = Chain(dve, vdone)
            for j in range(SEGS):
                link(nc.vector.tensor_tensor(whole(inp, j), whole(inp, j), whole(conv, j), ALU.mult))
            for j in range(SEGS):
                dve.wait_ge(square_done, j + 1)
                nc.vector.tensor_scalar(whole(beta, j), whole(beta, j), -1.0, 1.0, ALU.mult, ALU.add).then_inc(one_minus, 1)
            for j in range(SEGS):
                dve.wait_ge(beta_done, j + 1)
                link(nc.vector.tensor_tensor(whole(inp, j), whole(inp, j), whole(beta, j), ALU.mult))
                link(nc.vector.tensor_tensor_scan(whole(conv, j), whole(forget, j), whole(inp, j), 0.0, ALU.mult, ALU.add))
                link(nc.vector.tensor_tensor(whole(gate, j), whole(gate, j), whole(conv, j), ALU.mult))


def hawk_out(nc, tag, g, gate, z):
    w = g.w1
    with Scope(nc, tag) as s:
        yt = s.sb("yt", [P, 2, GROUP])
        p_y = s.ps("p_y", [P, 2, GROUP])
        p_r = s.ps("p_r", [P, 2, GROUP])
        projected = s.counter("projected")
        copied = s.counter("copied", 2)
        transposed = s.counter("transposed", 2)
        added = s.counter("added", 2)
        block = s.block()

        @block.tensor
        def _(pe):
            pe.sem_inc(transposed.sem, 2)
            with pe.Fori(0, QUARTERS) as i:
                for b in range(2):
                    pe.wait_ge(copied.sem, copied.free(2 * i + b))
                    nc.tensor.matmul(p_y[:, b, :], w["out_a"], seg(gate, b, i), start=True, stop=False)
                    nc.tensor.matmul(p_y[:, b, :], w["out_r"][:, b, :], seg(gate, 2, i), start=False, stop=True)\
                        .then_inc(projected.sem, 1)
                for b in range(2):
                    pe.wait_ge(copied.sem, copied.ready(2 * i + b))
                    pe.wait_ge(added.sem, added.free(2 * i + b))
                    for t in range(TPG):
                        last = nc.tensor.transpose(p_r[:, b, t * P:(t + 1) * P], yt[:, b, t * P:(t + 1) * P], g.ident)
                    last.then_inc(transposed.sem, 1)

        @block.scalar
        def _(act):
            act.sem_inc(copied.sem, 2)
            with act.Fori(0, QUARTERS) as i:
                for b in range(2):
                    act.wait_ge(projected.sem, projected.ready(2 * i + b))
                    act.wait_ge(transposed.sem, transposed.free(2 * i + b))
                    nc.scalar.activation(yt[:, b, :], p_y[:, b, :], ACT.Copy).then_inc(copied.sem, 1)

        @block.vector
        def _(dve):
            dve.sem_inc(added.sem, 2)
            with dve.Fori(0, QUARTERS) as i:
                for b in range(2):
                    dve.wait_ge(transposed.sem, transposed.ready(2 * i + b))
                    nc.vector.tensor_tensor(btiles(z, b, i), p_r[:, b, :].rearrange("p (t d) -> p t d", d=D), btiles(z, b, i),
                                            ALU.add).then_inc(added.sem, 1)
                for b in range(2):
                    dve.wait_ge(added.sem, added.ready(2 * i + b))
                    for t in range(TPG):
                        nc.vector.bn_stats(btiles(g.stats, b, i, t, 1), btiles(z, b, i, t, 1))


def hawk_mlp(nc, tag, g, x, z, r_rms):
    w = g.w1
    GC = 2
    with Scope(nc, tag) as s:
        zs = s.sb("zs", [P, 2, TPG, D])
        zg = s.sb("zg", [P, 2, GROUP])
        hid = s.sb("hid", [P, 2, GC, GROUP])
        yt = s.sb("yt", [P, 2, GROUP])
        p_x = s.ps("p_x", [P, 2, GROUP])
        p_g = s.ps("p_g", [P, GC, GROUP])
        p_v = s.ps("p_v", [P, GC, GROUP])
        p_y = s.ps("p_y", [P, GROUP])
        p_r = s.ps("p_r", [P, GROUP])
        normalized = s.counter("normalized")
        transposed = s.counter("transposed", 2)
        copied = s.counter("copied", 2)
        gate_done = s.counter("gate_done")
        value_done = s.counter("value_done", 2 * GC)
        gelu_done = s.counter("gelu_done", GC)
        product_done = s.counter("product_done", GC)
        shrunk = s.counter("shrunk", 2)
        y_copied = s.counter("y_copied", 1)
        y_transposed = s.counter("y_transposed", 2)
        added = s.counter("added", 1)
        x_done = s.counter("x_done")
        block = s.block()

        def in_turns(eng, turn):
            turn(0, at_first=True)
            with eng.Fori(1, QUARTERS - 1) as i:
                turn(i)
            turn(QUARTERS - 1, at_last=True)

        def before(i, b):
            return (i, 0) if b else (i - 1, 1)

        def behind(i, b):
            return (i + 1, 0) if b else (i, 1)

        @block.vector
        def _(dve):
            dve.sem_inc(product_done.sem, GC)
            dve.sem_inc(added.sem, 1)

            def normalize(i, b):
                dve.wait_ge(transposed.sem, transposed.free(2 * i + b))
                for t in range(TPG):
                    last = nc.vector.tensor_scalar(zs[:, b, t:t + 1, :], btiles(z, b, i, t, 1), bcol(r_rms, b, i, t),
                                                   None, ALU.mult)
                last.then_inc(normalized.sem, 1)

            def multiply(i, b):
                for c in range(GC):
                    k = GC * (2 * i + b) + c
                    dve.wait_ge(value_done.sem, value_done.ready(k))
                    dve.wait_ge(gelu_done.sem, gelu_done.ready(k))
                    nc.vector.tensor_tensor(hid[:, b, c, :], hid[:, b, c, :], p_v[:, c, :], ALU.mult)\
                        .then_inc(product_done.sem, 1)

            def add(i, b):
                u = 2 * i + b
                dve.wait_ge(y_transposed.sem, y_transposed.ready(u))
                nc.vector.tensor_tensor(btiles(z, b, i), p_r[:, :].rearrange("p (t d) -> p t d", d=D), btiles(z, b, i),
                                        ALU.add).then_inc(added.sem, 1)
                dve.wait_ge(added.sem, added.ready(u))
                nc.vector.tensor_tensor(btiles(x, b, i), btiles(x, b, i), btiles(z, b, i), ALU.add).then_inc(x_done.sem, 1)
                dve.wait_ge(x_done.sem, x_done.ready(u))
                for t in range(TPG):
                    nc.vector.bn_stats(btiles(g.stats, b, i, t, 1), btiles(x, b, i, t, 1))

            def turn(i, at_first=False, at_last=False):
                for b in range(2):
                    multiply(i, b)
                    if not at_last:
                        normalize(i + 1, b)
                    if not at_first:
                        add(i - 1, b)

            for b in range(2):
                normalize(0, b)
            in_turns(dve, turn)
            for b in range(2):
                add(QUARTERS - 1, b)

        @block.tensor
        def _(pe):
            pe.sem_inc(transposed.sem, 2)
            pe.sem_inc(value_done.sem, 2 * GC)
            pe.sem_inc(shrunk.sem, 2)
            pe.sem_inc(y_transposed.sem, 2)

            def transpose(i, b):
                pe.wait_ge(normalized.sem, normalized.ready(2 * i + b))
                pe.wait_ge(copied.sem, copied.free(2 * i + b))
                for t in range(TPG):
                    last = nc.tensor.transpose(p_x[:, b, t * P:(t + 1) * P], zs[:, b, t, :], g.ident)
                last.then_inc(transposed.sem, 1)

            def grow(i, b):
                pe.wait_ge(copied.sem, copied.ready(2 * i + b))
                for c in range(GC):
                    k = GC * (2 * i + b) + c
                    pe.wait_ge(gelu_done.sem, gelu_done.free(k))
                    nc.tensor.matmul(p_g[:, c, :], w["grow"][:, c * P:(c + 1) * P], zg[:, b, :], start=True, stop=True)\
                        .then_inc(gate_done.sem, 1)
                    pe.wait_ge(product_done.sem, product_done.free(k))
                    nc.tensor.matmul(p_v[:, c, :], w["grow"][:, (GC + c) * P:(GC + c + 1) * P], zg[:, b, :],
                                     start=True, stop=True).then_inc(value_done.sem, 1)

            def shrink(i, b):
                pe.wait_ge(product_done.sem, product_done.ready(GC * (2 * i + b) + GC - 1))
                pe.wait_ge(y_copied.sem, y_copied.free(2 * i + b))
                for c in range(GC):
                    last = nc.tensor.matmul(p_y[:, :], w["shrink"][:, c, :], hid[:, b, c, :], start=(c == 0), stop=(c == GC - 1))
                last.then_inc(shrunk.sem, 1)

            def transpose_back(i, b):
                pe.wait_ge(y_copied.sem, y_copied.ready(2 * i + b))
                pe.wait_ge(added.sem, added.free(2 * i + b))
                for t in range(TPG):
                    last = nc.tensor.transpose(p_r[:, t * P:(t + 1) * P], yt[:, b, t * P:(t + 1) * P], g.ident)
                last.then_inc(y_transposed.sem, 1)

            def turn(i, at_first=False, at_last=False):
                for b in range(2):
                    if not (at_last and b == 1):
                        transpose(*behind(i, b))
                    grow(i, b)
                    if not (at_first and b == 0):
                        shrink(*before(i, b))
                    if not at_first:
                        transpose_back(i - 1, b)

            transpose(0, 0)
            in_turns(pe, turn)
            shrink(QUARTERS - 1, 1)
            for b in range(2):
                transpose_back(QUARTERS - 1, b)

        @block.scalar
        def _(act):
            act.sem_inc(copied.sem, 2)
            act.sem_inc(gelu_done.sem, GC)
            act.sem_inc(y_copied.sem, 1)

            def copy_x(i, b):
                act.wait_ge(transposed.sem, transposed.ready(2 * i + b))
                act.wait_ge(value_done.sem, value_done.free(GC * (2 * i + b) + GC - 1))
                nc.scalar.activation(zg[:, b, :], p_x[:, b, :], ACT.Copy).then_inc(copied.sem, 1)

            def gelu(i, b):
                act.wait_ge(shrunk.sem, shrunk.free(2 * i + b))
                for c in range(GC):
                    act.wait_ge(gate_done.sem, gate_done.ready(GC * (2 * i + b) + c))
                    nc.scalar.activation(hid[:, b, c, :], p_g[:, c, :], ACT.Gelu).then_inc(gelu_done.sem, 1)

            def copy_y(i, b):
                act.wait_ge(shrunk.sem, shrunk.ready(2 * i + b))
                act.wait_ge(y_transposed.sem, y_transposed.free(2 * i + b))
                nc.scalar.activation(yt[:, b, :], p_y[:, :], ACT.Copy).then_inc(y_copied.sem, 1)

            def turn(i, at_first=False, at_last=False):
                for b in range(2):
                    if not (at_last and b == 1):
                        copy_x(*behind(i, b))
                    gelu(i, b)
                    if not (at_first and b == 0):
                        copy_y(*before(i, b))

            copy_x(0, 0)
            in_turns(act, turn)
            copy_y(QUARTERS - 1, 1)


def hawk_constants(nc, s, g):
    w = g.w1
    a, e, d, y, y2, acc = (s.sb(n, [P, 2]) for n in ("a", "e", "d", "y", "y2", "acc"))
    cdone, negated, exps = s.sem("cdone"), s.sem("negated"), s.sem("exps")

    def scalar(act):
        act.wait_ge(negated, 1)
        nc.scalar.activation(e[:, :], a[:, :], ACT.Exp).then_inc(exps, 1)

    def vector(dve):
        link = Chain(dve, cdone)
        dve.wait_ge(g.pack_in[1], 16)
        for m in (w["in_all"], w["grow"]):
            link(nc.vector.tensor_scalar(m, m, w["gamma1"] if m is w["in_all"] else w["gamma2"], None, ALU.mult))
        link(nc.vector.memset(g.tiny[:, :], 1e-6))
        link(nc.vector.tensor_scalar(d[:, :], w["forget_base"], -1.0, None, ALU.mult))
        nc.vector.tensor_tensor(a[:, :], w["forget_base"], d[:, :], ALU.min).then_inc(negated, 1)
        dve.wait_ge(exps, 1)
        link(nc.vector.tensor_scalar(d[:, :], e[:, :], 2.0, None, ALU.add))
        link(nc.vector.reciprocal(d[:, :], d[:, :]))
        link(nc.vector.tensor_tensor(y[:, :], e[:, :], d[:, :], ALU.mult))
        link(nc.vector.tensor_tensor(y2[:, :], y[:, :], y[:, :], ALU.mult))
        link(nc.vector.memset(acc[:, :], 1.0 / 17))
        for k in range(15, 0, -2):
            link(nc.vector.tensor_tensor(acc[:, :], acc[:, :], y2[:, :], ALU.mult))
            link(nc.vector.tensor_scalar(acc[:, :], acc[:, :], 1.0 / k, None, ALU.add))
        link(nc.vector.tensor_tensor(acc[:, :], acc[:, :], y[:, :], ALU.mult))
        link(nc.vector.tensor_scalar(d[:, :], w["forget_base"], 0.0, None, ALU.max))
        link(nc.vector.scalar_tensor_tensor(acc[:, :], acc[:, :], 2.0, d[:, :], ALU.mult, ALU.add))
        link(nc.vector.tensor_scalar(g.decay[:, :], acc[:, :], -8.0, None, ALU.mult))

    return vector, scalar



HEADS, HD = 4, 32
SC = 2 * 2 * HEADS


def fuse_experts(nc, s, g, io):
    w = g.w2
    w1t = s.sb("w1t", [P, E * FC, D])
    w2 = s.sb("w2", [P, E * FC, D])
    b12t = s.sb("b12t", [P, TPG, 32])
    p_w = s.ps("p_w", [P, E, D])
    p_b = s.ps("p_b", [P, E])
    p_t = s.ps("p_t", [P, P])
    w1_in, w2_in, emptied, fused, copied, turned = (
        s.sem(n) for n in ("w1_in", "w2_in", "emptied", "fused", "copied", "turned"))

    def sync(sp):
        sp.dma_start(w1t[:, :, :], io["w1t_top1"].rearrange("p (n d) -> p n d", d=D)).then_inc(w1_in, 16)
        sp.dma_start(w2[:, :, :], io["w2_top1"].rearrange("p (n d) -> p n d", d=D)).then_inc(w2_in, 16)

    def tensor(pe):
        pe.wait_ge(g.pack_in[2], 16)
        pe.wait_ge(w1_in, 16)
        pe.wait_ge(w2_in, 16)
        for e in range(E):
            for c in range(FC):
                nc.tensor.matmul(p_b[:, e:e + 1], w2[:, e * FC + c, :], w["b1"][:, e * FC + c:e * FC + c + 1],
                                 start=(c == 0), stop=(c == FC - 1))
        for e in range(E):
            for c in range(FC):
                last = nc.tensor.matmul(p_w[:, e, :], w1t[:, e * FC + c, :], w2[:, e * FC + c, :],
                                        start=(c == 0), stop=(c == FC - 1))
        last.then_inc(fused, 1)
        pe.wait_ge(copied, 1)
        nc.tensor.transpose(p_t[:, :], b12t[:, :, :].rearrange("p t e -> p (t e)"), g.ident).then_inc(turned, 1)

    def vector(dve):
        link = Chain(dve, emptied)
        link(nc.vector.memset(g.b12[:, :, :], 0.0))
        link(nc.vector.memset(b12t[:, :, :], 0.0))
        dve.wait_ge(fused, 1)
        for t in range(TPG):
            last = nc.vector.tensor_tensor(b12t[:, t, 0:E], p_b[:, :], w["b2"], ALU.add)
        last.then_inc(copied, 1)
        nc.vector.tensor_copy(g.w12[:, :, :], p_w[:, :, :])
        dve.wait_ge(turned, 1)
        for t in range(TPG):
            nc.vector.tensor_copy(g.b12[t * 32:(t + 1) * 32, t, :], p_t[t * 32:(t + 1) * 32, :])

    return sync, tensor, vector


def pair_moe(nc, tag, g, x, src=None):
    with Scope(nc, tag) as s:
        mean, rstd = s.sb("mean", [P, TILES]), s.sb("rstd", [P, TILES])
        z = s.sb("z", [P, TILES, D])
        row_stats(nc, tag + "s", g.stats, mean, [(rstd, LN_EPS, True)], src)
        with Scope(nc, tag + "A") as s2:
            v = s2.sb("v", [P, BTILES, 2, D])
            scores = s2.sb("scores", [P, BTILES, SC])
            pair_scores(nc, tag + "q", g, x, mean, rstd, z, v, scores)
            pair_softmax(nc, tag + "m", g, scores)
            pair_attend(nc, tag + "a", g, scores, v, z)
        row_stats(nc, tag + "t", g.stats, mean, [(rstd, LN_EPS, True)], z)
        with Scope(nc, tag + "B") as s2:
            yt = s2.sb("yt", [P, TOK])
            logits = s2.sb("logits", [P, TILES, E])
            wt = s2.sb("wt", [P, TILES, 32])
            wtt = s2.sb("wtt", [P, GROUPS, P])
            top1_logits(nc, tag + "g", g, z, mean, rstd, yt, logits)
            route_top1(nc, tag + "r", g, logits, wt, wtt)
            experts_top1(nc, tag + "e", g, yt, wt, wtt, z)
        row_stats(nc, tag + "u", g.stats, mean, [(rstd, LN_EPS, True)], z)
        add_normed(nc, tag + "f", g, z, mean, rstd, x)


def pair_scores(nc, tag, g, x, mean, rstd, z, v, scores):
    w = g.w2
    with Scope(nc, tag) as s:
        zs = s.sb("zs", [P, 2, TPG, D])
        zg = s.sb("zg", [P, 2, GROUP])
        qk = s.sb("qk", [P, 2, 2, 2 * D])
        prod = s.sb("prod", [P, 2, 2, 2, D])
        p_x = s.ps("p_x", [P, 2, GROUP])
        p_q = s.ps("p_q", [P, 2, 2, GROUP])
        normalized = s.counter("normalized")
        z_kept = s.counter("z_kept", 2)
        transposed = s.counter("transposed", 2)
        copied = s.counter("copied", 2)
        projected = s.counter("projected", TPG)
        biased = s.counter("biased")
        values_kept = s.counter("values_kept", 2)
        multiplied = s.counter("multiplied", 2)
        reduced = s.counter("reduced", 2)
        block = s.block()

        @block.vector
        def _(dve):
            dve.sem_inc(multiplied.sem, 2)
            dve.sem_inc(reduced.sem, 2)

            def normalize(i):
                for b in range(2):
                    dve.wait_ge(transposed.sem, transposed.free(2 * i + b))
                    dve.wait_ge(z_kept.sem, z_kept.free(2 * i + b))
                    for t in range(TPG):
                        last = nc.vector.tensor_scalar(zs[:, b, t:t + 1, :], btiles(x, b, i, t, 1), bcol(mean, b, i, t),
                                                       bcol(rstd, b, i, t), ALU.subtract, ALU.mult)
                    last.then_inc(normalized.sem, 1)

            def score(i):
                for two in range(0, TPG, 2):
                    for h in range(2):
                        k = TPG * i + two + h
                        dve.wait_ge(projected.sem, projected.ready(k))
                        dve.wait_ge(multiplied.sem, multiplied.free(k))
                        nc.vector.tensor_tensor(qk[:, h, :, :], p_q[:, h, :, 0:2 * D],
                                                w["qkv_b"][:, 0:2 * D].unsqueeze(1).to_broadcast([P, 2, 2 * D]), ALU.add)\
                            .then_inc(biased.sem, 1)
                    for h in range(2):
                        k = TPG * i + two + h
                        dve.wait_ge(biased.sem, biased.ready(k))
                        dve.wait_ge(reduced.sem, reduced.free(k))
                        nc.vector.tensor_tensor(prod[:, h, :, :, :], qk[:, h, :, 0:D].unsqueeze(2).to_broadcast([P, 2, 2, D]),
                                                qk[:, h, :, D:2 * D].unsqueeze(1).to_broadcast([P, 2, 2, D]), ALU.mult)\
                            .then_inc(multiplied.sem, 1)
                    for h in range(2):
                        k = TPG * i + two + h
                        dve.wait_ge(multiplied.sem, multiplied.ready(k))
                        nc.vector.tensor_reduce(scores[:, bass.ds(k, 1), :],
                                                prod[:, h, :, :, :].rearrange("p l m (h c) -> p (l m h) c", c=HD), AX, ALU.add)\
                            .then_inc(reduced.sem, 1)

            normalize(0)
            with dve.Fori(0, QUARTERS - 1) as i:
                normalize(i + 1)
                score(i)
            score(QUARTERS - 1)

        @block.gpsimd
        def _(pool):
            pool.sem_inc(z_kept.sem, 2)
            with pool.Fori(0, QUARTERS) as i:
                for b in range(2):
                    pool.wait_ge(normalized.sem, normalized.ready(2 * i + b))
                    nc.gpsimd.tensor_tensor(btiles(z, b, i), zs[:, b, :, :],
                                            w["out_b"].unsqueeze(1).to_broadcast([P, TPG, D]), ALU.add).then_inc(z_kept.sem, 1)
                for t in range(TPG):
                    k = TPG * i + t
                    pool.wait_ge(values_kept.sem, values_kept.ready(k))
                    vk = v[:, bass.ds(k, 1), :, :].rearrange("p a m d -> p (a m) d")
                    nc.gpsimd.tensor_tensor(vk, vk, w["qkv_b"][:, 2 * D:3 * D].unsqueeze(1).to_broadcast([P, 2, D]), ALU.add)

        @block.tensor
        def _(pe):
            pe.sem_inc(transposed.sem, 2)
            pe.sem_inc(projected.sem, TPG)

            def transpose(i):
                for b in range(2):
                    pe.wait_ge(normalized.sem, normalized.ready(2 * i + b))
                    pe.wait_ge(copied.sem, copied.free(2 * i + b))
                    for t in range(TPG):
                        last = nc.tensor.transpose(p_x[:, b, t * P:(t + 1) * P], zs[:, b, t, :], g.ident)
                    last.then_inc(transposed.sem, 1)

            def project(i):
                pe.wait_ge(copied.sem, copied.ready(2 * i + 1))
                for t in range(TPG):
                    pe.wait_ge(values_kept.sem, values_kept.free(TPG * i + t))
                    for b in range(2):
                        last = nc.tensor.matmul(p_q[:, t % 2, b, 0:3 * D], zg[:, b, t * P:(t + 1) * P], w["qkv"],
                                                start=True, stop=True)
                    last.then_inc(projected.sem, 1)

            transpose(0)
            with pe.Fori(0, QUARTERS - 1) as i:
                project(i)
                transpose(i + 1)
            project(QUARTERS - 1)

        @block.scalar
        def _(act):
            act.sem_inc(copied.sem, 2)
            act.sem_inc(values_kept.sem, 2)

            def copy_x(i):
                act.wait_ge(projected.sem, projected.free(TPG * i + TPG - 1))
                for b in range(2):
                    act.wait_ge(transposed.sem, transposed.ready(2 * i + b))
                    nc.scalar.activation(zg[:, b, :], p_x[:, b, :], ACT.Copy).then_inc(copied.sem, 1)

            def keep_values(i, tiles):
                for t in tiles:
                    k = TPG * i + t
                    act.wait_ge(biased.sem, biased.ready(k))
                    nc.scalar.activation(v[:, bass.ds(k, 1), :, :].rearrange("p a m d -> p (a m) d"), p_q[:, t % 2, :, 2 * D:3 * D],
                                         ACT.Copy).then_inc(values_kept.sem, 1)

            copy_x(0)
            with act.Fori(0, QUARTERS - 1) as i:
                keep_values(i, (0, 1))
                copy_x(i + 1)
                keep_values(i, (2, 3))
            keep_values(QUARTERS - 1, range(TPG))


def pair_softmax(nc, tag, g, scores):
    with Scope(nc, tag) as s:
        most = s.sb("most", [P, BTILES * 2, HEADS])
        shifted, exps, vdone = s.sem("shifted"), s.sem("exps"), s.sem("vdone")
        block = s.block()
        by = scores[:, :, :].rearrange("p a (l m h) -> p (a l) m h", l=2, m=2)
        wide = most[:, :, :].unsqueeze(2).to_broadcast([P, BTILES * 2, 2, HEADS])

        @block.scalar
        def _(act):
            act.wait_ge(shifted, 1)
            nc.scalar.activation(scores[:, :, :], scores[:, :, :], ACT.Exp, scale=float(1 / np.float32(np.sqrt(HD))))\
                .then_inc(exps, 1)

        @block.vector
        def _(dve):
            link = Chain(dve, vdone)
            link(nc.vector.tensor_tensor(most[:, :, :], by[:, :, 0, :], by[:, :, 1, :], ALU.max))
            nc.vector.tensor_tensor(by, by, wide, ALU.subtract).then_inc(shifted, 1)
            dve.wait_ge(exps, 1)
            link(nc.vector.tensor_tensor(most[:, :, :], by[:, :, 0, :], by[:, :, 1, :], ALU.add))
            link(nc.vector.reciprocal(most[:, :, :], most[:, :, :]))
            link(nc.vector.tensor_tensor(by, by, wide, ALU.mult))


def pair_attend(nc, tag, g, scores, v, z):
    w = g.w2
    with Scope(nc, tag) as s:
        prod = s.sb("prod", [P, 2, 2, 2, D])
        o = s.sb("o", [P, TPG, 2, D])
        og = s.sb("og", [P, 2, GROUP])
        p_x = s.ps("p_x", [P, 2, GROUP])
        p_r = s.ps("p_r", [P, 2, GROUP])
        multiplied = s.counter("multiplied")
        summed = s.counter("summed", 2)
        transposed = s.counter("transposed", 1)
        copied = s.counter("copied", 2)
        projected = s.counter("projected", 2)
        added = s.counter("added", 2)
        block = s.block()

        @block.vector
        def _(dve):
            dve.sem_inc(added.sem, 2)
            dve.sem_inc(summed.sem, 2)

            def attend(i):
                dve.wait_ge(transposed.sem, transposed.free(i))
                for two in range(0, TPG, 2):
                    for h in range(2):
                        k = TPG * i + two + h
                        dve.wait_ge(summed.sem, summed.free(k))
                        nc.vector.tensor_tensor(prod[:, h, :, :, :].rearrange("p l m (h c) -> p l (m h) c", c=HD),
                                                scores[:, bass.ds(k, 1), :].rearrange("p a (l n) -> p (a l) n", l=2)
                                                .unsqueeze(3).to_broadcast([P, 2, 2 * HEADS, HD]),
                                                v[:, bass.ds(k, 1), :, :].rearrange("p a m (h c) -> p a (m h) c", c=HD)
                                                .to_broadcast([P, 2, 2 * HEADS, HD]), ALU.mult).then_inc(multiplied.sem, 1)
                    for h in range(2):
                        k = TPG * i + two + h
                        dve.wait_ge(multiplied.sem, multiplied.ready(k))
                        nc.vector.tensor_tensor(o[:, two + h, :, :], prod[:, h, :, 0, :], prod[:, h, :, 1, :], ALU.add)\
                            .then_inc(summed.sem, 1)

            def add(i):
                for b in range(2):
                    dve.wait_ge(projected.sem, projected.ready(2 * i + b))
                    nc.vector.tensor_tensor(btiles(z, b, i), p_r[:, b, :].rearrange("p (t d) -> p t d", d=D), btiles(z, b, i),
                                            ALU.add).then_inc(added.sem, 1)

            attend(0)
            with dve.Fori(1, QUARTERS) as i:
                attend(i)
                add(i - 1)
            add(QUARTERS - 1)

        @block.tensor
        def _(pe):
            pe.sem_inc(transposed.sem, 1)
            pe.sem_inc(projected.sem, 2)
            with pe.Fori(0, QUARTERS) as i:
                for b in range(2):
                    pe.wait_ge(copied.sem, copied.free(2 * i + b))
                for t in range(TPG):
                    pe.wait_ge(summed.sem, summed.ready(TPG * i + t))
                    for b in range(2):
                        last = nc.tensor.transpose(p_x[:, b, t * P:(t + 1) * P], o[:, t, b, :], g.ident)
                last.then_inc(transposed.sem, 1)
                for b in range(2):
                    pe.wait_ge(copied.sem, copied.ready(2 * i + b))
                    pe.wait_ge(added.sem, added.free(2 * i + b))
                    for t in range(TPG):
                        last = nc.tensor.matmul(p_r[:, b, t * P:(t + 1) * P], og[:, b, t * P:(t + 1) * P], w["out"],
                                                start=True, stop=True)
                    last.then_inc(projected.sem, 1)

        @block.scalar
        def _(act):
            act.sem_inc(copied.sem, 2)
            with act.Fori(0, QUARTERS) as i:
                for b in range(2):
                    act.wait_ge(transposed.sem, transposed.ready(i))
                    act.wait_ge(projected.sem, projected.free(2 * i + b))
                    nc.scalar.activation(og[:, b, :], p_x[:, b, :], ACT.Copy).then_inc(copied.sem, 1)


def top1_logits(nc, tag, g, z, mean, rstd, yt, logits):
    w = g.w2
    with Scope(nc, tag) as s:
        ys = s.sb("ys", [P, 2, TPG, D])
        yg = s.sb("yg", [P, 2, GROUP])
        p_x = s.ps("p_x", [P, 2, GROUP])
        p_l = s.ps("p_l", [P, 2, GROUP])
        centred = s.counter("centred")
        scaled = s.counter("scaled")
        normalized = s.counter("normalized")
        kept = s.counter("kept", 2)
        yt_kept = s.counter("yt_kept", 2)
        transposed = s.counter("transposed", 2)
        copied = s.counter("copied", 2)
        routed = s.counter("routed", 2)
        logits_kept = s.counter("logits_kept", 2)
        block = s.block()
        wide = lambda r: r.unsqueeze(1).to_broadcast([P, TPG, D])

        @block.vector
        def _(dve):
            dve.sem_inc(logits_kept.sem, 2)

            def normalize(i, b):
                u = 2 * i + b
                dve.wait_ge(transposed.sem, transposed.free(u))
                dve.wait_ge(kept.sem, kept.free(u))
                for t in range(TPG):
                    last = nc.vector.tensor_scalar(ys[:, b, t:t + 1, :], btiles(z, b, i, t, 1), bcol(mean, b, i, t),
                                                   bcol(rstd, b, i, t), ALU.subtract, ALU.mult)
                last.then_inc(centred.sem, 1)
                dve.wait_ge(centred.sem, centred.ready(u))
                nc.vector.tensor_tensor(ys[:, b, :, :], ys[:, b, :, :], wide(w["ln1_g"]), ALU.mult).then_inc(scaled.sem, 1)
                dve.wait_ge(scaled.sem, scaled.ready(u))
                nc.vector.tensor_tensor(ys[:, b, :, :], ys[:, b, :, :], wide(w["ln1_b"]), ALU.add).then_inc(normalized.sem, 1)

            def keep(i, b):
                u = 2 * i + b
                dve.wait_ge(routed.sem, routed.ready(u))
                nc.vector.tensor_copy(btiles(logits, b, i), p_l[:, b, 0:TPG * E].rearrange("p (t e) -> p t e", e=E))\
                    .then_inc(logits_kept.sem, 1)

            in_pairs(dve, normalize, keep)

        @block.gpsimd
        def _(pool):
            pool.sem_inc(kept.sem, 2)
            pool.sem_inc(yt_kept.sem, 2)
            with pool.Fori(0, QUARTERS) as i:
                for b in range(2):
                    pool.wait_ge(normalized.sem, normalized.ready(2 * i + b))
                    nc.gpsimd.tensor_copy(btiles(z, b, i), ys[:, b, :, :]).then_inc(kept.sem, 1)
                for b in range(2):
                    pool.wait_ge(copied.sem, copied.ready(2 * i + b))
                    nc.gpsimd.tensor_copy(yt[:, bass.ds(GROUP * i + SEQ * b, GROUP)], yg[:, b, :]).then_inc(yt_kept.sem, 1)

        @block.tensor
        def _(pe):
            pe.sem_inc(transposed.sem, 2)
            pe.sem_inc(routed.sem, 2)

            def transpose(i, b):
                pe.wait_ge(normalized.sem, normalized.ready(2 * i + b))
                pe.wait_ge(copied.sem, copied.free(2 * i + b))
                for t in range(TPG):
                    last = nc.tensor.transpose(p_x[:, b, t * P:(t + 1) * P], ys[:, b, t, :], g.ident)
                last.then_inc(transposed.sem, 1)

            def route(i, b):
                pe.wait_ge(copied.sem, copied.ready(2 * i + b))
                pe.wait_ge(logits_kept.sem, logits_kept.free(2 * i + b))
                for t in range(TPG):
                    last = nc.tensor.matmul(p_l[:, b, t * E:(t + 1) * E], yg[:, b, t * P:(t + 1) * P], w["wg"],
                                            start=True, stop=True)
                last.then_inc(routed.sem, 1)

            in_pairs(pe, transpose, route)

        @block.scalar
        def _(act):
            act.sem_inc(copied.sem, 2)
            with act.Fori(0, QUARTERS) as i:
                for b in range(2):
                    act.wait_ge(transposed.sem, transposed.ready(2 * i + b))
                    act.wait_ge(routed.sem, routed.free(2 * i + b))
                    act.wait_ge(yt_kept.sem, yt_kept.free(2 * i + b))
                    nc.scalar.activation(yg[:, b, :], p_x[:, b, :], ACT.Copy).then_inc(copied.sem, 1)


def route_top1(nc, tag, g, logits, wt, wtt):
    with Scope(nc, tag) as s:
        probs = s.sb("probs", [P, TILES, E])
        top = s.sb("top", [P, TILES])
        code = s.sb("code", [P, TILES, E])
        best = s.sb("best", [P, TILES])
        hot = s.sb("hot", [P, TILES, E])
        mask = s.sb("mask", [P, E, TILES], BF16)
        before = s.sb("before", [P, E, TILES])
        p_c = s.ps("p_c", [P, 2, GROUP])
        p_t = s.ps("p_t", [P, GROUPS, P])
        vdone, masked, counted, weighted, transposed = (
            s.sem(n) for n in ("vdone", "masked", "counted", "weighted", "transposed"))
        soft_v, soft_a = probabilities(nc, tag, s, logits, probs, top[:, :])
        block = s.block()
        N = E * TILES
        view = lambda ap: ap.rearrange("p (e t) -> p e t", e=E)

        @block.scalar
        def _(act):
            soft_a(act)

        @block.tensor
        def _(pe):
            pe.wait_ge(masked, 1)
            flat = mask[:, :, :].rearrange("p e t -> p (e t)")
            nc.tensor.matmul(p_c[:, 0, 0:N], g.upto[:, :], flat, start=True, stop=True)
            nc.tensor.matmul(p_c[:, 1, 0:N], g.ones[:, :], flat, start=True, stop=True).then_inc(counted, 1)
            pe.wait_ge(weighted, 1)
            for q in range(GROUPS):
                last = nc.tensor.transpose(p_t[:, q, :], wt[:, q * TPG:(q + 1) * TPG, :].rearrange("p t e -> p (t e)"), g.ident)
            last.then_inc(transposed, 1)

        @block.vector
        def _(dve):
            link = Chain(dve, vdone)
            soft_v(link)
            first_largest(nc, link, probs[:, :, :], top[:, :], g.rank, code, best, hot[:, :, :])
            link(nc.vector.memset(wt[:, :, :], 0.0))
            nc.vector.tensor_copy(mask[:, :, :].rearrange("p e t -> p t e"), hot[:, :, :]).then_inc(masked, 1)
            dve.wait_ge(counted, 1)
            link(nc.vector.tensor_tensor_scan(before[:, :, :].rearrange("p e t -> p (e t)"), g.carry[:, :], p_c[:, 1, 0:N],
                                              0.0, ALU.mult, ALU.add))
            link(nc.vector.tensor_tensor(before[:, :, :], before[:, :, :], view(p_c[:, 1, 0:N]), ALU.subtract))
            link(nc.vector.tensor_tensor(before[:, :, :], view(p_c[:, 0, 0:N]), before[:, :, :], ALU.add))
            link(nc.vector.tensor_scalar(before[:, :, :], before[:, :, :], float(CAP1), None, ALU.is_le))
            link(nc.vector.tensor_tensor(hot[:, :, :], hot[:, :, :], before[:, :, :].rearrange("p e t -> p t e"), ALU.mult))
            nc.vector.tensor_tensor(wt[:, :, 0:E], hot[:, :, :], over(top[:, :], E), ALU.mult).then_inc(weighted, 1)
            dve.wait_ge(transposed, 1)
            nc.vector.tensor_copy(wtt[:, :, :], p_t[:, :, :])


def experts_top1(nc, tag, g, yt, wt, wtt, z):
    H = E // 2
    with Scope(nc, tag) as s:
        yg = s.sb("yg", [P, 2, GROUP])
        wg = s.sb("wg", [P, 2, P])
        gates = s.sb("gates", [P, 2, TPG, E])
        terms = s.sb("terms", [P, 2, TPG, E, D])
        base = s.sb("base", [P, 2, TPG, D])
        p_b = s.ps("p_b", [P, 2, GROUP])
        p_e = s.ps("p_e", [P, 2, E, D])
        gates_in = s.counter("gates_in")
        copied = s.counter("copied")
        biases = s.counter("biases")
        products = s.counter("products", TPG)
        started = s.counter("started", 2)
        low_scaled = s.counter("low_scaled", 2)
        high_scaled = s.counter("high_scaled", 2)
        sums = s.counter("sums")
        high_sums = s.counter("high_sums")
        summed = s.counter("summed", 1)
        block = s.block()

        def in_turns(eng, turn):
            turn(0, at_first=True)
            with eng.Fori(1, QUARTERS - 1) as i:
                turn(i)
            turn(QUARTERS - 1, at_last=True)

        @block.gpsimd
        def _(pool):
            def take_gates(i, b):
                nc.gpsimd.tensor_copy(gates[:, b, :, :], wt[:, bass.ds(TPG * i + BTILES * b, TPG), 0:E]).then_inc(gates_in.sem, 1)

            def turn(i, at_first=False, at_last=False):
                for b in range(2):
                    u = 2 * i + b
                    upper = terms[:, b, :, H:E, :]
                    pool.wait_ge(high_scaled.sem, high_scaled.ready(TPG * u + TPG - 1))
                    nc.gpsimd.tensor_tensor(upper[:, :, 0:2, :], upper[:, :, 0:2, :], upper[:, :, 2:4, :], ALU.add)\
                        .then_inc(high_sums.sem, 1)
                    pool.wait_ge(high_sums.sem, high_sums.ready(2 * u))
                    nc.gpsimd.tensor_tensor(upper[:, :, 0, :], upper[:, :, 0, :], upper[:, :, 1, :], ALU.add)\
                        .then_inc(high_sums.sem, 1)
                    if not at_last:
                        pool.wait_ge(low_scaled.sem, low_scaled.ready(TPG * u + TPG - 1))
                        take_gates(i + 1, b)

            take_gates(0, 0)
            take_gates(0, 1)
            in_turns(pool, turn)

        @block.scalar
        def _(act):
            act.sem_inc(high_scaled.sem, 2)

            def copies(i, b):
                act.wait_ge(products.sem, products.ready(TPG * (2 * i + b) - 1) - TPG)
                nc.scalar.activation(wg[:, b, :], wtt[:, bass.ds(i + QUARTERS * b, 1), :].rearrange("p a n -> p (a n)"), ACT.Copy)
                nc.scalar.activation(yg[:, b, :], yt[:, bass.ds(GROUP * i + SEQ * b, GROUP)], ACT.Copy)\
                    .then_inc(copied.sem, 1)

            def turn(i, at_first=False, at_last=False):
                for b in range(2):
                    u = 2 * i + b
                    if b == 0:
                        copies(i, 1)
                    elif not at_last:
                        copies(i + 1, 0)
                    act.wait_ge(gates_in.sem, gates_in.ready(u))
                    if not (at_first and b < 1):
                        act.wait_ge(summed.sem, summed.free(u, 2))
                    for t in range(TPG):
                        act.wait_ge(products.sem, products.ready(TPG * u + t))
                        for e in range(H, E):
                            last = nc.scalar.activation(terms[:, b, t, e, :], p_e[:, t % 2, e, :], ACT.Identity,
                                                        scale=gates[:, b, t, e:e + 1])
                        last.then_inc(high_scaled.sem, 1)

            copies(0, 0)
            in_turns(act, turn)

        @block.tensor
        def _(pe):
            pe.sem_inc(products.sem, TPG)
            with pe.Fori(0, QUARTERS) as i:
                for b in range(2):
                    u = 2 * i + b
                    pe.wait_ge(copied.sem, copied.ready(u))
                    pe.wait_ge(started.sem, started.free(u))
                    nc.tensor.matmul(p_b[:, b, :], wg[:, b, :], g.b12[:, :, :].rearrange("p t d -> p (t d)"),
                                     start=True, stop=True).then_inc(biases.sem, 1)
                    for t in range(TPG):
                        k = TPG * u + t
                        for half, taken in enumerate((low_scaled, high_scaled)):
                            pe.wait_ge(taken.sem, taken.free(k))
                            last = nc.tensor.matmul(p_e[:, t % 2, half * H:(half + 1) * H, :].rearrange("p e d -> p (e d)"),
                                                    yg[:, b, t * P:(t + 1) * P],
                                                    g.w12[:, half * H:(half + 1) * H, :].rearrange("p e d -> p (e d)"),
                                                    start=True, stop=True)
                        last.then_inc(products.sem, 1)

        @block.vector
        def _(dve):
            dve.sem_inc(started.sem, 2)
            dve.sem_inc(low_scaled.sem, 2)
            dve.sem_inc(summed.sem, 1)

            def lower(i, b, at_first=False):
                u = 2 * i + b
                if not at_first:
                    dve.wait_ge(summed.sem, summed.free(u, 2))
                dve.wait_ge(biases.sem, biases.ready(u))
                nc.vector.tensor_tensor(base[:, b, :, :], p_b[:, b, :].rearrange("p (t d) -> p t d", d=D), btiles(z, b, i),
                                        ALU.add).then_inc(started.sem, 1)
                dve.wait_ge(gates_in.sem, gates_in.ready(u))
                for t in range(TPG):
                    k = TPG * u + t
                    dve.wait_ge(products.sem, products.ready(k))
                    nc.vector.tensor_tensor(terms[:, b, t, 0:H, :], p_e[:, t % 2, 0:H, :], over(gates[:, b, t, 0:H], D), ALU.mult)\
                        .then_inc(low_scaled.sem, 1)
                dve.wait_ge(low_scaled.sem, low_scaled.ready(TPG * u + TPG - 1))
                nc.vector.tensor_tensor(terms[:, b, :, 0:2, :], terms[:, b, :, 0:2, :], terms[:, b, :, 2:4, :], ALU.add)\
                    .then_inc(sums.sem, 1)
                dve.wait_ge(started.sem, started.ready(u))
                for e in range(2):
                    dve.wait_ge(sums.sem, sums.ready(3 * u + e))
                    nc.vector.tensor_tensor(base[:, b, :, :], base[:, b, :, :], terms[:, b, :, e, :], ALU.add).then_inc(sums.sem, 1)

            def add_upper(i, b):
                u = 2 * i + b
                dve.wait_ge(sums.sem, sums.ready(3 * u + 2))
                dve.wait_ge(high_sums.sem, high_sums.ready(2 * u + 1))
                nc.vector.tensor_tensor(btiles(z, b, i), base[:, b, :, :], terms[:, b, :, H, :], ALU.add).then_inc(summed.sem, 1)

            def turn(i, at_first=False, at_last=False):
                lower(i, 0, at_first)
                if not at_first:
                    add_upper(i - 1, 1)
                lower(i, 1, at_first)
                add_upper(i, 0)

            in_turns(dve, turn)
            add_upper(QUARTERS - 1, 1)


def add_normed(nc, tag, g, z, mean, rstd, x):
    w = g.w2
    PART = 8
    with Scope(nc, tag) as s:
        vdone, centred = s.sem("vdone"), s.sem("centred")
        block = s.block()
        wide = lambda r: r.unsqueeze(1).to_broadcast([P, PART, D])

        @block.vector
        def _(dve):
            for t in range(TILES):
                last = nc.vector.tensor_scalar(z[:, t, :], z[:, t, :], mean[:, t:t + 1], rstd[:, t:t + 1], ALU.subtract, ALU.mult)
            last.then_inc(centred, 1)
            dve.wait_ge(centred, 1)
            link = Chain(dve, vdone)
            for q in range(TILES // PART):
                part = z[:, q * PART:(q + 1) * PART, :]
                xp = x[:, q * PART:(q + 1) * PART, :]
                link(nc.vector.tensor_tensor(part, part, wide(w["ln2_g"]), ALU.mult))
                link(nc.vector.tensor_tensor(part, part, wide(w["ln2_b"]), ALU.add))
                link(nc.vector.scalar_tensor_tensor(xp, part, 0.5, xp, ALU.mult, ALU.add))



IH, ID = 4, 64
TOPK = 32
TIE = 2.0 ** -120
NONE = -3.0e38
MASKED = -1.0e30
HALF = SEQ // 2
SCALE = float(1 / np.sqrt(np.float32(D)))


def sparse_attention(nc, tag, g, x):
    with Scope(nc, tag) as s:
        mean, rstd = s.sb("mean", [P, TILES]), s.sb("rstd", [P, TILES])
        row_stats(nc, tag + "s", g.stats, mean, [(rstd, LN_EPS, True)], x)
        qt, kt = s.sb("qt", [P, SEQ]), s.sb("kt", [P, SEQ])
        v = s.sb("v", [P, BTILES, D])
        iqt = s.sb("iqt", [P, IH, SEQ])
        ikt = s.sb("ikt", [P, 2, SEQ], F32R)
        iw = s.sb("iw", [P, BTILES, IH])
        g.tiebreak = s.sb("tiebreak", [P, SEQ])
        make_tiebreak(nc, tag + "t", g, g.tiebreak)
        for b in range(2):
            attention_project(nc, f"{tag}p{b}", g, b, x, mean, rstd, qt, kt, v, iqt, ikt, iw)
            attention_select(nc, f"{tag}a{b}", g, b, x, qt, kt, v, iqt, ikt, iw)


def make_tiebreak(nc, tag, g, tiebreak):
    with Scope(nc, tag) as s:
        made = s.sem("made")
        block = s.block()

        @block.sync
        def _(sp):
            sp.wait_ge(g.pack_in[3], 16)

        @block.gpsimd
        def _(pool):
            link = Chain(pool, made)
            link(nc.gpsimd.iota(tiebreak[:, :], pattern=[[1, SEQ]], base=1, channel_multiplier=0,
                                allow_small_or_imprecise_dtypes=True))
            link(nc.gpsimd.tensor_scalar(tiebreak[:, :], tiebreak[:, :], -TIE, None, ALU.mult))


def attention_project(nc, tag, g, b, x, mean, rstd, qt, kt, v, iqt, ikt, iw):
    w = g.w3
    with Scope(nc, tag) as s:
        cos, sin = s.sb("cos", [P, SEQ]), s.sb("sin", [P, SEQ])
        zs = s.sb("zs", [P, 2, TPG, D])
        zg = s.sb("zg", [P, 2, GROUP])
        rot = s.sb("rot", [P, 2, 2, GROUP])
        p_x = s.ps("p_x", [P, GROUP])
        p_qk = s.ps("p_qk", [P, 4, GROUP])
        p_i = s.ps("p_i", [P, GROUP])
        p_v = s.ps("p_v", [P, GROUP])
        p_w = s.ps("p_w", [P, TPG * IH])
        tables = s.sem("tables")
        normalized = s.counter("normalized")
        transposed = s.counter("transposed", 2)
        copied = s.counter("copied", 1)
        turned = s.counter("turned")
        rotated = s.counter("rotated", 4)
        summed = s.counter("summed", 2)
        indexed = s.counter("indexed")
        index_kept = s.counter("index_kept", 1)
        low_kept = s.counter("low_kept", 1)
        valued = s.counter("valued")
        value_kept = s.counter("value_kept", 1)
        weighed = s.counter("weighed", 2)
        weight_kept = s.counter("weight_kept", 1)
        block = s.block()
        NI = IH + 1

        @block.sync
        def _(sp):
            sp.dma_start(cos[:, :], g.cos).then_inc(tables, 16)
            sp.dma_start(sin[:, :], g.sin).then_inc(tables, 16)

        @block.vector
        def _(dve):
            dve.sem_inc(rotated.sem, 4)
            dve.sem_inc(summed.sem, 2)
            dve.sem_inc(value_kept.sem, 1)
            dve.sem_inc(weight_kept.sem, 1)
            dve.sem_inc(low_kept.sem, 1)
            with dve.Fori(0, QUARTERS // 2) as i:
                for h in range(2):
                    u = 2 * i + h
                    dve.wait_ge(transposed.sem, transposed.free(u))
                    for t in range(TPG):
                        last = nc.vector.tensor_scalar(zs[:, h, t:t + 1, :], btiles(x, b, u, t, 1), bcol(mean, b, u, t),
                                                       bcol(rstd, b, u, t), ALU.subtract, ALU.mult)
                    last.then_inc(normalized.sem, 1)
                for h in range(2):
                    u = 2 * i + h
                    if h == 0:
                        dve.wait_ge(tables, 32)
                    for m, out in enumerate((qt, kt)):
                        dve.wait_ge(summed.sem, summed.free(2 * u + m))
                        for part, table in enumerate((cos, sin)):
                            n = 2 * m + part
                            dve.wait_ge(turned.sem, turned.ready(4 * u + n))
                            nc.vector.scalar_tensor_tensor(rot[:, m, part, :], p_qk[:, n, :], w["qk_b"][:, n:n + 1],
                                                           table[:, bass.ds(GROUP * u, GROUP)], ALU.add, ALU.mult)\
                                .then_inc(rotated.sem, 1)
                        dve.wait_ge(rotated.sem, rotated.ready(4 * u + 2 * m + 1))
                        nc.vector.tensor_tensor(out[:, bass.ds(GROUP * u, GROUP)], rot[:, m, 0, :], rot[:, m, 1, :],
                                                ALU.add).then_inc(summed.sem, 1)
                    high = ikt[:, 0, bass.ds(GROUP * u, GROUP)]
                    dve.wait_ge(index_kept.sem, index_kept.ready(NI * u + IH))
                    nc.vector.scalar_tensor_tensor(ikt[:, 1, bass.ds(GROUP * u, GROUP)], p_i[:, :], w["iqk_b"][:, IH:IH + 1],
                                                   high.bitcast(F32), ALU.add, ALU.subtract).then_inc(low_kept.sem, 1)
                    dve.wait_ge(valued.sem, valued.ready(u))
                    nc.vector.tensor_tensor(v[:, bass.ds(TPG * u, TPG), :], p_v[:, :].rearrange("p (t d) -> p t d", d=D),
                                            w["v_b"].unsqueeze(1).to_broadcast([P, TPG, D]), ALU.add).then_inc(value_kept.sem, 1)
                    dve.wait_ge(weighed.sem, weighed.ready(u))
                    nc.vector.tensor_tensor(iw[:, bass.ds(TPG * u, TPG), :], p_w[:, :].rearrange("p (t h) -> p t h", h=IH),
                                            w["iw_b"].unsqueeze(1).to_broadcast([P, TPG, IH]), ALU.add).then_inc(weight_kept.sem, 1)

        @block.gpsimd
        def _(pool):
            with pool.Fori(0, QUARTERS) as u:
                pool.wait_ge(normalized.sem, normalized.ready(u))
                nc.gpsimd.tensor_tensor(btiles(x, b, u), btiles(x, b, u), w["o_b"].unsqueeze(1).to_broadcast([P, TPG, D]), ALU.add)

        @block.tensor
        def _(pe):
            pe.sem_inc(transposed.sem, 2)
            pe.sem_inc(weighed.sem, 2)
            with pe.Fori(0, QUARTERS // 2) as i:
                for h in range(2):
                    u = 2 * i + h
                    pe.wait_ge(normalized.sem, normalized.ready(u))
                    pe.wait_ge(copied.sem, copied.free(u))
                    for t in range(TPG):
                        last = nc.tensor.transpose(p_x[:, t * P:(t + 1) * P], zs[:, h, t, :], g.ident)
                    last.then_inc(transposed.sem, 1)
                    pe.wait_ge(copied.sem, copied.ready(u))
                    for n in range(NI):
                        if n < 4:
                            pe.wait_ge(rotated.sem, rotated.free(4 * u + n))
                            nc.tensor.matmul(p_qk[:, n, :], w["qk"][:, n * D:(n + 1) * D], zg[:, h, :], start=True, stop=True)\
                                .then_inc(turned.sem, 1)
                        pe.wait_ge(index_kept.sem, index_kept.free(NI * u + n))
                        if n == 0:
                            pe.wait_ge(low_kept.sem, low_kept.free(u))
                        nc.tensor.matmul(p_i[:, :], w["iqk"][:, n * P:(n + 1) * P], zg[:, h, :], start=True, stop=True)\
                            .then_inc(indexed.sem, 1)
                    pe.wait_ge(value_kept.sem, value_kept.free(u))
                    for t in range(TPG):
                        last = nc.tensor.matmul(p_v[:, t * D:(t + 1) * D], zg[:, h, t * P:(t + 1) * P], w["v"], start=True, stop=True)
                    last.then_inc(valued.sem, 1)
                    pe.wait_ge(weight_kept.sem, weight_kept.free(u))
                    for t in range(TPG):
                        last = nc.tensor.matmul(p_w[:, t * IH:(t + 1) * IH], zg[:, h, t * P:(t + 1) * P], w["iw"], start=True, stop=True)
                    last.then_inc(weighed.sem, 1)

        @block.scalar
        def _(act):
            act.sem_inc(copied.sem, 1)
            act.sem_inc(index_kept.sem, 1)
            with act.Fori(0, QUARTERS // 2) as i:
                for h in range(2):
                    u = 2 * i + h
                    act.wait_ge(transposed.sem, transposed.ready(u))
                    act.wait_ge(weighed.sem, weighed.free(u))
                    nc.scalar.activation(zg[:, h, :], p_x[:, :], ACT.Copy).then_inc(copied.sem, 1)
                    for n in range(NI):
                        part = bass.ds(GROUP * u, GROUP)
                        out = ikt[:, 0, part] if n == IH else iqt[:, n, part]
                        act.wait_ge(indexed.sem, indexed.ready(NI * u + n))
                        nc.scalar.activation(out, p_i[:, :], ACT.Identity, bias=w["iqk_b"][:, n:n + 1]).then_inc(index_kept.sem, 1)


def attention_select(nc, tag, g, b, x, qt, kt, v, iqt, ikt, iw):
    w = g.w3
    UNITS = 2 * IH
    RING = UNITS
    EARLY = 4
    SPAN = 64
    SPANS = SEQ // SPAN
    ROUNDS = TOPK // 8
    N = BTILES
    with Scope(nc, tag) as s:
        iqs = s.sb("iqs", [P, IH, P], F32R)
        qs = s.sb("qs", [P, P])
        relu = s.sb("relu", [P, RING, HALF])
        score = s.sb("score", [P, SEQ])
        tiebreak = g.tiebreak
        cand = s.sb("cand", [P, SPANS, 8])
        best = s.sb("best", [P, 8])
        after = s.sb("after", [P, 8])
        prob = s.sb("prob", [P, SEQ])
        probt = s.sb("probt", [P, SEQ])
        half_most, most, bias, total, inv, eighth, unsure = (
            s.sb(n, [P, 1]) for n in ("half_most", "most", "bias", "total", "inv", "eighth", "unsure"))
        unsure_row = s.sb("unsure_row", [1, P])
        again = s.sb("again", [1, 1], U32)
        ot = s.sb("ot", [P, P])
        p_s = s.ps("p_s", [P, 2, HALF])
        p_l = s.ps("p_l", [P, SEQ])
        rounded = s.counter("rounded")
        index_queries = s.counter("index_queries")
        queries = s.counter("queries")
        scored = s.counter("scored")
        logits = s.counter("logits", 1)
        rectified = s.counter("rectified", 2)
        added = s.counter("added", RING)
        vdone = s.sem("vdone")
        row_max = s.counter("row_max")
        flagged = s.counter("flagged")
        flags_in = s.sem("flags_in")
        masked = s.counter("masked")
        exped = s.counter("exped")
        prob_t = s.counter("prob_t")
        prob_t_kept = s.counter("prob_t_kept")
        attended = s.counter("attended", 1)
        inverted = s.counter("inverted")
        o_kept = s.counter("o_kept")
        projected = s.counter("projected")
        finished = s.counter("finished", 1)
        block = s.block()

        def in_turn(eng, first, second):
            first(0, None)
            with eng.Fori(1, N) as n:
                first(n, second)
            second(N - 1)

        @block.gpsimd
        def _(pool):
            def index_part(n):
                nc.gpsimd.tensor_copy(iqs[:, :, :], iqt[:, :, bass.ds(P * n, P)]).then_inc(rounded.sem, 1)
                pool.wait_ge(rounded.sem, rounded.ready(n))
                low = iqs[ID:P, :, :]
                nc.gpsimd.tensor_tensor(low, iqt[ID:P, :, bass.ds(P * n, P)], low.bitcast(F32), ALU.subtract)\
                    .then_inc(index_queries.sem, 1)
                pool.wait_ge(index_queries.sem, index_queries.ready(n))

            def query_part(n):
                pool.wait_ge(logits.sem, logits.free(n))
                nc.gpsimd.tensor_copy(qs[:, :], qt[:, bass.ds(P * n, P)]).then_inc(queries.sem, 1)

            index_part(0)
            query_part(0)
            with pool.Fori(1, N) as n:
                pool.wait_ge(scored.sem, scored.ready(UNITS * n - 1))
                index_part(n)
                query_part(n)

        @block.sync
        def _(sp):
            with sp.Fori(0, N) as n:
                sp.wait_ge(flagged.sem, flagged.ready(n))
                sp.dma_start(unsure_row[:, :], unsure[:, :]).then_inc(flags_in, 16)

        @block.tensor
        def _(pe):
            pe.sem_inc(logits.sem, 1)
            pe.sem_inc(attended.sem, 1)

            def select(n, then):
                pe.wait_ge(index_queries.sem, index_queries.ready(n))
                for k in range(UNITS):
                    h, half = divmod(k, 2)
                    pe.wait_ge(rectified.sem, rectified.free(UNITS * n + k))
                    for part in range(2):
                        for c in range(HALF // GROUP):
                            at = half * HALF + c * GROUP
                            last = nc.tensor.matmul(p_s[:, k % 2, c * GROUP:(c + 1) * GROUP], iqs[:, h, :],
                                                    ikt[:, part, at:at + GROUP], start=(part == 0), stop=(part == 1))
                    last.then_inc(scored.sem, 1)
                if then is not None:
                    then(n - 1)
                pe.wait_ge(queries.sem, queries.ready(n))
                pe.wait_ge(finished.sem, finished.free(n))
                for c in range(SEQ // GROUP):
                    last = nc.tensor.matmul(p_l[:, c * GROUP:(c + 1) * GROUP], qs[:, :], kt[:, c * GROUP:(c + 1) * GROUP],
                                            start=True, stop=True)
                last.then_inc(logits.sem, 1)

            def attend(n):
                pe.wait_ge(exped.sem, exped.ready(n))
                for half in range(2):
                    for k in range(half * N // 2, (half + 1) * N // 2):
                        last = nc.tensor.transpose(p_l[:, k * P:(k + 1) * P], prob[:, k * P:(k + 1) * P], g.ident)
                    last.then_inc(prob_t.sem, 1)
                pe.wait_ge(prob_t_kept.sem, prob_t_kept.ready(2 * n + 1))
                for k in range(N):
                    last = nc.tensor.matmul(p_l[:, 0:P], v[:, k, :], probt[:, k * P:(k + 1) * P],
                                            start=(k == 0), stop=(k == N - 1))
                last.then_inc(attended.sem, 1)
                pe.wait_ge(o_kept.sem, o_kept.ready(n))
                nc.tensor.matmul(p_l[:, GROUP:GROUP + D], ot[:, :], w["o"], start=True, stop=True).then_inc(projected.sem, 1)

            in_turn(pe, select, attend)

        @block.scalar
        def _(act):
            act.sem_inc(rectified.sem, 2)

            def rectify(n, units):
                for k in units:
                    unit = UNITS * n + k
                    act.wait_ge(scored.sem, scored.ready(unit))
                    act.wait_ge(added.sem, added.free(unit))
                    nc.scalar.activation(relu[:, k % RING, :], p_s[:, k % 2, :], ACT.Relu).then_inc(rectified.sem, 1)

            def exponentials(n):
                act.wait_ge(masked.sem, masked.ready(n))
                nc.scalar.activation(prob[:, :], prob[:, :], ACT.Exp, bias=bias[:, :], accum_out=total[:, :]).then_inc(exped.sem, 1)

            def copies(n):
                act.wait_ge(attended.sem, attended.free(n))
                for half in range(2):
                    act.wait_ge(prob_t.sem, prob_t.ready(2 * n + half))
                    part = slice(half * HALF, (half + 1) * HALF)
                    nc.scalar.activation(probt[:, part], p_l[:, part], ACT.Copy).then_inc(prob_t_kept.sem, 1)
                act.wait_ge(attended.sem, attended.ready(n))
                nc.scalar.activation(ot[:, :], p_l[:, 0:P], ACT.Copy).then_inc(o_kept.sem, 1)

            def select(n, then):
                rectify(n, range(EARLY))
                if then is not None:
                    exponentials(n - 1)
                rectify(n, range(EARLY, UNITS))
                if then is not None:
                    copies(n - 1)

            def attend(n):
                exponentials(n)
                copies(n)

            in_turn(act, select, attend)

        @block.vector
        def _(dve):
            dve.sem_inc(added.sem, RING)
            dve.sem_inc(finished.sem, 1)

            def select(n, then):
                steps = [0]

                def link(ins):
                    steps[0] += 1
                    ins.then_inc(vdone, 1)
                    dve.wait_ge(vdone, steps[0])

                def restart():
                    dve.sem_clear(vdone)
                    steps[0] = 0

                def wanted(h):
                    return iw[:, bass.ds(n, 1), h]

                for k in range(UNITS):
                    h, half = divmod(k, 2)
                    part = score[:, half * HALF:(half + 1) * HALF]
                    unit = UNITS * n + k
                    dve.wait_ge(rectified.sem, rectified.ready(unit))
                    if h == 0:
                        nc.vector.scalar_tensor_tensor(part, relu[:, k % RING, :], wanted(0), tiebreak[:, half * HALF:(half + 1) * HALF],
                                                       ALU.mult, ALU.add).then_inc(added.sem, 1)
                    else:
                        dve.wait_ge(added.sem, added.ready(unit - 2))
                        nc.vector.scalar_tensor_tensor(part, relu[:, k % RING, :], wanted(h), part, ALU.mult, ALU.add)\
                            .then_inc(added.sem, 1)
                dve.wait_ge(added.sem, added.ready(UNITS * n + UNITS - 1))
                dve.sem_inc(vdone, 1)
                restart()
                for k in range(SPANS):
                    last = nc.vector.max(cand[:, k, :], score[:, :].rearrange("p (j k) -> p k j", k=SPANS)[:, k, :])
                link(last)
                if then is not None:
                    then(n - 1)
                link(nc.vector.tensor_reduce(eighth[:, :], cand[:, :, 7], AX, ALU.max))
                every = cand[:, :, :].rearrange("p g k -> p (g k)")
                for r in range(ROUNDS):
                    link(nc.vector.max(best[:, :], every))
                    link(nc.vector.match_replace(every, best[:, :], every, NONE))
                link(nc.vector.max(after[:, :], every))
                nc.vector.scalar_tensor_tensor(unsure[:, :], after[:, 0:1], eighth[:, :], best[:, 7:8], ALU.max, ALU.is_ge)\
                    .then_inc(flagged.sem, 1)
                if then is not None:
                    dve.wait_ge(prob_t.sem, prob_t.ready(2 * n - 1))
                nc.vector.tensor_scalar(prob[:, :], score[:, :], best[:, 7:8], MASKED, ALU.is_lt, ALU.mult).then_inc(vdone, 1)
                dve.wait_ge(logits.sem, logits.ready(n))
                dve.sem_inc(vdone, 1)
                steps[0] += 2
                dve.wait_ge(vdone, steps[0])
                link(masked_logits(0, NONE))
                dve.wait_ge(flags_in, 16 * n + 16)
                nc.vector.tensor_reduce(again[:, :], unsure_row[:, :], AX, ALU.max).then_inc(vdone, 1)
                masked_logits(1, half_most[:, :]).then_inc(row_max.sem, 1)
                steps[0] += 1
                dve.wait_ge(vdone, steps[0])
                restart()
                with dve.If(dve.value_load(again[0:1, 0:1], min_val=0, max_val=1) != 0):
                    dve.wait_ge(row_max.sem, row_max.ready(n))
                    dve.sem_inc(vdone, 1)
                    restart()
                    for r in range(ROUNDS):
                        link(nc.vector.max(best[:, :], score[:, :]))
                        link(nc.vector.match_replace(score[:, :], best[:, :], score[:, :], NONE))
                    link(nc.vector.tensor_scalar(prob[:, :], score[:, :], NONE / 2, MASKED, ALU.is_gt, ALU.mult))
                    link(masked_logits(0, NONE))
                    link(masked_logits(1, half_most[:, :]))
                    restart()
                dve.wait_ge(row_max.sem, row_max.ready(n))
                nc.vector.tensor_scalar(bias[:, :], most[:, :], -1.0, None, ALU.mult).then_inc(masked.sem, 1)

            def masked_logits(half, most_before):
                part = slice(half * HALF, (half + 1) * HALF)
                return nc.vector.tensor_tensor_reduce(out=prob[:, part], in0=prob[:, part], in1=p_l[:, part], scale=SCALE,
                                                      scalar=most_before, op0=ALU.add, op1=ALU.max,
                                                      accum_out=(most if half else half_most)[:, :])

            def finish_rows(n):
                dve.wait_ge(exped.sem, exped.ready(n))
                nc.vector.reciprocal(inv[:, :], total[:, :]).then_inc(inverted.sem, 1)
                dve.wait_ge(inverted.sem, inverted.ready(n))
                dve.wait_ge(projected.sem, projected.ready(n))
                rows = x[:, bass.ds(n + N * b, 1), :].rearrange("p a d -> p (a d)")
                nc.vector.scalar_tensor_tensor(rows, p_l[:, GROUP:GROUP + D], inv[:, :], rows, ALU.mult, ALU.add)\
                    .then_inc(finished.sem, 1)

            in_turn(dve, select, finish_rows)



PACK0 = dict(wr=E, fw1=FF, fw2=FC * D, fb1=FC, fb2=1)
PACK1 = dict(in_ga=P, in_va=P, in_gr=2 * P, in_vr=2 * P, grow=FF, shrink=2 * P,
             f_aa=P, f_ra=2 * P, f_ar=2 * P, f_rr=P, i_aa=P, i_ra=2 * P, i_ar=2 * P, i_rr=P,
             out_a=P, out_r=2 * P, gamma1=1, gamma2=1, conv_w=8, conv_b=2, b_gates=4, forget_base=2)
PACK2 = dict(qkv=3 * D, out=D, wg=E, b1=E * FC, b2=E, qkv_b=3 * D, out_b=D, ln1_g=D, ln1_b=D, ln2_g=D, ln2_b=D)
PACK3 = dict(qk=4 * D, iqk=(IH + 1) * P, v=D, iw=IH, o=D, qk_b=4, iqk_b=IH + 1, v_b=D, iw_b=IH, o_b=D)


def pack_views(buf, widths, split={}):
    at, views = 0, {}
    for name, n in widths.items():
        view = buf[:, at:at + n]
        if name in split:
            view = view.rearrange("p (c d) -> p c d", c=split[name])
        views[name] = view
        at += n
    return views


def build(nc, io, out, stages=range(6)):
    with Scope(nc, "g") as g:
        x = g.sb("x", [P, TILES, D])
        pack0 = g.sb("pack0", [P, sum(PACK0.values())])
        g.w0 = pack_views(pack0, PACK0, {"fw2": FC})
        g.w0["w1"], g.w0["w2"], g.w0["b12"] = io["w1_top2"], io["w2_top2"], io["b12_top2"]
        pack1 = g.sb("pack1", [P, sum(PACK1.values())])
        g.w1 = pack_views(pack1, PACK1, {n: 2 for n in ("in_gr", "in_vr", "shrink", "f_ra", "f_ar", "i_ra", "i_ar", "out_r")})
        g.w1["in_all"] = pack1[:, 0:6 * P]
        g.decay = g.sb("decay", [P, 2])
        g.tiny = g.sb("tiny", [P, 1])
        pack3 = g.sb("pack3", [P, sum(PACK3.values())])
        g.w3 = pack_views(pack3, PACK3)
        g.cos, g.sin = io["cos"], io["sin"]
        pack2 = g.sb("pack2", [P, sum(PACK2.values())])
        g.w2 = pack_views(pack2, PACK2)
        g.w12 = g.sb("w12", [P, E, D])
        g.b12 = g.sb("b12", [P, TPG, D])
        g.carry = g.sb("carry", [P, E * TILES])
        g.stats = g.sb("stats", [P, TILES, 6])
        ident = g.sb("ident", [P, P])
        g.ident = ident[:, :]
        g.upto = g.sb("upto", [P, P], BF16)
        g.ones = g.sb("ones", [P, P], BF16)
        g.one32 = g.sb("one32", [P, TILES])
        g.rank = g.sb("rank", [P, TILES, E])
        g.trash = g.sb("trash", [P, 1])
        g.zeros = g.sb("zeros", [P, D])
        g.pack_in = [g.sem(f"pack_in{k}") for k in range(4)]
        g.cleared = g.sem("cleared")
        g.x_slots = nc.dram_tensor("x_slots", (TRASH + P, D), F32, kind="Internal").ap()
        g.y_slots = nc.dram_tensor("y_slots", (TRASH + P, D), F32, kind="Internal").ap()
        setup(nc, g, io, x, (pack0, pack1, pack2, pack3), ident)
        if 0 in stages:
            moe_top2(nc, "a", g, x, True, io)
        else:
            with Scope(nc, "dev") as s:
                sync, tensor, vector, scalar = later_constants(nc, s, g, io)
                block = s.block()
                block.sync(sync)
                block.tensor(tensor)
                block.scalar(scalar)
                block.vector(vector)

                @block.gpsimd
                def _(pool):
                    pool.wait_ge(g.cleared, 16 * (E + 2))
                    for k in range(4):
                        pool.wait_ge(g.pack_in[k], 16)
        if 1 in stages:
            hawk(nc, "b", g, x, None if 0 in stages else x)
        if 2 in stages:
            moe_top2(nc, "c", g, x, 1 not in stages)
        if 3 in stages:
            pair_moe(nc, "d", g, x, None if 2 in stages else x)
        if 4 in stages:
            sparse_attention(nc, "e", g, x)
        if 5 in stages:
            pair_moe(nc, "k", g, x, x)
        finish(nc, out, x)


def setup(nc, g, io, x, packs, ident):
    with Scope(nc, "setup") as s:
        loaded, made, zeroed = (s.sem(n) for n in ("loaded", "made", "zeroed"))
        block = s.block()

        @block.sync
        def _(sp):
            sp.dma_start(x[:, :, :], io["x"].rearrange("b (t p) d -> p (b t) d", p=P)).then_inc(loaded, 16)
            for k, pack in enumerate(packs):
                sp.dma_start(pack[:, :], io[f"pack{k}"]).then_inc(g.pack_in[k], 16)
            sp.wait_ge(loaded, 16)
            sp.wait_ge(g.pack_in[0], 16)

        @block.scalar
        def _(act):
            act.wait_ge(zeroed, 1)
            for e in range(E):
                act.dma_start(g.x_slots[e * CAP0:(e + 1) * CAP0, :].rearrange("(p j) d -> p j d", p=P),
                              g.zeros[:, :].unsqueeze(1).to_broadcast([P, ROWS0, D])).then_inc(g.cleared, 16)
            act.dma_start(g.x_slots[TRASH:TRASH + P, :], g.zeros[:, :]).then_inc(g.cleared, 16)
            act.dma_start(g.y_slots[TRASH:TRASH + P, :], g.zeros[:, :]).then_inc(g.cleared, 16)

        @block.vector
        def _(dve):
            nc.vector.memset(g.zeros[:, :], 0.0).then_inc(zeroed, 1)

        @block.gpsimd
        def _(pool):
            link = Chain(pool, made)
            link(nc.gpsimd.memset(ident[:, :], 0.0))
            link(nc.gpsimd.affine_select(out=ident[:, :], in_=ident[:, :], compare_op=ALU.not_equal, fill=1.0,
                                         base=0, pattern=[[-1, P]], channel_multiplier=1))
            link(nc.gpsimd.memset(g.ones[:, :], 1.0))
            link(nc.gpsimd.memset(g.one32[:, :], 1.0))
            link(nc.gpsimd.affine_select(out=g.upto[:, :], in_=g.ones[:, :], compare_op=ALU.is_ge, fill=0.0,
                                         base=0, pattern=[[1, P]], channel_multiplier=-1))
            link(nc.gpsimd.iota(g.rank[:, :, :], pattern=[[0, TILES], [-1, E]], base=E, channel_multiplier=0,
                                allow_small_or_imprecise_dtypes=True))
            link(nc.gpsimd.memset(g.carry[:, :], 1.0))
            link(nc.gpsimd.memset(g.carry[:, :].rearrange("p (e t) -> p e t", t=TILES)[:, :, 0], 0.0))
            link(nc.gpsimd.iota(g.trash[:, :], pattern=[[0, 1]], base=TRASH, channel_multiplier=1,
                                allow_small_or_imprecise_dtypes=True))


def finish(nc, out, x):
    with Scope(nc, "finish") as s:
        stored = s.sem("stored")
        block = s.block()

        @block.sync
        def _(sp):
            sp.dma_start(out.rearrange("b (t p) d -> p (b t) d", p=P), x[:, :, :]).then_inc(stored, 16)
            sp.wait_ge(stored, 16)


def chunks(a, rows=P):
    return np.concatenate([a[k:k + rows] for k in range(0, a.shape[0], rows)], axis=1)


def lay_out(i):
    cols = lambda v: np.ascontiguousarray(v.reshape(-1, P).T)
    f = {k: np.asarray(v) for k, v in i.items()}
    pack0 = np.concatenate([
        f["L0_ffn_Wr"].T, f["L0_ffn_fw1"], chunks(f["L0_ffn_fw2"]), cols(f["L0_ffn_fb1"]), cols(f["L0_ffn_fb2"])], axis=1)
    rest = lambda a, axis: [np.pad(a, [(0, REST) if k == axis else (0, 0) for k in range(2)]),
                            np.pad(a, [(REST, 0) if k == axis else (0, 0) for k in range(2)])]
    w_in, w_g = f["L0_attn_W_in"].T, f["L0_attn_W_gates"].T
    gate, value = w_in[:, :HID], w_in[:, HID:]
    both = lambda v: np.concatenate([v[:P], v[P:], v[P:]], axis=0).reshape(2, P, -1)
    pair = lambda v: np.concatenate(list(both(v.reshape(HID, -1))), axis=1)
    gates = []
    for m in (w_g[:, :HID], w_g[:, HID:]):
        gates += [m[:P, :P], *rest(m[P:, :P], 0), *rest(m[:P, P:], 1),
                  np.concatenate(rest(m[P:, P:], 1), axis=0)]
    w_out = f["L0_attn_W_out"].T
    pack1 = np.concatenate([
        gate[:, :P], value[:, :P], *rest(gate[:, P:], 1), *rest(value[:, P:], 1), f["L0_attn_W_grow"].T,
        chunks(f["L0_attn_W_shrink"].T), *gates, w_out[:P], *rest(w_out[P:], 0),
        f["L0_attn_gamma1"][:, None], f["L0_attn_gamma2"][:, None], pair(f["L0_attn_conv_w"][:, 0, :]),
        pair(f["L0_attn_conv_b"]), pair(f["L0_attn_b_gates"][:HID]), pair(f["L0_attn_b_gates"][HID:]),
        pair(f["L0_attn_forget_base"])], axis=1)
    rows = lambda v: np.broadcast_to(v[None, :], (P, v.size))
    w1 = f["L1_ffn_w1"]
    pack2 = np.concatenate([
        f["L1_ffn_in_proj_w"].T, f["L1_ffn_out_proj_w"].T, f["L1_ffn_wg"], cols(f["L1_ffn_b1"].reshape(-1)),
        cols(f["L1_ffn_b2"].reshape(-1)), rows(f["L1_ffn_in_proj_b"]), rows(f["L1_ffn_out_proj_b"]),
        rows(f["L1_ffn_ln1_g"]), rows(f["L1_ffn_ln1_b"]), rows(f["L1_ffn_ln2_g"]), rows(f["L1_ffn_ln2_b"])], axis=1)
    q, k, v = np.split(f["L1_attn_w_qkv"], 3)
    q_b, k_b, v_b = np.split(f["L1_attn_b_qkv"], 3)
    swap = lambda a: np.concatenate([a[D // 2:], a[:D // 2]], axis=0)
    twice = lambda a: np.concatenate([a, a], axis=0)
    heads = lambda a: np.concatenate([twice(part) for part in np.split(a, IH)], axis=0)
    pack3 = np.concatenate([
        q.T, swap(q).T, k.T, swap(k).T, heads(f["L1_attn_w_iq"]).T, twice(f["L1_attn_w_ik"]).T, v.T, f["L1_attn_w_iw"].T,
        f["L1_attn_w_o"].T, cols(q_b), cols(swap(q_b)), cols(k_b), cols(swap(k_b)), cols(heads(f["L1_attn_b_iq"])),
        cols(twice(f["L1_attn_b_ik"])), rows(v_b), rows(f["L1_attn_b_iw"]), rows(f["L1_attn_b_o"])], axis=1)
    half = D // 2
    freq = (1.0 / np.float32(10000.0) ** (np.arange(half, dtype=np.float32) / np.float32(half))).astype(np.float32)
    angle = freq[:, None] * np.arange(SEQ, dtype=np.float32)[None, :]
    return {
        "pack3": pack3,
        "cos": twice(np.cos(angle)),
        "sin": np.concatenate([-np.sin(angle), np.sin(angle)], axis=0),
        "pack2": pack2,
        "w1t_top1": chunks(w1.transpose(0, 2, 1).reshape(E * FF, D)),
        "w2_top1": chunks(f["L1_ffn_w2"].reshape(E * FF, D)),
        "pack1": pack1,
        "x": f["L0_attn_x"],
        "pack0": pack0,
        "w1_top2": f["L0_ffn_W1"].reshape(E * D, FF),
        "b12_top2": np.concatenate([np.concatenate([cols(f["L0_ffn_b1"][e]), cols(f["L0_ffn_b2"][e])], axis=1)
                                    for e in range(E)], axis=0),
        "w2_top2": np.concatenate([chunks(f["L0_ffn_W2"][e]) for e in range(E)], axis=0),
    }


def kernel(**inputs):
    import concourse.bacc as bacc
    from concourse.bass_utils import run_bass_kernel_spmd

    nc = bacc.Bacc("TRN2", target_bir_lowering=False, num_devices=1)
    arrays, io = {}, {}
    for name, a in lay_out(inputs).items():
        arrays[name] = np.ascontiguousarray(a)
        io[name] = nc.dram_tensor(name, a.shape, mybir.dt.from_np(a.dtype), kind="ExternalInput").ap()
    out = nc.dram_tensor("out", (BATCH, SEQ, D), F32, kind="ExternalOutput").ap()
    build(nc, io, out)
    r = run_bass_kernel_spmd(nc, [arrays], core_ids=[0])
    return r.results[0]["out"]
```

```python
from contextlib import ExitStack

import concourse.bass as bass
import numpy as np
from concourse import mybir

P = 128
F32 = mybir.dt.float32
F32R = mybir.dt.float32r
BF16 = mybir.dt.bfloat16
U32 = mybir.dt.uint32
ALU = mybir.AluOpType
ACT = mybir.ActivationFunctionType
AX = mybir.AxisListType.X

BATCH, SEQ, D = 2, 2048, 128
TOK = BATCH * SEQ
TILES = TOK // P
TPG = 4
GROUP = TPG * P
GROUPS = TOK // GROUP
PAIRS = GROUPS // 2

E = 8
FF = 512
FC = FF // P
CAP0 = int(1.25 * (TOK * 2 / E))
ROWS0 = CAP0 // P
UNITS0 = [TPG] * (ROWS0 // TPG) + ([ROWS0 % TPG] if ROWS0 % TPG else [])
TRASH = E * CAP0
CAP1 = TOK // E
LN_EPS = 1e-5


class Scope:

    def __init__(self, nc, tag):
        self.nc, self.tag, self.stack, self.sems = nc, tag, ExitStack(), []

    def __enter__(self):
        self.stack.__enter__()
        return self

    def __exit__(self, *a):
        self.stack.__exit__(*a)
        for sem in self.sems:
            self.nc.gpsimd.sem_clear(sem)
            self.nc.release_semaphore(sem)

    def sb(self, name, shape, dt=F32):
        return self.stack.enter_context(self.nc.sbuf_tensor(f"{self.tag}_{name}", shape, dt))

    def ps(self, name, shape, dt=F32):
        return self.stack.enter_context(self.nc.psum_tensor(f"{self.tag}_{name}", shape, dt))

    def sem(self, name):
        self.sems.append(self.nc.alloc_semaphore(f"{self.tag}_{name}"))
        return self.sems[-1]

    def gather_sem(self, name):
        return self.nc.alloc_semaphore(f"{self.tag}_{name}")

    def counter(self, name, credit=0):
        return Signal(self.sem(name), credit)

    def block(self):
        return self.stack.enter_context(self.nc.Block())


class Signal:

    def __init__(self, sem, credit=0):
        self.sem, self.credit = sem, credit

    def ready(self, u):
        return self.credit + 1 + u

    def free(self, u, back=None):
        return self.credit + 1 - (self.credit if back is None else back) + u


class Chain:

    def __init__(self, eng, sem):
        self.eng, self.sem, self.n = eng, sem, 0

    def __call__(self, ins):
        self.n += 1
        ins.then_inc(self.sem, 1)
        self.eng.wait_ge(self.sem, self.n)


def tiles_of(buf, first, n):
    return buf[:, bass.ds(first, n), :]


def over(ap, n):
    return ap.unsqueeze(2).to_broadcast([ap.shape[0], ap.shape[1], n])




def row_stats(nc, tag, stats, mean, factors, src=None):
    with Scope(nc, tag) as s:
        diff = s.sb("diff", [P, TILES])
        var = s.sb("var", [P, TILES])
        sq = s.sb("sq", [P, TILES])
        arg = [s.sb(f"arg{k}", [P, TILES]) for k in range(len(factors))]
        root = [s.sb(f"root{k}", [P, TILES]) for k in range(len(factors))]
        counted, vdone, arg_ready, root_ready = (s.sem(n) for n in ("counted", "vdone", "arg_ready", "root_ready"))
        block = s.block()

        @block.vector
        def _(dve):
            if src is not None:
                for t in range(TILES):
                    last = nc.vector.bn_stats(stats[:, t, :], src[:, t, :])
                last.then_inc(counted, 1)
                dve.wait_ge(counted, 1)
            link = Chain(dve, vdone)
            nc.vector.tensor_tensor(mean[:, :], stats[:, :, 1], stats[:, :, 4], ALU.add).then_inc(vdone, 1)
            nc.vector.tensor_tensor(diff[:, :], stats[:, :, 1], stats[:, :, 4], ALU.subtract).then_inc(vdone, 1)
            nc.vector.tensor_tensor(var[:, :], stats[:, :, 2], stats[:, :, 5], ALU.add).then_inc(vdone, 1)
            link.n = 3
            dve.wait_ge(vdone, 3)
            link(nc.vector.tensor_scalar(mean[:, :], mean[:, :], 0.5, None, ALU.mult))
            link(nc.vector.scalar_tensor_tensor(diff[:, :], diff[:, :], 0.25, diff[:, :], ALU.mult, ALU.mult))
            link(nc.vector.scalar_tensor_tensor(var[:, :], var[:, :], 1.0 / D, diff[:, :], ALU.mult, ALU.add))
            for k, (_, eps, about_mean) in enumerate(factors):
                base = var
                if not about_mean:
                    link(nc.vector.tensor_tensor(sq[:, :], mean[:, :], mean[:, :], ALU.mult))
                    link(nc.vector.tensor_tensor(sq[:, :], sq[:, :], var[:, :], ALU.add))
                    base = sq
                nc.vector.tensor_scalar(arg[k][:, :], base[:, :], eps, None, ALU.add).then_inc(arg_ready, 1)
            for k, (out, _, _) in enumerate(factors):
                dve.wait_ge(root_ready, k + 1)
                link(nc.vector.reciprocal(out[:, :], root[k][:, :]))
                link(nc.vector.tensor_tensor(root[k][:, :], out[:, :], out[:, :], ALU.mult))
                link(nc.vector.tensor_tensor(root[k][:, :], root[k][:, :], arg[k][:, :], ALU.mult))
                link(nc.vector.tensor_scalar(root[k][:, :], root[k][:, :], -0.5, 1.5, ALU.mult, ALU.add))
                link(nc.vector.tensor_tensor(out[:, :], out[:, :], root[k][:, :], ALU.mult))

        @block.scalar
        def _(act):
            for k in range(len(factors)):
                act.wait_ge(arg_ready, k + 1)
                nc.scalar.activation(root[k][:, :], arg[k][:, :], ACT.Sqrt).then_inc(root_ready, 1)


def a_pair_behind(eng, first, second):
    for h in range(2):
        first(0, h)
    with eng.Fori(1, PAIRS) as i:
        for h in range(2):
            first(i, h)
            second(i - 1, h)
    for h in range(2):
        second(PAIRS - 1, h)


def a_group_behind(eng, first, second):
    first(0, 0)
    with eng.Fori(0, PAIRS - 1) as i:
        first(i, 1)
        second(i, 0)
        first(i + 1, 0)
        second(i, 1)
    first(PAIRS - 1, 1)
    second(PAIRS - 1, 0)
    second(PAIRS - 1, 1)




class FfnPipe:

    def __init__(self, s, ahead=2):
        self.ahead = ahead
        self.operands(s)
        self.yt = s.sb("yt", [P, 2, GROUP])
        self.p_x = s.ps("p_x", [P, 2, GROUP])
        self.p_h = s.ps("p_h", [P, 2, GROUP])
        self.p_y = s.ps("p_y", [P, GROUP])
        self.p_r = s.ps("p_r", [P, GROUP])
        self.x_transposed = s.counter("x_transposed", ahead)
        self.x_copied = s.counter("x_copied", 2)
        self.up_done = s.counter("up_done", 2 * FC)
        self.gelu_done = s.counter("gelu_done", 2)
        self.down_done = s.counter("down_done", ahead)
        self.y_copied = s.counter("y_copied", ahead)
        self.y_transposed = s.counter("y_transposed", 2)
        self.rows_taken = s.counter("rows_taken", 1)

    def operands(self, s):
        self.xg = s.sb("xg", [P, 2, GROUP])
        self.hid = s.sb("hid", [P, 2, FC, GROUP])

    def pe_credits(self, pe):
        pe.sem_inc(self.x_transposed.sem, self.ahead)
        pe.sem_inc(self.up_done.sem, 2 * FC)
        pe.sem_inc(self.down_done.sem, self.ahead)
        pe.sem_inc(self.y_transposed.sem, 2)

    def act_credits(self, act):
        act.sem_inc(self.x_copied.sem, 2)
        act.sem_inc(self.gelu_done.sem, 2)
        act.sem_inc(self.y_copied.sem, self.ahead)

    def transpose_x(self, nc, pe, u, h, rows, ident):
        pe.wait_ge(self.x_copied.sem, self.x_copied.free(u))
        for t, row in enumerate(rows):
            last = nc.tensor.transpose(self.p_x[:, h, t * P:(t + 1) * P], row, ident)
        last.then_inc(self.x_transposed.sem, 1)

    def up(self, nc, pe, u, xg, w1):
        for c in range(FC):
            pe.wait_ge(self.gelu_done.sem, self.gelu_done.free(FC * u + c))
            nc.tensor.matmul(self.p_h[:, c % 2, 0:xg.shape[1]], w1[:, c * P:(c + 1) * P], xg,
                             start=True, stop=True).then_inc(self.up_done.sem, 1)

    def down(self, nc, pe, u, h, n, w2):
        pe.wait_ge(self.y_copied.sem, self.y_copied.free(u, 1))
        for c in range(FC):
            pe.wait_ge(self.gelu_done.sem, self.gelu_done.ready(FC * u + c))
            last = nc.tensor.matmul(self.p_y[:, 0:n * P], w2[:, c, :], self.hid[:, h, c, 0:n * P],
                                    start=(c == 0), stop=(c == FC - 1))
        last.then_inc(self.down_done.sem, 1)

    def transpose_y(self, nc, pe, u, h, n, ident):
        pe.wait_ge(self.y_copied.sem, self.y_copied.ready(u))
        pe.wait_ge(self.rows_taken.sem, self.rows_taken.free(u))
        for t in range(n):
            last = nc.tensor.transpose(self.p_r[:, t * P:(t + 1) * P], self.yt[:, h, t * P:(t + 1) * P], ident)
        last.then_inc(self.y_transposed.sem, 1)

    def copy_x(self, nc, act, u, h, n):
        act.wait_ge(self.x_transposed.sem, self.x_transposed.ready(u))
        act.wait_ge(self.up_done.sem, self.up_done.free(FC * u + FC - 1))
        nc.scalar.activation(self.xg[:, h, 0:n * P], self.p_x[:, h, 0:n * P], ACT.Copy).then_inc(self.x_copied.sem, 1)

    def gelu(self, nc, act, u, h, n, b1):
        act.wait_ge(self.down_done.sem, self.down_done.free(u, 2))
        for c in range(FC):
            act.wait_ge(self.up_done.sem, self.up_done.ready(FC * u + c))
            nc.scalar.activation(self.hid[:, h, c, 0:n * P], self.p_h[:, c % 2, 0:n * P], ACT.Gelu,
                                 bias=b1[:, c:c + 1]).then_inc(self.gelu_done.sem, 1)

    def copy_y(self, nc, act, u, h, n, b2):
        act.wait_ge(self.down_done.sem, self.down_done.ready(u))
        act.wait_ge(self.y_transposed.sem, self.y_transposed.free(u))
        nc.scalar.activation(self.yt[:, h, 0:n * P], self.p_y[:, 0:n * P], ACT.Identity, bias=b2).then_inc(self.y_copied.sem, 1)

    def take_rows(self, nc, dve, u, n, out):
        dve.wait_ge(self.y_transposed.sem, self.y_transposed.ready(u))
        nc.vector.tensor_copy(out, self.p_r[:, 0:n * P].rearrange("p (t d) -> p t d", d=P)).then_inc(self.rows_taken.sem, 1)


class SplitFfnPipe(FfnPipe):

    def operands(self, s):
        self.xh, self.xl = (s.sb(n, [P, 2, GROUP], F32R) for n in ("xh", "xl"))
        self.hid = s.sb("hid", [P, FC, GROUP])
        self.hh, self.hl = (s.sb(n, [P, 2, FC, GROUP], F32R) for n in ("hh", "hl"))
        self.x_split = s.counter("x_split", 2)
        self.h_high = s.counter("h_high")
        self.h_split = [s.counter(f"h_split{k}", FC // 2) for k in range(2)]

    def dve_credits(self, dve):
        dve.sem_inc(self.x_split.sem, 2)
        dve.sem_inc(self.h_split[0].sem, FC // 2)
        dve.sem_inc(self.rows_taken.sem, 1)

    def transpose_x(self, nc, pe, u, h, rows, ident):
        pe.wait_ge(self.x_split.sem, self.x_split.free(u))
        for t, row in enumerate(rows):
            last = nc.tensor.transpose(self.p_x[:, h, t * P:(t + 1) * P], row, ident)
        last.then_inc(self.x_transposed.sem, 1)

    def up(self, nc, pe, u, h, n, w1h, w1l):
        pe.wait_ge(self.x_split.sem, self.x_split.ready(u))
        xh, xl = self.xh[:, h, 0:n * P], self.xl[:, h, 0:n * P]
        for c in range(FC):
            pe.wait_ge(self.gelu_done.sem, self.gelu_done.free(FC * u + c))
            bank, part = self.p_h[:, c % 2, 0:n * P], slice(c * P, (c + 1) * P)
            nc.tensor.matmul(bank, w1h[:, part], xh, start=True, stop=False)
            nc.tensor.matmul(bank, w1h[:, part], xl, start=False, stop=False)
            nc.tensor.matmul(bank, w1l[:, part], xh, start=False, stop=True).then_inc(self.up_done.sem, 1)

    def down(self, nc, pe, u, h, n, w2h, w2l):
        pe.wait_ge(self.y_copied.sem, self.y_copied.free(u, 1))
        for c in range(FC):
            pe.wait_ge(self.h_split[c % 2].sem, self.h_split[c % 2].ready(FC // 2 * u + c // 2))
            bank, part = self.p_y[:, 0:n * P], slice(c * D, (c + 1) * D)
            nc.tensor.matmul(bank, w2h[:, part], self.hh[:, h, c, 0:n * P], start=(c == 0), stop=False)
            nc.tensor.matmul(bank, w2h[:, part], self.hl[:, h, c, 0:n * P], start=False, stop=False)
            last = nc.tensor.matmul(bank, w2l[:, part], self.hh[:, h, c, 0:n * P], start=False, stop=(c == FC - 1))
        last.then_inc(self.down_done.sem, 1)

    def copy_x(self, nc, act, u, h, n):
        act.wait_ge(self.x_transposed.sem, self.x_transposed.ready(u))
        act.wait_ge(self.up_done.sem, self.up_done.free(FC * u + FC - 1))
        nc.scalar.activation(self.xh[:, h, 0:n * P], self.p_x[:, h, 0:n * P], ACT.Copy).then_inc(self.x_copied.sem, 1)

    def split_x(self, nc, dve, u, h, n):
        dve.wait_ge(self.x_copied.sem, self.x_copied.ready(u))
        nc.vector.tensor_tensor(self.xl[:, h, 0:n * P], self.p_x[:, h, 0:n * P], self.xh[:, h, 0:n * P].bitcast(F32),
                                ALU.subtract).then_inc(self.x_split.sem, 1)

    def gelu(self, nc, act, u, h, n, b1):
        for c in range(FC):
            act.wait_ge(self.up_done.sem, self.up_done.ready(FC * u + c))
            act.wait_ge(self.h_split[c % 2].sem, self.h_split[c % 2].free(FC // 2 * u + c // 2))
            nc.scalar.activation(self.hid[:, c, 0:n * P], self.p_h[:, c % 2, 0:n * P], ACT.Gelu,
                                 bias=b1[:, c:c + 1]).then_inc(self.gelu_done.sem, 1)

    def low(self, engine, eng, u, h, n, c):
        eng.wait_ge(self.h_high.sem, self.h_high.ready(FC * u + c))
        engine.tensor_tensor(self.hl[:, h, c, 0:n * P], self.hid[:, c, 0:n * P], self.hh[:, h, c, 0:n * P].bitcast(F32),
                             ALU.subtract).then_inc(self.h_split[c % 2].sem, 1)

    def split_h(self, nc, dve, u, h, n):
        dve.wait_ge(self.down_done.sem, self.down_done.free(u, 2))
        for c in range(FC):
            dve.wait_ge(self.gelu_done.sem, self.gelu_done.ready(FC * u + c))
            nc.vector.tensor_copy(self.hh[:, h, c, 0:n * P], self.hid[:, c, 0:n * P]).then_inc(self.h_high.sem, 1)
            if c % 2:
                self.low(nc.vector, dve, u, h, n, c - 1)

    def split_odd_h(self, nc, pool, u, h, n):
        for c in range(1, FC, 2):
            self.low(nc.gpsimd, pool, u, h, n, c)




def moe_top2(nc, tag, g, x, take_stats, io=None):
    with Scope(nc, tag) as s:
        mean, rstd = s.sb("mean", [P, TILES]), s.sb("rstd", [P, TILES])
        yfb = s.sb("yfb", [P, TILES, D])
        logits = s.sb("logits", [P, TILES, E])
        slot = s.sb("slot", [P, 2, TILES], U32)
        wt = s.sb("wt", [P, 2, TILES])
        fallback = s.sb("fallback", [P, TILES])
        row_stats(nc, tag + "s", g.stats, mean, [(rstd, LN_EPS, True)], x if take_stats else None)
        with Scope(nc, tag + "x") as s2:
            xn = s2.sb("xn", [P, TILES, D])
            xt = s2.sb("xt", [P, TOK])
            router(nc, tag + "l", g, x, mean, rstd, xn, xt, logits)
            route_top2(nc, tag + "r", g, logits, slot, wt, fallback)
            fallback_ffn(nc, tag + "f", g, xn, xt, slot, yfb)
        experts_top2(nc, tag + "e", g)
        combine_top2(nc, tag + "c", g, x, yfb, slot, wt, fallback, io)


def router(nc, tag, g, x, mean, rstd, xn, xt, logits):
    with Scope(nc, tag) as s:
        xs = s.sb("xs", [P, 2, TPG, D])
        xg = s.sb("xg", [P, 2, GROUP])
        p_x = s.ps("p_x", [P, 2, GROUP])
        p_l = s.ps("p_l", [P, 2, GROUP])
        normalized = s.counter("normalized")
        xs_kept = s.counter("xs_kept", 2)
        transposed = s.counter("transposed", 2)
        copied = s.counter("copied", 2)
        x_kept = s.counter("x_kept", 2)
        routed = s.counter("routed", 2)
        logits_kept = s.counter("logits_kept", 2)
        block = s.block()
        w = g.w0

        @block.vector
        def _(dve):
            dve.sem_inc(logits_kept.sem, 2)

            def keep(i, h):
                u = 2 * i + h
                dve.wait_ge(routed.sem, routed.ready(u))
                nc.vector.tensor_copy(tiles_of(logits, TPG * u, TPG),
                                      p_l[:, h, 0:TPG * E].rearrange("p (t e) -> p t e", e=E)).then_inc(logits_kept.sem, 1)

            def normalize(i, h):
                u = 2 * i + h
                dve.wait_ge(transposed.sem, transposed.free(u))
                dve.wait_ge(xs_kept.sem, xs_kept.free(u))
                for t in range(TPG):
                    k = TPG * u + t
                    last = nc.vector.tensor_scalar(xs[:, h, t:t + 1, :], x[:, bass.ds(k, 1), :],
                                                   mean[:, bass.ds(k, 1)], rstd[:, bass.ds(k, 1)],
                                                   ALU.subtract, ALU.mult)
                last.then_inc(normalized.sem, 1)

            a_pair_behind(dve, normalize, keep)

        @block.gpsimd
        def _(pool):
            pool.sem_inc(xs_kept.sem, 2)
            with pool.Fori(0, PAIRS) as i:
                for h in range(2):
                    u = 2 * i + h
                    pool.wait_ge(normalized.sem, normalized.ready(u))
                    nc.gpsimd.tensor_copy(tiles_of(xn, TPG * u, TPG), xs[:, h, :, :]).then_inc(xs_kept.sem, 1)

        @block.tensor
        def _(pe):
            pe.sem_inc(transposed.sem, 2)
            pe.sem_inc(routed.sem, 2)

            def transpose(i, h):
                u = 2 * i + h
                pe.wait_ge(normalized.sem, normalized.ready(u))
                pe.wait_ge(x_kept.sem, x_kept.free(u))
                for t in range(TPG):
                    last = nc.tensor.transpose(p_x[:, h, t * P:(t + 1) * P], xs[:, h, t, :], g.ident)
                last.then_inc(transposed.sem, 1)

            def route(i, h):
                u = 2 * i + h
                pe.wait_ge(copied.sem, copied.ready(u))
                pe.wait_ge(logits_kept.sem, logits_kept.free(u))
                for t in range(TPG):
                    last = nc.tensor.matmul(p_l[:, h, t * E:(t + 1) * E], xg[:, h, t * P:(t + 1) * P],
                                            w["wr"], start=True, stop=True)
                last.then_inc(routed.sem, 1)

            a_group_behind(pe, transpose, route)

        @block.scalar
        def _(act):
            act.sem_inc(copied.sem, 2)
            act.sem_inc(x_kept.sem, 2)
            with act.Fori(0, PAIRS) as i:
                for h in range(2):
                    u = 2 * i + h
                    act.wait_ge(transposed.sem, transposed.ready(u))
                    act.wait_ge(routed.sem, routed.free(u))
                    nc.scalar.activation(xg[:, h, :], p_x[:, h, :], ACT.Copy).then_inc(copied.sem, 1)
                    nc.scalar.activation(xt[:, bass.ds(GROUP * u, GROUP)], p_x[:, h, :], ACT.Copy).then_inc(x_kept.sem, 1)


def fallback_ffn(nc, tag, g, xn, xt, slot, yfb):
    with Scope(nc, tag) as s:
        pipe = FfnPipe(s)
        scattered = s.gather_sem("scattered")
        block = s.block()
        w = g.w0

        @block.vector
        def _(dve):
            dve.sem_inc(pipe.rows_taken.sem, 1)
            with dve.Fori(0, PAIRS) as i:
                for h in range(2):
                    u = 2 * i + h
                    pipe.take_rows(nc, dve, u, TPG, tiles_of(yfb, TPG * u, TPG))

        @block.gpsimd
        def _(pool):
            pool.wait_ge(g.cleared, 16 * (E + 2))
            for k in range(2):
                for t in range(TILES):
                    pool.indirect_dma_start(g.x_slots, bass.IndirectOffsetOnAxis(ap=slot[:, k, t:t + 1], axis=0),
                                            xn[:, t, :], None).then_inc(scattered, 16)
            pool.wait_ge(scattered, 16 * 2 * TILES)

        @block.tensor
        def _(pe):
            pipe.pe_credits(pe)

            def turn(i, first):
                for h in range(2):
                    u = 2 * i + h
                    pipe.up(nc, pe, u, xt[:, bass.ds(GROUP * u, GROUP)], w["fw1"])
                    if not (first and h == 0):
                        pipe.down(nc, pe, u - 1, 1 - h, TPG, w["fw2"])
                    if not first:
                        pipe.transpose_y(nc, pe, u - 2, h, TPG, g.ident)

            turn(0, True)
            with pe.Fori(1, PAIRS) as i:
                turn(i, False)
            pipe.down(nc, pe, GROUPS - 1, 1, TPG, w["fw2"])
            for h in range(2):
                pipe.transpose_y(nc, pe, GROUPS - 2 + h, h, TPG, g.ident)

        @block.scalar
        def _(act):
            pipe.act_credits(act)

            def turn(i, first):
                for h in range(2):
                    u = 2 * i + h
                    pipe.gelu(nc, act, u, h, TPG, w["fb1"])
                    if not (first and h == 0):
                        pipe.copy_y(nc, act, u - 1, 1 - h, TPG, w["fb2"])

            turn(0, True)
            with act.Fori(1, PAIRS) as i:
                turn(i, False)
            pipe.copy_y(nc, act, GROUPS - 1, 1, TPG, w["fb2"])


def probabilities(nc, tag, s, logits, probs, top):
    rest = s.sb("rest", [P, TILES, E])
    total = s.sb("total", [P, TILES])
    shifted, exps = s.sem("shifted"), s.sem("exps")

    def vector(link):
        link(nc.vector.tensor_reduce(total[:, :], logits[:, :, :], AX, ALU.max))
        link(nc.vector.tensor_tensor(rest[:, :, :], logits[:, :, :], over(total[:, :], E), ALU.subtract))
        link.eng.sem_inc(shifted, 1)
        link.eng.wait_ge(exps, 1)
        link(nc.vector.tensor_reduce(total[:, :], probs[:, :, :], AX, ALU.add))
        link(nc.vector.reciprocal(total[:, :], total[:, :]))
        link(nc.vector.tensor_tensor(probs[:, :, :], probs[:, :, :], over(total[:, :], E), ALU.mult))
        link(nc.vector.tensor_reduce(top, probs[:, :, :], AX, ALU.max))

    def scalar(act):
        act.wait_ge(shifted, 1)
        nc.scalar.activation(probs[:, :, :], rest[:, :, :], ACT.Exp).then_inc(exps, 1)

    return vector, scalar


def first_largest(nc, link, probs, top, rank, code, best, onehot):
    link(nc.vector.tensor_tensor(code[:, :, :], probs, over(top, E), ALU.is_equal))
    link(nc.vector.tensor_tensor(code[:, :, :], code[:, :, :], rank[:, :, :], ALU.mult))
    link(nc.vector.tensor_reduce(best[:, :], code[:, :, :], AX, ALU.max))
    link(nc.vector.tensor_tensor(onehot, rank[:, :, :], over(best[:, :], E), ALU.is_equal))


def route_top2(nc, tag, g, logits, slot, wt, fallback):
    with Scope(nc, tag) as s:
        probs = s.sb("probs", [P, TILES, E])
        top = s.sb("top", [P, 2, TILES])
        den = s.sb("den", [P, TILES])
        code = s.sb("code", [P, TILES, E])
        best = s.sb("best", [P, TILES])
        hot = s.sb("hot", [P, 2, TILES, E])
        match = s.sb("match", [P, TILES, E])
        second = s.sb("second", [P, TILES, E])
        pos = s.sb("pos", [P, TILES, E])
        elig = s.sb("elig", [P, TILES], BF16)
        before = s.sb("before", [P, TILES])
        over_cap = s.sb("over_cap", [P, TILES])
        valid = s.sb("valid", [P, TILES])
        slot_f = s.sb("slot_f", [P, 2, TILES])
        p_c = s.ps("p_c", [P, 2, TILES])
        vdone, counted, eligible = s.sem("vdone"), s.sem("counted"), s.sem("eligible")
        soft_v, soft_a = probabilities(nc, tag, s, logits, probs, top[:, 0, :])
        block = s.block()

        @block.scalar
        def _(act):
            soft_a(act)

        @block.tensor
        def _(pe):
            for e in range(E):
                pe.wait_ge(eligible, e + 1)
                nc.tensor.matmul(p_c[:, 0, :], g.upto[:, :], elig[:, :], start=True, stop=True)
                nc.tensor.matmul(p_c[:, 1, :], g.ones[:, :], elig[:, :], start=True, stop=True).then_inc(counted, 1)

        @block.vector
        def _(dve):
            link = Chain(dve, vdone)
            soft_v(link)
            first_largest(nc, link, probs[:, :, :], top[:, 0, :], g.rank, code, best, hot[:, 0, :, :])
            link(nc.vector.scalar_tensor_tensor(second[:, :, :], hot[:, 0, :, :], -2.0, probs[:, :, :], ALU.mult, ALU.add))
            link(nc.vector.tensor_reduce(top[:, 1, :], second[:, :, :], AX, ALU.max))
            first_largest(nc, link, second[:, :, :], top[:, 1, :], g.rank, code, best, hot[:, 1, :, :])
            link(nc.vector.tensor_tensor(den[:, :], top[:, 0, :], top[:, 1, :], ALU.add))
            link(nc.vector.tensor_scalar(den[:, :], den[:, :], 1e-9, None, ALU.max))
            link(nc.vector.reciprocal(den[:, :], den[:, :]))
            link(nc.vector.tensor_tensor(match[:, :, :], hot[:, 0, :, :], hot[:, 1, :, :], ALU.add))
            link(nc.vector.memset(fallback[:, :], 0.0))
            for e in range(E):
                nc.vector.scalar_tensor_tensor(elig[:, :], fallback[:, :], 0.5, match[:, :, e], ALU.is_lt, ALU.mult)\
                    .then_inc(eligible, 1)
                dve.wait_ge(counted, e + 1)
                link(nc.vector.tensor_tensor_scan(before[:, :], g.one32[:, :], p_c[:, 1, :], 0.0, ALU.mult, ALU.add))
                link(nc.vector.tensor_tensor(before[:, :], before[:, :], p_c[:, 1, :], ALU.subtract))
                link(nc.vector.scalar_tensor_tensor(before[:, :], p_c[:, 0, :], -1.0, before[:, :], ALU.add, ALU.add))
                nc.vector.tensor_scalar(pos[:, :, e], before[:, :], float(e * CAP0), None, ALU.add)
                link(nc.vector.scalar_tensor_tensor(over_cap[:, :], before[:, :], float(CAP0), elig[:, :], ALU.is_ge, ALU.mult))
                link(nc.vector.tensor_tensor(fallback[:, :], fallback[:, :], over_cap[:, :], ALU.max))
            link(nc.vector.tensor_scalar(valid[:, :], fallback[:, :], -1.0, 1.0, ALU.mult, ALU.add))
            for k in range(2):
                link(nc.vector.tensor_tensor(code[:, :, :], hot[:, k, :, :], pos[:, :, :], ALU.mult))
                link(nc.vector.tensor_reduce(slot_f[:, k, :], code[:, :, :], AX, ALU.add))
                link(nc.vector.scalar_tensor_tensor(slot_f[:, k, :], slot_f[:, k, :], g.trash[:, :], valid[:, :],
                                                    ALU.subtract, ALU.mult))
                link(nc.vector.tensor_scalar(slot_f[:, k, :], slot_f[:, k, :], g.trash[:, :], None, ALU.add))
                link(nc.vector.tensor_copy(slot[:, k, :], slot_f[:, k, :]))
                link(nc.vector.tensor_tensor(wt[:, k, :], top[:, k, :], den[:, :], ALU.mult))
                link(nc.vector.tensor_tensor(wt[:, k, :], wt[:, k, :], valid[:, :], ALU.mult))


def experts_top2(nc, tag, g):
    w = g.w0
    with Scope(nc, tag) as s:
        NU = len(UNITS0)
        pipe = SplitFfnPipe(s, ahead=2 * NU)
        rows = s.sb("rows", [P, 2, ROWS0, D])
        outs = s.sb("outs", [P, E * ROWS0, D])
        weights = s.sb("weights", [P, 2, 2, FF])
        w_high, w_low = (s.sb(n, [P, 2, 2, FF], F32R) for n in ("w_high", "w_low"))
        bias = s.sb("bias", [P, 2, FC + 1])
        rows_in = [s.sem(f"rows_in{h}") for h in range(2)]
        weights_in = [s.sem(f"weights_in{h}") for h in range(2)]
        stored = [s.gather_sem(f"stored{h}") for h in range(2)]
        w_rounded = s.counter("w_rounded")
        weights_split = s.counter("weights_split")
        outs_ready = s.counter("outs_ready")
        block = s.block()
        first = [sum(UNITS0[:k]) for k in range(NU)]
        turn = [(h, k, UNITS0[k]) for h in range(2) for k in range(NU)]
        U = 2 * NU
        TURNS = E // 2

        def in_turns(eng, body):
            body(0, at_first=True)
            with eng.Fori(1, TURNS - 1) as i:
                body(i)
            body(TURNS - 1, at_last=True)

        @block.gpsimd
        def _(pool):
            def store(i, h):
                pool.wait_ge(outs_ready.sem, outs_ready.ready(2 * i + h))
                pool.dma_start(g.y_slots[bass.ds((2 * i + h) * CAP0, CAP0), :].rearrange("(p j) d -> p j d", p=P),
                               tiles_of(outs, (2 * i + h) * ROWS0, ROWS0)).then_inc(stored[h], 16)

            def two_experts(i, at_first=False, at_last=False):
                for n in range(U):
                    pipe.split_odd_h(nc, pool, U * i + n, n % 2, turn[n][2])
                    if n == 1:
                        if not at_first:
                            store(i - 1, 1)
                    if n == NU + 1:
                        store(i, 0)

            pool.sem_inc(pipe.h_split[1].sem, FC // 2)
            in_turns(pool, two_experts)
            store(TURNS - 1, 1)
            for h in range(2):
                pool.wait_ge(stored[h], 16 * (E // 2))

        @block.sync
        def _(sp):
            with sp.Fori(0, E // 2) as i:
                for h in range(2):
                    e = 2 * i + h
                    sp.wait_ge(pipe.y_copied.sem, pipe.y_copied.free(NU * e + NU - 1))
                    sp.dma_start(weights[:, h, 0, :], w["w1"][bass.ds(e * D, D), :]).then_inc(weights_in[h], 16)
                    sp.dma_start(weights[:, h, 1, :], w["w2"][bass.ds(e * P, P), :]).then_inc(weights_in[h], 16)
                    sp.dma_start(bias[:, h, :], w["b12"][bass.ds(e * P, P), :]).then_inc(weights_in[h], 16)
                    sp.wait_ge(pipe.x_transposed.sem, pipe.x_transposed.free(NU * e + NU - 1))
                    sp.dma_start(rows[:, h, :, :], g.x_slots[bass.ds(e * CAP0, CAP0), :]
                                 .rearrange("(p j) d -> p j d", p=P)).then_inc(rows_in[h], 16)

        @block.tensor
        def _(pe):
            pipe.pe_credits(pe)

            def into(i, n):
                h, k, m = turn[n % U]
                if k == 0:
                    pe.wait_ge(rows_in[h], 16 * (i + n // U) + 16)
                pipe.transpose_x(nc, pe, U * i + n, n % 2, [rows[:, h, first[k] + t, :] for t in range(m)], g.ident)

            def up(i, n):
                h, k, m = turn[n]
                if k == 0:
                    pe.wait_ge(weights_split.sem, weights_split.ready(2 * i + h))
                pipe.up(nc, pe, U * i + n, n % 2, m, w_high[:, h, 0, :], w_low[:, h, 0, :])

            def down(i, n):
                h, k, m = turn[n % U]
                pipe.down(nc, pe, U * i + n, n % 2, m, w_high[:, h, 1, :], w_low[:, h, 1, :])

            def out(i, n):
                pipe.transpose_y(nc, pe, U * i + n, n % 2, turn[n % U][2], g.ident)

            def two_experts(i, at_first=False, at_last=False):
                for n in range(U):
                    if not (at_last and n == U - 1):
                        into(i, n + 1)
                    up(i, n)
                    if not (at_first and n < 1):
                        down(i, n - 1)
                    if not (at_first and n < 2):
                        out(i, n - 2)

            into(0, 0)
            in_turns(pe, two_experts)
            down(TURNS - 1, U - 1)
            out(TURNS - 1, U - 2)
            out(TURNS - 1, U - 1)

        @block.scalar
        def _(act):
            pipe.act_credits(act)

            def copy_y(i, n):
                h, k, m = turn[n % U]
                pipe.copy_y(nc, act, U * i + n, n % 2, m, bias[:, h, FC:FC + 1])

            def two_experts(i, at_first=False, at_last=False):
                for n in range(U):
                    h, _, m = turn[n]
                    if not (at_last and n == U - 1):
                        pipe.copy_x(nc, act, U * i + n + 1, (n + 1) % 2, turn[(n + 1) % U][2])
                    pipe.gelu(nc, act, U * i + n, n % 2, m, bias[:, h, 0:FC])
                    if not (at_first and n < 1):
                        copy_y(i, n - 1)

            pipe.copy_x(nc, act, 0, 0, turn[0][2])
            in_turns(act, two_experts)
            copy_y(TURNS - 1, U - 1)

        @block.vector
        def _(dve):
            pipe.dve_credits(dve)

            def take_rows(i, n):
                h, k, m = turn[n % U]
                u = U * i + n
                pipe.take_rows(nc, dve, u, m, tiles_of(outs, (2 * (i + n // U) + h) * ROWS0 + first[k], m))
                if k == NU - 1:
                    dve.wait_ge(pipe.rows_taken.sem, pipe.rows_taken.ready(u))
                    dve.sem_inc(outs_ready.sem, 1)

            def split_weights(i, h):
                e = 2 * i + h
                dve.wait_ge(weights_in[h], 48 * i + 48)
                dve.wait_ge(pipe.down_done.sem, pipe.down_done.free(NU * e + NU - 1))
                nc.vector.tensor_copy(w_high[:, h, :, :], weights[:, h, :, :]).then_inc(w_rounded.sem, 1)
                dve.wait_ge(w_rounded.sem, w_rounded.ready(e))
                nc.vector.tensor_tensor(w_low[:, h, :, :], weights[:, h, :, :], w_high[:, h, :, :].bitcast(F32), ALU.subtract)\
                    .then_inc(weights_split.sem, 1)

            def two_experts(i, at_first=False, at_last=False):
                for n in range(U):
                    if not (at_last and n == U - 1):
                        pipe.split_x(nc, dve, U * i + n + 1, (n + 1) % 2, turn[(n + 1) % U][2])
                    pipe.split_h(nc, dve, U * i + n, n % 2, turn[n][2])
                    if not (at_first and n < 2):
                        take_rows(i, n - 2)
                    if n == 1 and not at_first:
                        split_weights(i, 1)
                    if n == NU + 1 and not at_last:
                        split_weights(i + 1, 0)

            split_weights(0, 0)
            pipe.split_x(nc, dve, 0, 0, turn[0][2])
            split_weights(0, 1)
            in_turns(dve, two_experts)
            take_rows(TURNS - 1, U - 2)
            take_rows(TURNS - 1, U - 1)


def later_constants(nc, s, g, io):
    hawk_vector, hawk_scalar = hawk_constants(nc, s, g)
    fuse_sync, fuse_tensor, fuse_vector = fuse_experts(nc, s, g, io)

    def vector(dve):
        hawk_vector(dve)
        fuse_vector(dve)

    return fuse_sync, fuse_tensor, vector, hawk_scalar


def combine_top2(nc, tag, g, x, yfb, slot, wt, fallback, io):
    PART = 8
    with Scope(nc, tag) as s:
        got = s.sb("got", [P, 2, TILES, D])
        gathered = [s.gather_sem(f"gathered{q}") for q in range(TILES // PART)]
        vdone = s.sem("vdone")
        beside = later_constants(nc, s, g, io) if io else None
        block = s.block()
        if beside:
            sync, tensor, vector, scalar = beside
            block.sync(sync)
            block.tensor(tensor)
            block.scalar(scalar)

        @block.gpsimd
        def _(pool):
            for t in range(TILES):
                for k in range(2):
                    pool.indirect_dma_start(got[:, k, t, :], None, g.y_slots,
                                            bass.IndirectOffsetOnAxis(ap=slot[:, k, t:t + 1], axis=0))\
                        .then_inc(gathered[t // PART], 16)

        @block.vector
        def _(dve):
            if beside:
                vector(dve)
            link = Chain(dve, vdone)
            for q in range(TILES // PART):
                part = slice(q * PART, (q + 1) * PART)
                a, b, f = got[:, 0, part, :], got[:, 1, part, :], yfb[:, part, :]
                link(nc.vector.tensor_tensor(f, f, over(fallback[:, part], D), ALU.mult))
                dve.wait_ge(gathered[q], 16 * 2 * PART)
                nc.vector.tensor_tensor(a, a, over(wt[:, 0, part], D), ALU.mult).then_inc(vdone, 1)
                link.n += 1
                link(nc.vector.tensor_tensor(b, b, over(wt[:, 1, part], D), ALU.mult))
                link(nc.vector.tensor_tensor(a, a, b, ALU.add))
                link(nc.vector.tensor_tensor(a, a, f, ALU.add))
                link(nc.vector.scalar_tensor_tensor(x[:, part, :], a, 0.5, x[:, part, :], ALU.mult, ALU.add))
                for t in range(q * PART, (q + 1) * PART):
                    nc.vector.bn_stats(g.stats[:, t, :], x[:, t, :])



HID = 192
REST = HID - P
SEGS = 3
TAPS = 4
QUARTERS = SEQ // GROUP
BTILES = SEQ // P


def seg(buf, j, i):
    return buf[:, bass.ds(j * SEQ + i * GROUP, GROUP)]


def whole(buf, j):
    return buf[:, j * SEQ:(j + 1) * SEQ]


def btiles(buf, b, i, t=0, n=TPG):
    return buf[:, bass.ds(TPG * i + (BTILES * b + t), n), :]


def bcol(buf, b, i, t):
    return buf[:, bass.ds(TPG * i + (BTILES * b + t), 1)]


def hawk(nc, tag, g, x):
    with Scope(nc, tag) as s:
        mean, r_ln, r_rms = (s.sb(n, [P, TILES]) for n in ("mean", "r_ln", "r_rms"))
        z = s.sb("z", [P, TILES, D])
        row_stats(nc, tag + "s", g.stats, mean, [(r_ln, LN_EPS, True), (r_rms, 0.0, True)])
        with Scope(nc, tag + "w") as s2:
            gate = s2.sb("gate", [P, SEGS * SEQ])
            conv = s2.sb("conv", [P, SEGS * SEQ])
            inp = s2.sb("inp", [P, SEGS * SEQ])
            with Scope(nc, tag + "v") as s3:
                v = s3.sb("v", [P, SEGS, TAPS + SEQ])
                hawk_project(nc, tag + "p", g, x, mean, r_ln, r_rms, z, gate, v, conv)
            with Scope(nc, tag + "f") as s3:
                forget = s3.sb("forget", [P, SEGS * SEQ])
                beta = s3.sb("beta", [P, SEGS * SEQ])
                hawk_recur(nc, tag + "g", g, conv, forget, inp, beta, gate)
            hawk_out(nc, tag + "o", g, gate, z)
        row_stats(nc, tag + "t", g.stats, mean, [(r_rms, 0.0, False)])
        hawk_mlp(nc, tag + "m", g, x, z, r_rms)


def hawk_project(nc, tag, g, x, mean, r_ln, r_rms, z, gate, v, conv):
    w = g.w1
    with Scope(nc, tag) as s:
        zs = s.sb("zs", [P, 2, TPG, D])
        zg = s.sb("zg", [P, 2, GROUP])
        p_x = s.ps("p_x", [P, 2, GROUP])
        p_g = s.ps("p_g", [P, SEGS, GROUP])
        p_v = s.ps("p_v", [P, SEGS, GROUP])
        normalized = s.counter("normalized")
        transposed = s.counter("transposed", 2)
        copied = s.counter("copied", 2)
        gate_done = s.counter("gate_done")
        v_done = s.counter("v_done")
        gate_kept = s.counter("gate_kept", SEGS)
        v_kept = s.counter("v_kept", SEGS)
        first_tap = s.counter("first_tap")
        tapped = s.counter("tapped")
        zeroed = s.sem("zeroed")
        block = s.block()

        def in_turns(eng, before, turn):
            before(0)
            with eng.Fori(0, QUARTERS - 1) as i:
                turn(i, before)
            turn(QUARTERS - 1, None)

        @block.vector
        def _(dve):
            dve.sem_inc(v_kept.sem, SEGS)
            nc.vector.memset(v[:, :, 0:TAPS], 0.0).then_inc(zeroed, 1)
            dve.wait_ge(zeroed, 1)

            def normalize(i):
                for b in range(2):
                    dve.wait_ge(transposed.sem, transposed.free(2 * i + b))
                    for t in range(TPG):
                        last = nc.vector.tensor_scalar(zs[:, b, t:t + 1, :], btiles(x, b, i, t, 1), bcol(mean, b, i, t),
                                                       bcol(r_rms, b, i, t), ALU.subtract, ALU.mult)
                    last.then_inc(normalized.sem, 1)

            def turn(i, then):
                if then is not None:
                    then(i + 1)
                for b in range(2):
                    for t in range(TPG):
                        nc.vector.tensor_scalar(btiles(z, b, i, t, 1), btiles(x, b, i, t, 1), bcol(mean, b, i, t),
                                                bcol(r_ln, b, i, t), ALU.subtract, ALU.mult)
                for j in range(SEGS):
                    dve.wait_ge(v_done.sem, v_done.ready(SEGS * i + j))
                    nc.vector.tensor_copy(v[:, j, bass.ds(GROUP * i + TAPS, GROUP)], p_v[:, j, :]).then_inc(v_kept.sem, 1)
                for k in range(1, TAPS):
                    for j in range(SEGS):
                        if k == 1:
                            dve.wait_ge(first_tap.sem, first_tap.ready(SEGS * i + j))
                        else:
                            dve.wait_ge(tapped.sem, tapped.ready(SEGS * (TAPS - 1) * i + SEGS * (k - 2) + j))
                        col = TAPS * (j // 2) + TAPS - 1 - k
                        nc.vector.scalar_tensor_tensor(seg(conv, j, i), v[:, j, bass.ds(GROUP * i + (TAPS - k), GROUP)],
                                                       w["conv_w"][:, col:col + 1], seg(conv, j, i), ALU.mult, ALU.add)\
                            .then_inc(tapped.sem, 1)

            in_turns(dve, normalize, turn)

        @block.tensor
        def _(pe):
            pe.sem_inc(transposed.sem, 2)

            def transpose(i):
                for b in range(2):
                    pe.wait_ge(normalized.sem, normalized.ready(2 * i + b))
                    pe.wait_ge(copied.sem, copied.free(2 * i + b))
                    for t in range(TPG):
                        last = nc.tensor.transpose(p_x[:, b, t * P:(t + 1) * P], zs[:, b, t, :], g.ident)
                    last.then_inc(transposed.sem, 1)

            def turn(i, then):
                pe.wait_ge(copied.sem, copied.ready(2 * i + 1))
                for bank, kept, done, w_a, w_r in ((p_v, v_kept, v_done, w["in_va"], w["in_vr"]),
                                                   (p_g, gate_kept, gate_done, w["in_ga"], w["in_gr"])):
                    for b in range(2):
                        pe.wait_ge(kept.sem, kept.free(SEGS * i + b))
                        nc.tensor.matmul(bank[:, b, :], w_a, zg[:, b, :], start=True, stop=True).then_inc(done.sem, 1)
                    pe.wait_ge(kept.sem, kept.free(SEGS * i + 2))
                    nc.tensor.matmul(bank[:, 2, :], w_r[:, 0, :], zg[:, 0, :], start=True, stop=False)
                    nc.tensor.matmul(bank[:, 2, :], w_r[:, 1, :], zg[:, 1, :], start=False, stop=True).then_inc(done.sem, 1)
                if then is not None:
                    then(i + 1)

            in_turns(pe, transpose, turn)

        @block.scalar
        def _(act):
            act.sem_inc(copied.sem, 2)
            act.sem_inc(gate_kept.sem, SEGS)

            def copy_x(i):
                for b in range(2):
                    act.wait_ge(transposed.sem, transposed.ready(2 * i + b))
                    nc.scalar.activation(zg[:, b, :], p_x[:, b, :], ACT.Copy).then_inc(copied.sem, 1)

            def turn(i, then):
                for j in range(SEGS):
                    c = j // 2
                    act.wait_ge(v_kept.sem, v_kept.ready(SEGS * i + j))
                    nc.scalar.activation(seg(conv, j, i), v[:, j, bass.ds(GROUP * i + TAPS, GROUP)], ACT.Identity,
                                         bias=w["conv_b"][:, c:c + 1],
                                         scale=w["conv_w"][:, TAPS * c + TAPS - 1:TAPS * c + TAPS]).then_inc(first_tap.sem, 1)
                for j in range(SEGS):
                    act.wait_ge(gate_done.sem, gate_done.ready(SEGS * i + j))
                    nc.scalar.activation(seg(gate, j, i), p_g[:, j, :], ACT.Gelu).then_inc(gate_kept.sem, 1)
                if then is not None:
                    act.wait_ge(gate_done.sem, gate_done.ready(SEGS * i + 2))
                    then(i + 1)

            in_turns(act, copy_x, turn)


def hawk_recur(nc, tag, g, conv, forget, inp, beta, gate):
    w = g.w1
    with Scope(nc, tag) as s:
        carry = s.sb("carry", [P, SEGS])
        p_f = s.ps("p_f", [P, SEGS, GROUP])
        p_i = s.ps("p_i", [P, SEGS, GROUP])
        done = s.counter("done")
        kept = s.counter("kept", 2 * SEGS)
        alpha_done = s.counter("alpha_done")
        squared = s.counter("squared")
        one_minus = s.counter("one_minus")
        beta_done = s.counter("beta_done")
        fed = s.counter("fed")
        scaled = s.counter("scaled")
        scanned = s.counter("scanned")
        carried = s.counter("carried", SEGS)
        passed = s.sem("passed")
        block = s.block()

        def in_turns(eng, first, second):
            first(0)
            with eng.Fori(1, QUARTERS) as i:
                first(i)
                second(i - 1)
            second(QUARTERS - 1)

        def weigh(engine, eng, i):
            for j in range(SEGS):
                eng.wait_ge(scanned.sem, scanned.ready(SEGS * i + j))
                engine.tensor_tensor(seg(gate, j, i), seg(gate, j, i), seg(conv, j, i), ALU.mult)

        @block.tensor
        def _(pe):
            with pe.Fori(0, QUARTERS) as i:
                for n, (bank, aa, ra, ar, rr) in enumerate(((p_f, w["f_aa"], w["f_ra"], w["f_ar"], w["f_rr"]),
                                                            (p_i, w["i_aa"], w["i_ra"], w["i_ar"], w["i_rr"]))):
                    for b in range(2):
                        pe.wait_ge(kept.sem, kept.free(2 * SEGS * i + SEGS * n + b))
                        nc.tensor.matmul(bank[:, b, :], aa, seg(conv, b, i), start=True, stop=False)
                        nc.tensor.matmul(bank[:, b, :], ra[:, b, :], seg(conv, 2, i), start=False, stop=True).then_inc(done.sem, 1)
                    pe.wait_ge(kept.sem, kept.free(2 * SEGS * i + SEGS * n + 2))
                    for b in range(2):
                        nc.tensor.matmul(bank[:, 2, :], ar[:, b, :], seg(conv, b, i), start=(b == 0), stop=False)
                    nc.tensor.matmul(bank[:, 2, :], rr, seg(conv, 2, i), start=False, stop=True).then_inc(done.sem, 1)

        @block.scalar
        def _(act):
            act.sem_inc(kept.sem, 2 * SEGS)

            def gates(i):
                for n, (bank, out) in enumerate(((p_f, forget), (p_i, inp))):
                    for j in range(SEGS):
                        act.wait_ge(done.sem, done.ready(2 * SEGS * i + SEGS * n + j))
                        nc.scalar.activation(seg(out, j, i), bank[:, j, :], ACT.Sigmoid,
                                             bias=w["b_gates"][:, 2 * n + j // 2:2 * n + j // 2 + 1]).then_inc(kept.sem, 1)
                for j in range(SEGS):
                    act.wait_ge(kept.sem, kept.ready(2 * SEGS * i + j))
                    act.sem_inc(passed, 1)
                    nc.scalar.activation(seg(forget, j, i), seg(forget, j, i), ACT.Exp, scale=g.decay[:, j // 2:j // 2 + 1])\
                        .then_inc(alpha_done.sem, 1)

            def roots(i):
                for j in range(SEGS):
                    act.wait_ge(one_minus.sem, one_minus.ready(SEGS * i + j))
                    act.sem_inc(passed, 1)
                    nc.scalar.activation(seg(beta, j, i), seg(beta, j, i), ACT.Sqrt, bias=g.tiny[:, :]).then_inc(beta_done.sem, 1)

            in_turns(act, gates, roots)

        @block.vector
        def _(dve):
            dve.sem_inc(carried.sem, SEGS - 1)
            nc.vector.memset(carry[:, :], 0.0).then_inc(carried.sem, 1)

            def square(i):
                for j in range(SEGS):
                    dve.wait_ge(alpha_done.sem, alpha_done.ready(SEGS * i + j))
                    nc.vector.tensor_tensor(seg(beta, j, i), seg(forget, j, i), seg(forget, j, i), ALU.mult).then_inc(squared.sem, 1)
                for j in range(SEGS):
                    dve.wait_ge(squared.sem, squared.ready(SEGS * i + j))
                    nc.vector.tensor_scalar(seg(beta, j, i), seg(beta, j, i), -1.0, 1.0, ALU.mult, ALU.add).then_inc(one_minus.sem, 1)

            def scan(i):
                for j in range(SEGS):
                    dve.wait_ge(fed.sem, fed.ready(SEGS * i + j))
                    dve.wait_ge(beta_done.sem, beta_done.ready(SEGS * i + j))
                    nc.vector.tensor_tensor(seg(inp, j, i), seg(inp, j, i), seg(beta, j, i), ALU.mult).then_inc(scaled.sem, 1)
                for j in range(SEGS):
                    dve.wait_ge(scaled.sem, scaled.ready(SEGS * i + j))
                    dve.wait_ge(carried.sem, carried.free(SEGS * i + j))
                    nc.vector.tensor_tensor_scan(seg(conv, j, i), seg(forget, j, i), seg(inp, j, i), carry[:, j:j + 1],
                                                 ALU.mult, ALU.add).then_inc(scanned.sem, 1)
                for j in range(SEGS):
                    dve.wait_ge(scanned.sem, scanned.ready(SEGS * i + j))
                    nc.vector.tensor_copy(carry[:, j:j + 1], conv[:, bass.ds(j * SEQ + i * GROUP + GROUP - 1, 1)]).then_inc(carried.sem, 1)

            in_turns(dve, square, scan)
            weigh(nc.vector, dve, QUARTERS - 1)

        @block.gpsimd
        def _(pool):
            def feed(i):
                for j in range(SEGS):
                    pool.wait_ge(kept.sem, kept.ready(2 * SEGS * i + SEGS + j))
                    nc.gpsimd.tensor_tensor(seg(inp, j, i), seg(inp, j, i), seg(conv, j, i), ALU.mult).then_inc(fed.sem, 1)

            feed(0)
            with pool.Fori(1, QUARTERS) as i:
                feed(i)
                weigh(nc.gpsimd, pool, i - 1)


def hawk_out(nc, tag, g, gate, z):
    w = g.w1
    with Scope(nc, tag) as s:
        yt = s.sb("yt", [P, 2, GROUP])
        p_y = s.ps("p_y", [P, 2, GROUP])
        p_r = s.ps("p_r", [P, 2, GROUP])
        projected = s.counter("projected")
        copied = s.counter("copied", 2)
        transposed = s.counter("transposed", 2)
        added = s.counter("added", 2)
        block = s.block()

        @block.tensor
        def _(pe):
            pe.sem_inc(transposed.sem, 2)

            def project(i, b):
                pe.wait_ge(copied.sem, copied.free(2 * i + b))
                nc.tensor.matmul(p_y[:, b, :], w["out_a"], seg(gate, b, i), start=True, stop=False)
                nc.tensor.matmul(p_y[:, b, :], w["out_r"][:, b, :], seg(gate, 2, i), start=False, stop=True)\
                    .then_inc(projected.sem, 1)

            def transpose(i, b):
                pe.wait_ge(copied.sem, copied.ready(2 * i + b))
                pe.wait_ge(added.sem, added.free(2 * i + b))
                for t in range(TPG):
                    last = nc.tensor.transpose(p_r[:, b, t * P:(t + 1) * P], yt[:, b, t * P:(t + 1) * P], g.ident)
                last.then_inc(transposed.sem, 1)

            a_group_behind(pe, project, transpose)

        @block.scalar
        def _(act):
            act.sem_inc(copied.sem, 2)
            with act.Fori(0, QUARTERS) as i:
                for b in range(2):
                    act.wait_ge(projected.sem, projected.ready(2 * i + b))
                    act.wait_ge(transposed.sem, transposed.free(2 * i + b))
                    nc.scalar.activation(yt[:, b, :], p_y[:, b, :], ACT.Copy).then_inc(copied.sem, 1)

        @block.vector
        def _(dve):
            dve.sem_inc(added.sem, 2)
            with dve.Fori(0, QUARTERS) as i:
                for b in range(2):
                    dve.wait_ge(transposed.sem, transposed.ready(2 * i + b))
                    nc.vector.tensor_tensor(btiles(z, b, i), p_r[:, b, :].rearrange("p (t d) -> p t d", d=D), btiles(z, b, i),
                                            ALU.add).then_inc(added.sem, 1)
                for b in range(2):
                    dve.wait_ge(added.sem, added.ready(2 * i + b))
                    for t in range(TPG):
                        nc.vector.bn_stats(btiles(g.stats, b, i, t, 1), btiles(z, b, i, t, 1))


def hawk_mlp(nc, tag, g, x, z, r_rms):
    w = g.w1
    GC = 2
    with Scope(nc, tag) as s:
        zs = s.sb("zs", [P, 2, TPG, D])
        zg = s.sb("zg", [P, 2, GROUP])
        hid = s.sb("hid", [P, 2, GC, GROUP])
        yt = s.sb("yt", [P, 2, GROUP])
        p_x = s.ps("p_x", [P, 2, GROUP])
        p_g = s.ps("p_g", [P, GC, GROUP])
        p_v = s.ps("p_v", [P, GC, GROUP])
        p_y = s.ps("p_y", [P, GROUP])
        p_r = s.ps("p_r", [P, GROUP])
        normalized = s.counter("normalized")
        transposed = s.counter("transposed", 2)
        copied = s.counter("copied", 2)
        gate_done = s.counter("gate_done")
        value_done = s.counter("value_done", 2 * GC)
        gelu_done = s.counter("gelu_done", GC)
        product_done = s.counter("product_done", GC)
        shrunk = s.counter("shrunk", 2)
        y_copied = s.counter("y_copied", 1)
        y_transposed = s.counter("y_transposed", 2)
        added = s.counter("added", 1)
        x_done = s.counter("x_done")
        block = s.block()

        def in_turns(eng, turn):
            turn(0, at_first=True)
            with eng.Fori(1, QUARTERS - 1) as i:
                turn(i)
            turn(QUARTERS - 1, at_last=True)

        def before(i, b):
            return (i, 0) if b else (i - 1, 1)

        def behind(i, b):
            return (i + 1, 0) if b else (i, 1)

        @block.vector
        def _(dve):
            dve.sem_inc(product_done.sem, GC)
            dve.sem_inc(added.sem, 1)

            def normalize(i, b):
                dve.wait_ge(transposed.sem, transposed.free(2 * i + b))
                for t in range(TPG):
                    last = nc.vector.tensor_scalar(zs[:, b, t:t + 1, :], btiles(z, b, i, t, 1), bcol(r_rms, b, i, t),
                                                   None, ALU.mult)
                last.then_inc(normalized.sem, 1)

            def multiply(i, b):
                for c in range(GC):
                    k = GC * (2 * i + b) + c
                    dve.wait_ge(value_done.sem, value_done.ready(k))
                    dve.wait_ge(gelu_done.sem, gelu_done.ready(k))
                    nc.vector.tensor_tensor(hid[:, b, c, :], hid[:, b, c, :], p_v[:, c, :], ALU.mult)\
                        .then_inc(product_done.sem, 1)

            def add(i, b):
                u = 2 * i + b
                dve.wait_ge(y_transposed.sem, y_transposed.ready(u))
                nc.vector.tensor_tensor(btiles(z, b, i), p_r[:, :].rearrange("p (t d) -> p t d", d=D), btiles(z, b, i),
                                        ALU.add).then_inc(added.sem, 1)
                dve.wait_ge(added.sem, added.ready(u))
                nc.vector.tensor_tensor(btiles(x, b, i), btiles(x, b, i), btiles(z, b, i), ALU.add).then_inc(x_done.sem, 1)
                dve.wait_ge(x_done.sem, x_done.ready(u))
                for t in range(TPG):
                    nc.vector.bn_stats(btiles(g.stats, b, i, t, 1), btiles(x, b, i, t, 1))

            def turn(i, at_first=False, at_last=False):
                for b in range(2):
                    multiply(i, b)
                    if not at_last:
                        normalize(i + 1, b)
                    if not at_first:
                        add(i - 1, b)

            for b in range(2):
                normalize(0, b)
            in_turns(dve, turn)
            for b in range(2):
                add(QUARTERS - 1, b)

        @block.tensor
        def _(pe):
            pe.sem_inc(transposed.sem, 2)
            pe.sem_inc(value_done.sem, 2 * GC)
            pe.sem_inc(shrunk.sem, 2)
            pe.sem_inc(y_transposed.sem, 2)

            def transpose(i, b):
                pe.wait_ge(normalized.sem, normalized.ready(2 * i + b))
                pe.wait_ge(copied.sem, copied.free(2 * i + b))
                for t in range(TPG):
                    last = nc.tensor.transpose(p_x[:, b, t * P:(t + 1) * P], zs[:, b, t, :], g.ident)
                last.then_inc(transposed.sem, 1)

            def grow(i, b):
                pe.wait_ge(copied.sem, copied.ready(2 * i + b))
                for c in range(GC):
                    k = GC * (2 * i + b) + c
                    pe.wait_ge(gelu_done.sem, gelu_done.free(k))
                    nc.tensor.matmul(p_g[:, c, :], w["grow"][:, c * P:(c + 1) * P], zg[:, b, :], start=True, stop=True)\
                        .then_inc(gate_done.sem, 1)
                    pe.wait_ge(product_done.sem, product_done.free(k))
                    nc.tensor.matmul(p_v[:, c, :], w["grow"][:, (GC + c) * P:(GC + c + 1) * P], zg[:, b, :],
                                     start=True, stop=True).then_inc(value_done.sem, 1)

            def shrink(i, b):
                pe.wait_ge(product_done.sem, product_done.ready(GC * (2 * i + b) + GC - 1))
                pe.wait_ge(y_copied.sem, y_copied.free(2 * i + b))
                for c in range(GC):
                    last = nc.tensor.matmul(p_y[:, :], w["shrink"][:, c, :], hid[:, b, c, :], start=(c == 0), stop=(c == GC - 1))
                last.then_inc(shrunk.sem, 1)

            def transpose_back(i, b):
                pe.wait_ge(y_copied.sem, y_copied.ready(2 * i + b))
                pe.wait_ge(added.sem, added.free(2 * i + b))
                for t in range(TPG):
                    last = nc.tensor.transpose(p_r[:, t * P:(t + 1) * P], yt[:, b, t * P:(t + 1) * P], g.ident)
                last.then_inc(y_transposed.sem, 1)

            def turn(i, at_first=False, at_last=False):
                for b in range(2):
                    if not (at_last and b == 1):
                        transpose(*behind(i, b))
                    grow(i, b)
                    if not (at_first and b == 0):
                        shrink(*before(i, b))
                    if not at_first:
                        transpose_back(i - 1, b)

            transpose(0, 0)
            in_turns(pe, turn)
            shrink(QUARTERS - 1, 1)
            for b in range(2):
                transpose_back(QUARTERS - 1, b)

        @block.scalar
        def _(act):
            act.sem_inc(copied.sem, 2)
            act.sem_inc(gelu_done.sem, GC)
            act.sem_inc(y_copied.sem, 1)

            def copy_x(i, b):
                act.wait_ge(transposed.sem, transposed.ready(2 * i + b))
                act.wait_ge(value_done.sem, value_done.free(GC * (2 * i + b) + GC - 1))
                nc.scalar.activation(zg[:, b, :], p_x[:, b, :], ACT.Copy).then_inc(copied.sem, 1)

            def gelu(i, b):
                act.wait_ge(shrunk.sem, shrunk.free(2 * i + b))
                for c in range(GC):
                    act.wait_ge(gate_done.sem, gate_done.ready(GC * (2 * i + b) + c))
                    nc.scalar.activation(hid[:, b, c, :], p_g[:, c, :], ACT.Gelu).then_inc(gelu_done.sem, 1)

            def copy_y(i, b):
                act.wait_ge(shrunk.sem, shrunk.ready(2 * i + b))
                act.wait_ge(y_transposed.sem, y_transposed.free(2 * i + b))
                nc.scalar.activation(yt[:, b, :], p_y[:, :], ACT.Copy).then_inc(y_copied.sem, 1)

            def turn(i, at_first=False, at_last=False):
                for b in range(2):
                    if not (at_last and b == 1):
                        copy_x(*behind(i, b))
                    gelu(i, b)
                    if not (at_first and b == 0):
                        copy_y(*before(i, b))

            copy_x(0, 0)
            in_turns(act, turn)
            copy_y(QUARTERS - 1, 1)


def hawk_constants(nc, s, g):
    w = g.w1
    a, e, d, y, y2, acc = (s.sb(n, [P, 2]) for n in ("a", "e", "d", "y", "y2", "acc"))
    cdone, negated, exps = s.sem("cdone"), s.sem("negated"), s.sem("exps")

    def scalar(act):
        act.wait_ge(negated, 1)
        nc.scalar.activation(e[:, :], a[:, :], ACT.Exp).then_inc(exps, 1)

    def vector(dve):
        link = Chain(dve, cdone)
        dve.wait_ge(g.pack_in[1], 16)
        for m in (w["in_all"], w["grow"]):
            link(nc.vector.tensor_scalar(m, m, w["gamma1"] if m is w["in_all"] else w["gamma2"], None, ALU.mult))
        link(nc.vector.memset(g.tiny[:, :], 1e-6))
        link(nc.vector.tensor_scalar(d[:, :], w["forget_base"], -1.0, None, ALU.mult))
        nc.vector.tensor_tensor(a[:, :], w["forget_base"], d[:, :], ALU.min).then_inc(negated, 1)
        dve.wait_ge(exps, 1)
        link(nc.vector.tensor_scalar(d[:, :], e[:, :], 2.0, None, ALU.add))
        link(nc.vector.reciprocal(d[:, :], d[:, :]))
        link(nc.vector.tensor_tensor(y[:, :], e[:, :], d[:, :], ALU.mult))
        link(nc.vector.tensor_tensor(y2[:, :], y[:, :], y[:, :], ALU.mult))
        link(nc.vector.memset(acc[:, :], 1.0 / 17))
        for k in range(15, 0, -2):
            link(nc.vector.tensor_tensor(acc[:, :], acc[:, :], y2[:, :], ALU.mult))
            link(nc.vector.tensor_scalar(acc[:, :], acc[:, :], 1.0 / k, None, ALU.add))
        link(nc.vector.tensor_tensor(acc[:, :], acc[:, :], y[:, :], ALU.mult))
        link(nc.vector.tensor_scalar(d[:, :], w["forget_base"], 0.0, None, ALU.max))
        link(nc.vector.scalar_tensor_tensor(acc[:, :], acc[:, :], 2.0, d[:, :], ALU.mult, ALU.add))
        link(nc.vector.tensor_scalar(g.decay[:, :], acc[:, :], -8.0, None, ALU.mult))

    return vector, scalar



HEADS, HD = 4, 32
SC = 2 * 2 * HEADS


def fuse_experts(nc, s, g, io):
    w = g.w2
    w1t = s.sb("w1t", [P, E * FC, D])
    w2 = s.sb("w2", [P, E * FC, D])
    b12t = s.sb("b12t", [P, TPG, 32])
    p_w = s.ps("p_w", [P, E, D])
    p_b = s.ps("p_b", [P, E])
    p_t = s.ps("p_t", [P, P])
    w1_in, w2_in, emptied, fused, copied, turned = (
        s.sem(n) for n in ("w1_in", "w2_in", "emptied", "fused", "copied", "turned"))

    def sync(sp):
        sp.dma_start(w1t[:, :, :], io["w1t_top1"].rearrange("p (n d) -> p n d", d=D)).then_inc(w1_in, 16)
        sp.dma_start(w2[:, :, :], io["w2_top1"].rearrange("p (n d) -> p n d", d=D)).then_inc(w2_in, 16)

    def tensor(pe):
        pe.wait_ge(g.pack_in[2], 16)
        pe.wait_ge(w1_in, 16)
        pe.wait_ge(w2_in, 16)
        for e in range(E):
            for c in range(FC):
                nc.tensor.matmul(p_b[:, e:e + 1], w2[:, e * FC + c, :], w["b1"][:, e * FC + c:e * FC + c + 1],
                                 start=(c == 0), stop=(c == FC - 1))
        for e in range(E):
            for c in range(FC):
                last = nc.tensor.matmul(p_w[:, e, :], w1t[:, e * FC + c, :], w2[:, e * FC + c, :],
                                        start=(c == 0), stop=(c == FC - 1))
        last.then_inc(fused, 1)
        pe.wait_ge(copied, 1)
        nc.tensor.transpose(p_t[:, :], b12t[:, :, :].rearrange("p t e -> p (t e)"), g.ident).then_inc(turned, 1)

    def vector(dve):
        link = Chain(dve, emptied)
        link(nc.vector.memset(g.b12[:, :, :], 0.0))
        link(nc.vector.memset(b12t[:, :, :], 0.0))
        dve.wait_ge(fused, 1)
        for t in range(TPG):
            last = nc.vector.tensor_tensor(b12t[:, t, 0:E], p_b[:, :], w["b2"], ALU.add)
        last.then_inc(copied, 1)
        link(nc.vector.tensor_copy(g.w12_high[:, :, :], p_w[:, :, :]))
        nc.vector.tensor_tensor(g.w12_low[:, :, :], p_w[:, :, :], g.w12_high[:, :, :].bitcast(F32), ALU.subtract)
        dve.wait_ge(turned, 1)
        for t in range(TPG):
            nc.vector.tensor_copy(g.b12[t * 32:(t + 1) * 32, t, :], p_t[t * 32:(t + 1) * 32, :])

    return sync, tensor, vector


def pair_moe(nc, tag, g, x, take_stats, out=None):
    with Scope(nc, tag) as s:
        mean, rstd = s.sb("mean", [P, TILES]), s.sb("rstd", [P, TILES])
        z = s.sb("z", [P, TILES, D])
        row_stats(nc, tag + "s", g.stats, mean, [(rstd, LN_EPS, True)], x if take_stats else None)
        with Scope(nc, tag + "A") as s2:
            v = s2.sb("v", [P, BTILES, 2, D])
            scores = s2.sb("scores", [P, BTILES, SC])
            pair_scores(nc, tag + "q", g, x, mean, rstd, z, v, scores)
            pair_softmax(nc, tag + "m", g, scores)
            pair_attend(nc, tag + "a", g, scores, v, z)
        row_stats(nc, tag + "t", g.stats, mean, [(rstd, LN_EPS, True)], z)
        with Scope(nc, tag + "B") as s2:
            yt = s2.sb("yt", [P, TOK])
            logits = s2.sb("logits", [P, TILES, E])
            wt = s2.sb("wt", [P, TILES, 32])
            wtt = s2.sb("wtt", [P, GROUPS, P])
            top1_logits(nc, tag + "g", g, z, mean, rstd, yt, logits)
            route_top1(nc, tag + "r", g, logits, wt, wtt)
            experts_top1(nc, tag + "e", g, yt, wt, wtt, z)
        row_stats(nc, tag + "u", g.stats, mean, [(rstd, LN_EPS, True)], z)
        add_normed(nc, tag + "f", g, z, mean, rstd, x, out)


def pair_scores(nc, tag, g, x, mean, rstd, z, v, scores):
    w = g.w2
    with Scope(nc, tag) as s:
        zs = s.sb("zs", [P, 2, TPG, D])
        zg = s.sb("zg", [P, 2, GROUP])
        qk = s.sb("qk", [P, 2, 2, 2 * D])
        prod = s.sb("prod", [P, 2, 2, 2, D])
        p_x = s.ps("p_x", [P, 2, GROUP])
        p_q = s.ps("p_q", [P, 2, 2, GROUP])
        normalized = s.counter("normalized")
        z_kept = s.counter("z_kept", 2)
        transposed = s.counter("transposed", 2)
        copied = s.counter("copied", 2)
        projected = s.counter("projected", TPG)
        biased = s.counter("biased")
        values_kept = s.counter("values_kept", 2)
        multiplied = s.counter("multiplied", 2)
        reduced = s.counter("reduced", 2)
        block = s.block()

        @block.vector
        def _(dve):
            dve.sem_inc(multiplied.sem, 2)
            dve.sem_inc(reduced.sem, 2)

            def normalize(i):
                for b in range(2):
                    dve.wait_ge(transposed.sem, transposed.free(2 * i + b))
                    dve.wait_ge(z_kept.sem, z_kept.free(2 * i + b))
                    for t in range(TPG):
                        last = nc.vector.tensor_scalar(zs[:, b, t:t + 1, :], btiles(x, b, i, t, 1), bcol(mean, b, i, t),
                                                       bcol(rstd, b, i, t), ALU.subtract, ALU.mult)
                    last.then_inc(normalized.sem, 1)

            def score(i):
                for two in range(0, TPG, 2):
                    for h in range(2):
                        k = TPG * i + two + h
                        dve.wait_ge(projected.sem, projected.ready(k))
                        dve.wait_ge(multiplied.sem, multiplied.free(k))
                        nc.vector.tensor_tensor(qk[:, h, :, :], p_q[:, h, :, 0:2 * D],
                                                w["qkv_b"][:, 0:2 * D].unsqueeze(1).to_broadcast([P, 2, 2 * D]), ALU.add)\
                            .then_inc(biased.sem, 1)
                    for h in range(2):
                        k = TPG * i + two + h
                        dve.wait_ge(biased.sem, biased.ready(k))
                        dve.wait_ge(reduced.sem, reduced.free(k))
                        nc.vector.tensor_tensor(prod[:, h, :, :, :], qk[:, h, :, 0:D].unsqueeze(2).to_broadcast([P, 2, 2, D]),
                                                qk[:, h, :, D:2 * D].unsqueeze(1).to_broadcast([P, 2, 2, D]), ALU.mult)\
                            .then_inc(multiplied.sem, 1)
                    for h in range(2):
                        k = TPG * i + two + h
                        dve.wait_ge(multiplied.sem, multiplied.ready(k))
                        nc.vector.tensor_reduce(scores[:, bass.ds(k, 1), :],
                                                prod[:, h, :, :, :].rearrange("p l m (h c) -> p (l m h) c", c=HD), AX, ALU.add)\
                            .then_inc(reduced.sem, 1)

            normalize(0)
            with dve.Fori(0, QUARTERS - 1) as i:
                normalize(i + 1)
                score(i)
            score(QUARTERS - 1)

        @block.gpsimd
        def _(pool):
            pool.sem_inc(z_kept.sem, 2)
            with pool.Fori(0, QUARTERS) as i:
                for b in range(2):
                    pool.wait_ge(normalized.sem, normalized.ready(2 * i + b))
                    nc.gpsimd.tensor_tensor(btiles(z, b, i), zs[:, b, :, :],
                                            w["out_b"].unsqueeze(1).to_broadcast([P, TPG, D]), ALU.add).then_inc(z_kept.sem, 1)
                for t in range(TPG):
                    k = TPG * i + t
                    pool.wait_ge(values_kept.sem, values_kept.ready(k))
                    vk = v[:, bass.ds(k, 1), :, :].rearrange("p a m d -> p (a m) d")
                    nc.gpsimd.tensor_tensor(vk, vk, w["qkv_b"][:, 2 * D:3 * D].unsqueeze(1).to_broadcast([P, 2, D]), ALU.add)

        @block.tensor
        def _(pe):
            pe.sem_inc(transposed.sem, 2)
            pe.sem_inc(projected.sem, TPG)

            def transpose(i):
                for b in range(2):
                    pe.wait_ge(normalized.sem, normalized.ready(2 * i + b))
                    pe.wait_ge(copied.sem, copied.free(2 * i + b))
                    for t in range(TPG):
                        last = nc.tensor.transpose(p_x[:, b, t * P:(t + 1) * P], zs[:, b, t, :], g.ident)
                    last.then_inc(transposed.sem, 1)

            def project(i):
                pe.wait_ge(copied.sem, copied.ready(2 * i + 1))
                for t in range(TPG):
                    pe.wait_ge(values_kept.sem, values_kept.free(TPG * i + t))
                    for b in range(2):
                        last = nc.tensor.matmul(p_q[:, t % 2, b, 0:3 * D], zg[:, b, t * P:(t + 1) * P], w["qkv"],
                                                start=True, stop=True)
                    last.then_inc(projected.sem, 1)

            transpose(0)
            with pe.Fori(0, QUARTERS - 1) as i:
                project(i)
                transpose(i + 1)
            project(QUARTERS - 1)

        @block.scalar
        def _(act):
            act.sem_inc(copied.sem, 2)
            act.sem_inc(values_kept.sem, 2)

            def copy_x(i):
                act.wait_ge(projected.sem, projected.free(TPG * i + TPG - 1))
                for b in range(2):
                    act.wait_ge(transposed.sem, transposed.ready(2 * i + b))
                    nc.scalar.activation(zg[:, b, :], p_x[:, b, :], ACT.Copy).then_inc(copied.sem, 1)

            def keep_values(i, tiles):
                for t in tiles:
                    k = TPG * i + t
                    act.wait_ge(biased.sem, biased.ready(k))
                    nc.scalar.activation(v[:, bass.ds(k, 1), :, :].rearrange("p a m d -> p (a m) d"), p_q[:, t % 2, :, 2 * D:3 * D],
                                         ACT.Copy).then_inc(values_kept.sem, 1)

            copy_x(0)
            with act.Fori(0, QUARTERS - 1) as i:
                keep_values(i, (0, 1))
                copy_x(i + 1)
                keep_values(i, (2, 3))
            keep_values(QUARTERS - 1, range(TPG))


def pair_softmax(nc, tag, g, scores):
    with Scope(nc, tag) as s:
        most = s.sb("most", [P, BTILES * 2, HEADS])
        shifted, exps, vdone = s.sem("shifted"), s.sem("exps"), s.sem("vdone")
        block = s.block()
        by = scores[:, :, :].rearrange("p a (l m h) -> p (a l) m h", l=2, m=2)
        wide = most[:, :, :].unsqueeze(2).to_broadcast([P, BTILES * 2, 2, HEADS])

        @block.scalar
        def _(act):
            act.wait_ge(shifted, 1)
            nc.scalar.activation(scores[:, :, :], scores[:, :, :], ACT.Exp, scale=float(1 / np.float32(np.sqrt(HD))))\
                .then_inc(exps, 1)

        @block.vector
        def _(dve):
            link = Chain(dve, vdone)
            link(nc.vector.tensor_tensor(most[:, :, :], by[:, :, 0, :], by[:, :, 1, :], ALU.max))
            nc.vector.tensor_tensor(by, by, wide, ALU.subtract).then_inc(shifted, 1)
            dve.wait_ge(exps, 1)
            link(nc.vector.tensor_tensor(most[:, :, :], by[:, :, 0, :], by[:, :, 1, :], ALU.add))
            link(nc.vector.reciprocal(most[:, :, :], most[:, :, :]))
            link(nc.vector.tensor_tensor(by, by, wide, ALU.mult))


def pair_attend(nc, tag, g, scores, v, z):
    w = g.w2
    with Scope(nc, tag) as s:
        prod = s.sb("prod", [P, 2, 2, 2, D])
        o = s.sb("o", [P, TPG, 2, D])
        og = s.sb("og", [P, 2, GROUP])
        p_x = s.ps("p_x", [P, 2, GROUP])
        p_r = s.ps("p_r", [P, 2, GROUP])
        multiplied = s.counter("multiplied")
        summed = s.counter("summed", 2)
        transposed = s.counter("transposed", 1)
        copied = s.counter("copied", 2)
        projected = s.counter("projected", 2)
        added = s.counter("added", 2)
        block = s.block()

        @block.vector
        def _(dve):
            dve.sem_inc(added.sem, 2)
            dve.sem_inc(summed.sem, 2)

            def attend(i):
                dve.wait_ge(transposed.sem, transposed.free(i))
                for two in range(0, TPG, 2):
                    for h in range(2):
                        k = TPG * i + two + h
                        dve.wait_ge(summed.sem, summed.free(k))
                        nc.vector.tensor_tensor(prod[:, h, :, :, :].rearrange("p l m (h c) -> p l (m h) c", c=HD),
                                                scores[:, bass.ds(k, 1), :].rearrange("p a (l n) -> p (a l) n", l=2)
                                                .unsqueeze(3).to_broadcast([P, 2, 2 * HEADS, HD]),
                                                v[:, bass.ds(k, 1), :, :].rearrange("p a m (h c) -> p a (m h) c", c=HD)
                                                .to_broadcast([P, 2, 2 * HEADS, HD]), ALU.mult).then_inc(multiplied.sem, 1)
                    for h in range(2):
                        k = TPG * i + two + h
                        dve.wait_ge(multiplied.sem, multiplied.ready(k))
                        nc.vector.tensor_tensor(o[:, two + h, :, :], prod[:, h, :, 0, :], prod[:, h, :, 1, :], ALU.add)\
                            .then_inc(summed.sem, 1)

            def add(i):
                for b in range(2):
                    dve.wait_ge(projected.sem, projected.ready(2 * i + b))
                    nc.vector.tensor_tensor(btiles(z, b, i), p_r[:, b, :].rearrange("p (t d) -> p t d", d=D), btiles(z, b, i),
                                            ALU.add).then_inc(added.sem, 1)

            attend(0)
            with dve.Fori(1, QUARTERS) as i:
                attend(i)
                add(i - 1)
            add(QUARTERS - 1)

        @block.tensor
        def _(pe):
            pe.sem_inc(transposed.sem, 1)
            pe.sem_inc(projected.sem, 2)
            with pe.Fori(0, QUARTERS) as i:
                for b in range(2):
                    pe.wait_ge(copied.sem, copied.free(2 * i + b))
                for t in range(TPG):
                    pe.wait_ge(summed.sem, summed.ready(TPG * i + t))
                    for b in range(2):
                        last = nc.tensor.transpose(p_x[:, b, t * P:(t + 1) * P], o[:, t, b, :], g.ident)
                last.then_inc(transposed.sem, 1)
                for b in range(2):
                    pe.wait_ge(copied.sem, copied.ready(2 * i + b))
                    pe.wait_ge(added.sem, added.free(2 * i + b))
                    for t in range(TPG):
                        last = nc.tensor.matmul(p_r[:, b, t * P:(t + 1) * P], og[:, b, t * P:(t + 1) * P], w["out"],
                                                start=True, stop=True)
                    last.then_inc(projected.sem, 1)

        @block.scalar
        def _(act):
            act.sem_inc(copied.sem, 2)
            with act.Fori(0, QUARTERS) as i:
                for b in range(2):
                    act.wait_ge(transposed.sem, transposed.ready(i))
                    act.wait_ge(projected.sem, projected.free(2 * i + b))
                    nc.scalar.activation(og[:, b, :], p_x[:, b, :], ACT.Copy).then_inc(copied.sem, 1)


def top1_logits(nc, tag, g, z, mean, rstd, yt, logits):
    w = g.w2
    with Scope(nc, tag) as s:
        ys = s.sb("ys", [P, 2, TPG, D])
        yg = s.sb("yg", [P, 2, GROUP])
        p_x = s.ps("p_x", [P, 2, GROUP])
        p_l = s.ps("p_l", [P, 2, GROUP])
        centred = s.counter("centred")
        scaled = s.counter("scaled")
        normalized = s.counter("normalized")
        kept = s.counter("kept", 2)
        transposed = s.counter("transposed", 2)
        copied = s.counter("copied")
        yt_kept = s.counter("yt_kept", 2)
        routed = s.counter("routed", 2)
        logits_kept = s.counter("logits_kept", 2)
        block = s.block()
        wide = lambda r: r.unsqueeze(1).to_broadcast([P, TPG, D])

        @block.vector
        def _(dve):
            dve.sem_inc(logits_kept.sem, 2)

            def normalize(i, b):
                u = 2 * i + b
                dve.wait_ge(transposed.sem, transposed.free(u))
                dve.wait_ge(kept.sem, kept.free(u))
                for t in range(TPG):
                    last = nc.vector.tensor_scalar(ys[:, b, t:t + 1, :], btiles(z, b, i, t, 1), bcol(mean, b, i, t),
                                                   bcol(rstd, b, i, t), ALU.subtract, ALU.mult)
                last.then_inc(centred.sem, 1)
                dve.wait_ge(centred.sem, centred.ready(u))
                nc.vector.tensor_tensor(ys[:, b, :, :], ys[:, b, :, :], wide(w["ln1_g"]), ALU.mult).then_inc(scaled.sem, 1)
                dve.wait_ge(scaled.sem, scaled.ready(u))
                nc.vector.tensor_tensor(ys[:, b, :, :], ys[:, b, :, :], wide(w["ln1_b"]), ALU.add).then_inc(normalized.sem, 1)

            def keep(i, b):
                u = 2 * i + b
                dve.wait_ge(routed.sem, routed.ready(u))
                nc.vector.tensor_copy(btiles(logits, b, i), p_l[:, b, 0:TPG * E].rearrange("p (t e) -> p t e", e=E))\
                    .then_inc(logits_kept.sem, 1)

            a_pair_behind(dve, normalize, keep)

        @block.gpsimd
        def _(pool):
            pool.sem_inc(kept.sem, 2)
            with pool.Fori(0, QUARTERS) as i:
                for b in range(2):
                    pool.wait_ge(normalized.sem, normalized.ready(2 * i + b))
                    nc.gpsimd.tensor_copy(btiles(z, b, i), ys[:, b, :, :]).then_inc(kept.sem, 1)

        @block.tensor
        def _(pe):
            pe.sem_inc(transposed.sem, 2)
            pe.sem_inc(routed.sem, 2)

            def transpose(i, b):
                pe.wait_ge(normalized.sem, normalized.ready(2 * i + b))
                pe.wait_ge(yt_kept.sem, yt_kept.free(2 * i + b))
                for t in range(TPG):
                    last = nc.tensor.transpose(p_x[:, b, t * P:(t + 1) * P], ys[:, b, t, :], g.ident)
                last.then_inc(transposed.sem, 1)

            def route(i, b):
                pe.wait_ge(copied.sem, copied.ready(2 * i + b))
                pe.wait_ge(logits_kept.sem, logits_kept.free(2 * i + b))
                for t in range(TPG):
                    last = nc.tensor.matmul(p_l[:, b, t * E:(t + 1) * E], yg[:, b, t * P:(t + 1) * P], w["wg"],
                                            start=True, stop=True)
                last.then_inc(routed.sem, 1)

            a_group_behind(pe, transpose, route)

        @block.scalar
        def _(act):
            act.sem_inc(yt_kept.sem, 2)
            with act.Fori(0, QUARTERS) as i:
                for b in range(2):
                    act.wait_ge(transposed.sem, transposed.ready(2 * i + b))
                    act.wait_ge(routed.sem, routed.free(2 * i + b))
                    nc.scalar.activation(yg[:, b, :], p_x[:, b, :], ACT.Copy).then_inc(copied.sem, 1)
                    nc.scalar.activation(yt[:, bass.ds(GROUP * i + SEQ * b, GROUP)], p_x[:, b, :], ACT.Copy).then_inc(yt_kept.sem, 1)


def route_top1(nc, tag, g, logits, wt, wtt):
    with Scope(nc, tag) as s:
        probs = s.sb("probs", [P, TILES, E])
        top = s.sb("top", [P, TILES])
        code = s.sb("code", [P, TILES, E])
        best = s.sb("best", [P, TILES])
        hot = s.sb("hot", [P, TILES, E])
        mask = s.sb("mask", [P, E, TILES], BF16)
        before = s.sb("before", [P, E, TILES])
        p_c = s.ps("p_c", [P, 2, GROUP])
        p_t = s.ps("p_t", [P, GROUPS, P])
        vdone, masked, counted, weighted, transposed = (
            s.sem(n) for n in ("vdone", "masked", "counted", "weighted", "transposed"))
        soft_v, soft_a = probabilities(nc, tag, s, logits, probs, top[:, :])
        block = s.block()
        N = E * TILES
        view = lambda ap: ap.rearrange("p (e t) -> p e t", e=E)

        @block.scalar
        def _(act):
            soft_a(act)

        @block.tensor
        def _(pe):
            pe.wait_ge(masked, 1)
            flat = mask[:, :, :].rearrange("p e t -> p (e t)")
            nc.tensor.matmul(p_c[:, 0, 0:N], g.upto[:, :], flat, start=True, stop=True)
            nc.tensor.matmul(p_c[:, 1, 0:N], g.ones[:, :], flat, start=True, stop=True).then_inc(counted, 1)
            pe.wait_ge(weighted, 1)
            for q in range(GROUPS):
                last = nc.tensor.transpose(p_t[:, q, :], wt[:, q * TPG:(q + 1) * TPG, :].rearrange("p t e -> p (t e)"), g.ident)
            last.then_inc(transposed, 1)

        @block.vector
        def _(dve):
            link = Chain(dve, vdone)
            soft_v(link)
            first_largest(nc, link, probs[:, :, :], top[:, :], g.rank, code, best, hot[:, :, :])
            link(nc.vector.memset(wt[:, :, :], 0.0))
            nc.vector.tensor_copy(mask[:, :, :].rearrange("p e t -> p t e"), hot[:, :, :]).then_inc(masked, 1)
            dve.wait_ge(counted, 1)
            link(nc.vector.tensor_tensor_scan(before[:, :, :].rearrange("p e t -> p (e t)"), g.carry[:, :], p_c[:, 1, 0:N],
                                              0.0, ALU.mult, ALU.add))
            link(nc.vector.tensor_tensor(before[:, :, :], before[:, :, :], view(p_c[:, 1, 0:N]), ALU.subtract))
            link(nc.vector.tensor_tensor(before[:, :, :], view(p_c[:, 0, 0:N]), before[:, :, :], ALU.add))
            link(nc.vector.tensor_scalar(before[:, :, :], before[:, :, :], float(CAP1), None, ALU.is_le))
            link(nc.vector.tensor_tensor(hot[:, :, :], hot[:, :, :], before[:, :, :].rearrange("p e t -> p t e"), ALU.mult))
            nc.vector.tensor_tensor(wt[:, :, 0:E], hot[:, :, :], over(top[:, :], E), ALU.mult).then_inc(weighted, 1)
            dve.wait_ge(transposed, 1)
            nc.vector.tensor_copy(wtt[:, :, :], p_t[:, :, :])


def experts_top1(nc, tag, g, yt, wt, wtt, z):
    H = E // 2
    with Scope(nc, tag) as s:
        y_high, y_low = (s.sb(n, [P, 2, GROUP], F32R) for n in ("y_high", "y_low"))
        wg = s.sb("wg", [P, 2, P])
        gates = s.sb("gates", [P, 2, TPG, E])
        terms = s.sb("terms", [P, 2, TPG, E, D])
        base = s.sb("base", [P, 2, TPG, D])
        p_b = s.ps("p_b", [P, 2, GROUP])
        p_e = s.ps("p_e", [P, 2, E, D])
        gates_in = s.counter("gates_in")
        copied = s.counter("copied")
        split = s.counter("split")
        biases = s.counter("biases")
        products = s.counter("products", TPG)
        started = s.counter("started", 2)
        low_scaled = s.counter("low_scaled", 2)
        high_scaled = s.counter("high_scaled", 2)
        sums = s.counter("sums")
        high_sums = s.counter("high_sums")
        summed = s.counter("summed", 1)
        block = s.block()

        def in_turns(eng, turn):
            turn(0, at_first=True)
            with eng.Fori(1, QUARTERS - 1) as i:
                turn(i)
            turn(QUARTERS - 1, at_last=True)

        @block.gpsimd
        def _(pool):
            def take_gates(i, b):
                nc.gpsimd.tensor_copy(gates[:, b, :, :], wt[:, bass.ds(TPG * i + BTILES * b, TPG), 0:E]).then_inc(gates_in.sem, 1)

            def split_y(i, b):
                pool.wait_ge(copied.sem, copied.ready(2 * i + b))
                nc.gpsimd.tensor_tensor(y_low[:, b, :], yt[:, bass.ds(GROUP * i + SEQ * b, GROUP)], y_high[:, b, :].bitcast(F32),
                                        ALU.subtract).then_inc(split.sem, 1)

            def turn(i, at_first=False, at_last=False):
                for b in range(2):
                    u = 2 * i + b
                    if b == 0:
                        split_y(i, 1)
                    elif not at_last:
                        split_y(i + 1, 0)
                    upper = terms[:, b, :, H:E, :]
                    pool.wait_ge(high_scaled.sem, high_scaled.ready(TPG * u + TPG - 1))
                    nc.gpsimd.tensor_tensor(upper[:, :, 0:2, :], upper[:, :, 0:2, :], upper[:, :, 2:4, :], ALU.add)\
                        .then_inc(high_sums.sem, 1)
                    pool.wait_ge(high_sums.sem, high_sums.ready(2 * u))
                    nc.gpsimd.tensor_tensor(upper[:, :, 0, :], upper[:, :, 0, :], upper[:, :, 1, :], ALU.add)\
                        .then_inc(high_sums.sem, 1)
                    if not at_last:
                        pool.wait_ge(low_scaled.sem, low_scaled.ready(TPG * u + TPG - 1))
                        take_gates(i + 1, b)

            take_gates(0, 0)
            take_gates(0, 1)
            split_y(0, 0)
            in_turns(pool, turn)

        @block.scalar
        def _(act):
            act.sem_inc(high_scaled.sem, 2)

            def copies(i, b):
                act.wait_ge(products.sem, products.ready(TPG * (2 * i + b) - 1) - TPG)
                nc.scalar.activation(wg[:, b, :], wtt[:, bass.ds(i + QUARTERS * b, 1), :].rearrange("p a n -> p (a n)"), ACT.Copy)
                nc.scalar.activation(y_high[:, b, :], yt[:, bass.ds(GROUP * i + SEQ * b, GROUP)], ACT.Copy)\
                    .then_inc(copied.sem, 1)

            def turn(i, at_first=False, at_last=False):
                for b in range(2):
                    u = 2 * i + b
                    if b == 0:
                        copies(i, 1)
                    elif not at_last:
                        copies(i + 1, 0)
                    act.wait_ge(gates_in.sem, gates_in.ready(u))
                    if not (at_first and b < 1):
                        act.wait_ge(summed.sem, summed.free(u, 2))
                    for t in range(TPG):
                        act.wait_ge(products.sem, products.ready(TPG * u + t))
                        for e in range(H, E):
                            last = nc.scalar.activation(terms[:, b, t, e, :], p_e[:, t % 2, e, :], ACT.Identity,
                                                        scale=gates[:, b, t, e:e + 1])
                        last.then_inc(high_scaled.sem, 1)

            copies(0, 0)
            in_turns(act, turn)

        @block.tensor
        def _(pe):
            pe.sem_inc(products.sem, TPG)
            with pe.Fori(0, QUARTERS) as i:
                for b in range(2):
                    u = 2 * i + b
                    pe.wait_ge(split.sem, split.ready(u))
                    pe.wait_ge(started.sem, started.free(u))
                    nc.tensor.matmul(p_b[:, b, :], wg[:, b, :], g.b12[:, :, :].rearrange("p t d -> p (t d)"),
                                     start=True, stop=True).then_inc(biases.sem, 1)
                    for t in range(TPG):
                        k = TPG * u + t
                        for half, taken in enumerate((low_scaled, high_scaled)):
                            pe.wait_ge(taken.sem, taken.free(k))
                            for y, w12 in ((y_high, g.w12_high), (y_low, g.w12_high), (y_high, g.w12_low)):
                                last = nc.tensor.matmul(p_e[:, t % 2, half * H:(half + 1) * H, :].rearrange("p e d -> p (e d)"),
                                                        y[:, b, t * P:(t + 1) * P],
                                                        w12[:, half * H:(half + 1) * H, :].rearrange("p e d -> p (e d)"),
                                                        start=(w12 is g.w12_high and y is y_high), stop=(w12 is g.w12_low))
                        last.then_inc(products.sem, 1)

        @block.vector
        def _(dve):
            dve.sem_inc(started.sem, 2)
            dve.sem_inc(low_scaled.sem, 2)
            dve.sem_inc(summed.sem, 1)

            def start(i, b):
                u = 2 * i + b
                dve.wait_ge(biases.sem, biases.ready(u))
                nc.vector.tensor_tensor(base[:, b, :, :], p_b[:, b, :].rearrange("p (t d) -> p t d", d=D), btiles(z, b, i),
                                        ALU.add).then_inc(started.sem, 1)
                dve.wait_ge(gates_in.sem, gates_in.ready(u))

            def scale(i, b, t):
                dve.wait_ge(products.sem, products.ready(TPG * (2 * i + b) + t))
                nc.vector.tensor_tensor(terms[:, b, t, 0:H, :], p_e[:, t % 2, 0:H, :], over(gates[:, b, t, 0:H], D), ALU.mult)\
                    .then_inc(low_scaled.sem, 1)

            def add(i, b, k):
                u = 2 * i + b
                if k == 0:
                    dve.wait_ge(low_scaled.sem, low_scaled.ready(TPG * u + TPG - 1))
                    nc.vector.tensor_tensor(terms[:, b, :, 0:2, :], terms[:, b, :, 0:2, :], terms[:, b, :, 2:4, :], ALU.add)\
                        .then_inc(sums.sem, 1)
                elif k < 3:
                    dve.wait_ge(started.sem, started.ready(u))
                    dve.wait_ge(sums.sem, sums.ready(3 * u + k - 1))
                    nc.vector.tensor_tensor(base[:, b, :, :], base[:, b, :, :], terms[:, b, :, k - 1, :], ALU.add)\
                        .then_inc(sums.sem, 1)
                else:
                    dve.wait_ge(sums.sem, sums.ready(3 * u + 2))
                    dve.wait_ge(high_sums.sem, high_sums.ready(2 * u + 1))
                    nc.vector.tensor_tensor(btiles(z, b, i), base[:, b, :, :], terms[:, b, :, H, :], ALU.add)\
                        .then_inc(summed.sem, 1)

            def turn(i, at_first=False, at_last=False):
                for b in range(2):
                    if not (at_first and b == 0):
                        before = (i, 0) if b else (i - 1, 1)
                    if not at_first:
                        dve.wait_ge(summed.sem, summed.free(2 * i + b, 2))
                    start(i, b)
                    for t in range(TPG):
                        scale(i, b, t)
                        if not (at_first and b == 0):
                            add(*before, t)

            in_turns(dve, turn)
            for k in range(4):
                add(QUARTERS - 1, 1, k)


def add_normed(nc, tag, g, z, mean, rstd, x, out=None):
    w = g.w2
    PART = 8
    PARTS = TILES // PART
    with Scope(nc, tag) as s:
        centred, scaled, shifted, added, stored = (s.sem(n) for n in ("centred", "scaled", "shifted", "added", "stored"))
        block = s.block()
        wide = lambda r: r.unsqueeze(1).to_broadcast([P, PART, D])
        part = lambda buf, q: buf[:, q * PART:(q + 1) * PART, :]

        @block.vector
        def _(dve):
            def centre(q):
                for t in range(q * PART, (q + 1) * PART):
                    last = nc.vector.tensor_scalar(z[:, t, :], z[:, t, :], mean[:, t:t + 1], rstd[:, t:t + 1],
                                                   ALU.subtract, ALU.mult)
                last.then_inc(centred, 1)

            centre(0)
            for q in range(PARTS):
                if q + 1 < PARTS:
                    centre(q + 1)
                dve.wait_ge(scaled, q + 1)
                nc.vector.tensor_tensor(part(z, q), part(z, q), wide(w["ln2_b"]), ALU.add).then_inc(shifted, 1)
                dve.wait_ge(shifted, q + 1)
                nc.vector.scalar_tensor_tensor(part(x, q), part(z, q), 0.5, part(x, q), ALU.mult, ALU.add).then_inc(added, 1)

        @block.gpsimd
        def _(pool):
            for q in range(PARTS):
                pool.wait_ge(centred, q + 1)
                nc.gpsimd.tensor_tensor(part(z, q), part(z, q), wide(w["ln2_g"]), ALU.mult).then_inc(scaled, 1)

        if out is not None:
            @block.sync
            def _(sp):
                for q in range(PARTS):
                    sp.wait_ge(added, q + 1)
                    sp.dma_start(part(out.rearrange("b (t p) d -> p (b t) d", p=P), q), part(x, q)).then_inc(stored, 16)
                sp.wait_ge(stored, 16 * PARTS)



IH, ID = 4, 64
TOPK = 32
TIE = 2.0 ** -120
NONE = -3.0e38
MASKED = -1.0e30
HALF = SEQ // 2
SCALE = float(1 / np.sqrt(np.float32(D)))


def sparse_attention(nc, tag, g, x):
    with Scope(nc, tag) as s:
        mean, rstd = s.sb("mean", [P, TILES]), s.sb("rstd", [P, TILES])
        row_stats(nc, tag + "s", g.stats, mean, [(rstd, LN_EPS, True)], x)
        qt, kt = s.sb("qt", [P, SEQ]), s.sb("kt", [P, SEQ])
        v = s.sb("v", [P, BTILES, D])
        iqt = s.sb("iqt", [P, IH, SEQ])
        ikt = s.sb("ikt", [P, 2, SEQ], F32R)
        iw = s.sb("iw", [P, BTILES, IH])
        g.tiebreak = s.sb("tiebreak", [P, SEQ])
        g.cos, g.sin = s.sb("cos", [P, SEQ]), s.sb("sin", [P, SEQ])
        g.tables_in = s.sem("tables_in")
        attention_constants(nc, tag + "t", g)
        for b in range(2):
            attention_project(nc, f"{tag}p{b}", g, b, x, mean, rstd, qt, kt, v, iqt, ikt, iw)
            attention_select(nc, f"{tag}a{b}", g, b, x, qt, kt, v, iqt, ikt, iw)


def attention_constants(nc, tag, g):
    with Scope(nc, tag) as s:
        made = s.sem("made")
        block = s.block()

        @block.sync
        def _(sp):
            sp.wait_ge(g.pack_in[3], 16)
            for table, source in ((g.cos, g.angles[0]), (g.sin, g.angles[1])):
                sp.dma_start(table[:, :], source).then_inc(g.tables_in, 16)

        @block.gpsimd
        def _(pool):
            link = Chain(pool, made)
            link(nc.gpsimd.iota(g.tiebreak[:, :], pattern=[[1, SEQ]], base=1, channel_multiplier=0,
                                allow_small_or_imprecise_dtypes=True))
            link(nc.gpsimd.tensor_scalar(g.tiebreak[:, :], g.tiebreak[:, :], -TIE, None, ALU.mult))


def attention_project(nc, tag, g, b, x, mean, rstd, qt, kt, v, iqt, ikt, iw):
    w = g.w3
    with Scope(nc, tag) as s:
        zs = s.sb("zs", [P, 2, TPG, D])
        zg = s.sb("zg", [P, 2, GROUP])
        zh, zl = (s.sb(n, [P, 2, GROUP], F32R) for n in ("zh", "zl"))
        w_high, w_low = (s.sb(n, [P, (4 + IH + 1) * P], F32R) for n in ("w_high", "w_low"))
        rot = s.sb("rot", [P, 2, 2, GROUP])
        p_x = s.ps("p_x", [P, 2, GROUP])
        p_qk = s.ps("p_qk", [P, 2, GROUP])
        p_i = s.ps("p_i", [P, 2, GROUP])
        p_v = s.ps("p_v", [P, GROUP])
        p_w = s.ps("p_w", [P, TPG * IH])
        normalized = s.counter("normalized")
        transposed = s.counter("transposed", 2)
        copied = s.counter("copied")
        w_high_kept, w_split = s.sem("w_high_kept"), s.sem("w_split")
        high_kept = s.counter("high_kept")
        split = s.counter("split", 2)
        turned = s.counter("turned")
        rotated = s.counter("rotated", 2)
        summed = s.counter("summed", 2)
        indexed = s.counter("indexed")
        index_kept = s.counter("index_kept", 2)
        low_kept = s.counter("low_kept", 1)
        valued = s.counter("valued")
        value_kept = s.counter("value_kept", 1)
        weighed = s.counter("weighed", 2)
        weight_kept = s.counter("weight_kept", 1)
        block = s.block()
        NI = IH + 1

        def in_turns(eng, turn):
            with eng.Fori(0, QUARTERS // 2 - 1) as i:
                for h in range(2):
                    turn(2 * i + h, h, 2)
            for h in range(2):
                turn(QUARTERS - 2 + h, h, 1 - h)

        @block.vector
        def _(dve):
            dve.sem_inc(rotated.sem, 2)
            dve.sem_inc(summed.sem, 2)
            dve.sem_inc(value_kept.sem, 1)
            dve.sem_inc(weight_kept.sem, 1)
            dve.sem_inc(low_kept.sem, 1)
            dve.sem_inc(split.sem, 2)

            def normalize(u, h):
                dve.wait_ge(transposed.sem, transposed.free(u))
                for t in range(TPG):
                    last = nc.vector.tensor_scalar(zs[:, h, t:t + 1, :], btiles(x, b, u, t, 1), bcol(mean, b, u, t),
                                                   bcol(rstd, b, u, t), ALU.subtract, ALU.mult)
                last.then_inc(normalized.sem, 1)

            def low(u, h):
                dve.wait_ge(high_kept.sem, high_kept.ready(u))
                nc.vector.tensor_tensor(zl[:, h, :], p_x[:, h, :], zh[:, h, :].bitcast(F32), ALU.subtract).then_inc(split.sem, 1)

            def keep_values(u):
                dve.wait_ge(valued.sem, valued.ready(u))
                nc.vector.tensor_tensor(v[:, bass.ds(TPG * u, TPG), :], p_v[:, :].rearrange("p (t d) -> p t d", d=D),
                                        w["v_b"].unsqueeze(1).to_broadcast([P, TPG, D]), ALU.add).then_inc(value_kept.sem, 1)
                dve.wait_ge(weighed.sem, weighed.ready(u))
                nc.vector.tensor_tensor(iw[:, bass.ds(TPG * u, TPG), :], p_w[:, :].rearrange("p (t h) -> p t h", h=IH),
                                        w["iw_b"].unsqueeze(1).to_broadcast([P, TPG, IH]), ALU.add).then_inc(weight_kept.sem, 1)

            def rotate(u, m, out):
                dve.wait_ge(summed.sem, summed.free(2 * u + m))
                for part, table in enumerate((g.cos, g.sin)):
                    n = 2 * m + part
                    dve.wait_ge(turned.sem, turned.ready(4 * u + n))
                    nc.vector.scalar_tensor_tensor(rot[:, m, part, :], p_qk[:, part, :], w["qk_b"][:, n:n + 1],
                                                   table[:, bass.ds(GROUP * u, GROUP)], ALU.add, ALU.mult)\
                        .then_inc(rotated.sem, 1)
                dve.wait_ge(rotated.sem, rotated.ready(4 * u + 2 * m + 1))
                nc.vector.tensor_tensor(out[:, bass.ds(GROUP * u, GROUP)], rot[:, m, 0, :], rot[:, m, 1, :],
                                        ALU.add).then_inc(summed.sem, 1)

            def keys_low(u, h):
                high = ikt[:, 0, bass.ds(GROUP * u, GROUP)]
                dve.wait_ge(index_kept.sem, index_kept.ready(NI * u + IH))
                nc.vector.scalar_tensor_tensor(ikt[:, 1, bass.ds(GROUP * u, GROUP)], p_i[:, (h + IH) % 2, :],
                                               w["iqk_b"][:, IH:IH + 1], high.bitcast(F32), ALU.add, ALU.subtract)\
                    .then_inc(low_kept.sem, 1)

            def turn(u, h, ahead):
                keep_values(u)
                if ahead > 1:
                    normalize(u + 2, h)
                rotate(u, 0, qt)
                if ahead > 0:
                    low(u + 1, 1 - h)
                rotate(u, 1, kt)
                keys_low(u, h)

            for h in range(2):
                normalize(h, h)
            low(0, 0)
            dve.wait_ge(g.tables_in, 32)
            in_turns(dve, turn)

        @block.gpsimd
        def _(pool):
            pool.wait_ge(w_high_kept, 1)
            nc.gpsimd.tensor_tensor(w_low[:, :], w["qk_iqk"], w_high[:, :].bitcast(F32), ALU.subtract).then_inc(w_split, 1)
            with pool.Fori(0, QUARTERS) as u:
                pool.wait_ge(normalized.sem, normalized.ready(u))
                nc.gpsimd.tensor_tensor(btiles(x, b, u), btiles(x, b, u), w["o_b"].unsqueeze(1).to_broadcast([P, TPG, D]), ALU.add)

        @block.tensor
        def _(pe):
            pe.sem_inc(transposed.sem, 2)
            pe.sem_inc(weighed.sem, 2)

            def transpose(u, h):
                pe.wait_ge(normalized.sem, normalized.ready(u))
                pe.wait_ge(split.sem, split.free(u))
                for t in range(TPG):
                    last = nc.tensor.transpose(p_x[:, h, t * P:(t + 1) * P], zs[:, h, t, :], g.ident)
                last.then_inc(transposed.sem, 1)

            def product(h, n, out):
                part = slice(n * P, (n + 1) * P)
                nc.tensor.matmul(out, w_high[:, part], zh[:, h, :], start=True, stop=False)
                nc.tensor.matmul(out, w_high[:, part], zl[:, h, :], start=False, stop=False)
                return nc.tensor.matmul(out, w_low[:, part], zh[:, h, :], start=False, stop=True)

            def turn(u, h, ahead):
                if ahead > 0:
                    transpose(u + 1, 1 - h)
                pe.wait_ge(copied.sem, copied.ready(u))
                pe.wait_ge(value_kept.sem, value_kept.free(u))
                for t in range(TPG):
                    last = nc.tensor.matmul(p_v[:, t * D:(t + 1) * D], zg[:, h, t * P:(t + 1) * P], w["v"], start=True, stop=True)
                last.then_inc(valued.sem, 1)
                pe.wait_ge(weight_kept.sem, weight_kept.free(u))
                for t in range(TPG):
                    last = nc.tensor.matmul(p_w[:, t * IH:(t + 1) * IH], zg[:, h, t * P:(t + 1) * P], w["iw"], start=True, stop=True)
                last.then_inc(weighed.sem, 1)
                pe.wait_ge(split.sem, split.ready(u))
                pe.wait_ge(w_split, 1)
                for n in range(NI):
                    if n < 4:
                        pe.wait_ge(rotated.sem, rotated.free(4 * u + n))
                        product(h, n, p_qk[:, n % 2, :]).then_inc(turned.sem, 1)
                    pe.wait_ge(index_kept.sem, index_kept.free(NI * u + n))
                    if n == 1:
                        pe.wait_ge(low_kept.sem, low_kept.free(u))
                    product(h, 4 + n, p_i[:, (h + n) % 2, :]).then_inc(indexed.sem, 1)

            transpose(0, 0)
            in_turns(pe, turn)

        @block.scalar
        def _(act):
            act.sem_inc(index_kept.sem, 2)
            nc.scalar.activation(w_high[:, :], w["qk_iqk"], ACT.Copy).then_inc(w_high_kept, 1)

            def copies(u, h):
                act.wait_ge(transposed.sem, transposed.ready(u))
                act.wait_ge(weighed.sem, weighed.free(u))
                nc.scalar.activation(zg[:, h, :], p_x[:, h, :], ACT.Copy).then_inc(copied.sem, 1)
                nc.scalar.activation(zh[:, h, :], p_x[:, h, :], ACT.Copy).then_inc(high_kept.sem, 1)

            def keep_index(u, h, n):
                part = bass.ds(GROUP * u, GROUP)
                out = ikt[:, 0, part] if n == IH else iqt[:, n, part]
                act.wait_ge(indexed.sem, indexed.ready(NI * u + n))
                nc.scalar.activation(out, p_i[:, (h + n) % 2, :], ACT.Identity, bias=w["iqk_b"][:, n:n + 1]).then_inc(index_kept.sem, 1)

            def turn(u, h, ahead):
                for n in range(2):
                    keep_index(u, h, n)
                if ahead > 0:
                    copies(u + 1, 1 - h)
                for n in range(2, NI):
                    keep_index(u, h, n)

            copies(0, 0)
            in_turns(act, turn)


def attention_select(nc, tag, g, b, x, qt, kt, v, iqt, ikt, iw):
    w = g.w3
    UNITS = 2 * IH
    SUMS = UNITS - 2
    EARLY = 6
    SPAN = 64
    SPANS = SEQ // SPAN
    ROUNDS = TOPK // 8
    N = BTILES
    with Scope(nc, tag) as s:
        iqs = s.sb("iqs", [P, IH, P], F32R)
        qs = s.sb("qs", [P, P])
        relu = s.sb("relu", [P, UNITS, HALF])
        score = s.sb("score", [P, SEQ])
        tiebreak = g.tiebreak
        cand = s.sb("cand", [P, SPANS, 8])
        best = s.sb("best", [P, 8])
        after = s.sb("after", [P, 8])
        prob = s.sb("prob", [P, SEQ])
        probt = s.sb("probt", [P, SEQ])
        first_weight, half_most, most, bias, total, inv, eighth, unsure = (
            s.sb(n, [P, 1]) for n in ("first_weight", "half_most", "most", "bias", "total", "inv", "eighth", "unsure"))
        unsure_row = s.sb("unsure_row", [1, P])
        again = s.sb("again", [1, 1], U32)
        ot = s.sb("ot", [P, P])
        p_s = s.ps("p_s", [P, 2, HALF])
        p_l = s.ps("p_l", [P, SEQ])
        rounded = s.counter("rounded")
        index_queries = s.counter("index_queries")
        queries = s.counter("queries")
        scored = s.counter("scored")
        logits = s.counter("logits", 1)
        rectified = s.counter("rectified", 2)
        weighed = s.counter("weighed")
        first_head = s.counter("first_head")
        added = s.counter("added", SUMS)
        vdone = s.sem("vdone")
        row_max = s.counter("row_max")
        flagged = s.counter("flagged")
        flags_in = s.sem("flags_in")
        masked = s.counter("masked")
        exped = s.counter("exped")
        prob_t = s.counter("prob_t")
        prob_t_kept = s.counter("prob_t_kept")
        attended = s.counter("attended", 1)
        inverted = s.counter("inverted")
        o_kept = s.counter("o_kept")
        projected = s.counter("projected")
        finished = s.counter("finished", 1)
        block = s.block()

        def weight(n, h):
            return iw[:, bass.ds(n, 1), h]

        def in_turn(eng, first, second):
            first(0, None)
            with eng.Fori(1, N - 1) as n:
                first(n, second)
            first(N - 1, second, at_last=True)
            second(N - 1)

        @block.gpsimd
        def _(pool):
            def index_part(n):
                nc.gpsimd.tensor_copy(first_weight[:, :], weight(n, 0))
                nc.gpsimd.tensor_copy(iqs[:, :, :], iqt[:, :, bass.ds(P * n, P)]).then_inc(rounded.sem, 1)
                pool.wait_ge(rounded.sem, rounded.ready(n))
                low = iqs[ID:P, :, :]
                nc.gpsimd.tensor_tensor(low, iqt[ID:P, :, bass.ds(P * n, P)], low.bitcast(F32), ALU.subtract)\
                    .then_inc(index_queries.sem, 1)
                pool.wait_ge(index_queries.sem, index_queries.ready(n))

            def query_part(n):
                pool.wait_ge(logits.sem, logits.free(n))
                nc.gpsimd.tensor_copy(qs[:, :], qt[:, bass.ds(P * n, P)]).then_inc(queries.sem, 1)

            def break_ties(n):
                for half in range(2):
                    part = relu[:, half, :]
                    pool.wait_ge(weighed.sem, weighed.ready(2 * n + half))
                    nc.gpsimd.tensor_tensor(part, part, tiebreak[:, half * HALF:(half + 1) * HALF], ALU.add).then_inc(first_head.sem, 1)

            index_part(0)
            query_part(0)
            break_ties(0)
            with pool.Fori(1, N) as n:
                pool.wait_ge(scored.sem, scored.ready(UNITS * n - 1))
                index_part(n)
                break_ties(n)
                query_part(n)

        @block.sync
        def _(sp):
            with sp.Fori(0, N) as n:
                sp.wait_ge(flagged.sem, flagged.ready(n))
                sp.dma_start(unsure_row[:, :], unsure[:, :]).then_inc(flags_in, 16)

        @block.tensor
        def _(pe):
            pe.sem_inc(logits.sem, 1)
            pe.sem_inc(attended.sem, 1)

            def score_units(n, units):
                for k in units:
                    h, half = divmod(k, 2)
                    pe.wait_ge(rectified.sem, rectified.free(UNITS * n + k))
                    for part in range(2):
                        for c in range(HALF // GROUP):
                            at = half * HALF + c * GROUP
                            last = nc.tensor.matmul(p_s[:, k % 2, c * GROUP:(c + 1) * GROUP], iqs[:, h, :],
                                                    ikt[:, part, at:at + GROUP], start=(part == 0), stop=(part == 1))
                    last.then_inc(scored.sem, 1)

            def begin(n):
                pe.wait_ge(index_queries.sem, index_queries.ready(n))
                score_units(n, range(2))

            def select(n, then, at_last=False):
                score_units(n, range(2, UNITS))
                if then is not None:
                    then(n - 1)
                if not at_last:
                    begin(n + 1)
                pe.wait_ge(queries.sem, queries.ready(n))
                pe.wait_ge(finished.sem, finished.free(n))
                for c in range(SEQ // GROUP):
                    last = nc.tensor.matmul(p_l[:, c * GROUP:(c + 1) * GROUP], qs[:, :], kt[:, c * GROUP:(c + 1) * GROUP],
                                            start=True, stop=True)
                last.then_inc(logits.sem, 1)

            def attend(n):
                pe.wait_ge(exped.sem, exped.ready(n))
                for half in range(2):
                    for k in range(half * N // 2, (half + 1) * N // 2):
                        last = nc.tensor.transpose(p_l[:, k * P:(k + 1) * P], prob[:, k * P:(k + 1) * P], g.ident)
                    last.then_inc(prob_t.sem, 1)
                pe.wait_ge(prob_t_kept.sem, prob_t_kept.ready(2 * n + 1))
                for k in range(N):
                    last = nc.tensor.matmul(p_l[:, 0:P], v[:, k, :], probt[:, k * P:(k + 1) * P],
                                            start=(k == 0), stop=(k == N - 1))
                last.then_inc(attended.sem, 1)
                pe.wait_ge(o_kept.sem, o_kept.ready(n))
                nc.tensor.matmul(p_l[:, GROUP:GROUP + D], ot[:, :], w["o"], start=True, stop=True).then_inc(projected.sem, 1)

            begin(0)
            in_turn(pe, select, attend)

        @block.scalar
        def _(act):
            act.sem_inc(rectified.sem, 2)

            def rectify(n, units):
                for k in units:
                    act.wait_ge(scored.sem, scored.ready(UNITS * n + k))
                    act.wait_ge(added.sem, added.free(SUMS * n + (k if k < 2 else k - 2)))
                    nc.scalar.activation(relu[:, k, :], p_s[:, k % 2, :], ACT.Relu).then_inc(rectified.sem, 1)

            def weigh_first_head(n):
                for half in range(2):
                    act.wait_ge(rectified.sem, rectified.ready(UNITS * n + half))
                    nc.scalar.activation(relu[:, half, :], relu[:, half, :], ACT.Copy, scale=first_weight[:, :]).then_inc(weighed.sem, 1)

            def exponentials(n):
                act.wait_ge(masked.sem, masked.ready(n))
                nc.scalar.activation(prob[:, :], prob[:, :], ACT.Exp, bias=bias[:, :], accum_out=total[:, :]).then_inc(exped.sem, 1)

            def copies(n):
                act.wait_ge(attended.sem, attended.free(n))
                for half in range(2):
                    act.wait_ge(prob_t.sem, prob_t.ready(2 * n + half))
                    part = slice(half * HALF, (half + 1) * HALF)
                    nc.scalar.activation(probt[:, part], p_l[:, part], ACT.Copy).then_inc(prob_t_kept.sem, 1)
                act.wait_ge(attended.sem, attended.ready(n))
                nc.scalar.activation(ot[:, :], p_l[:, 0:P], ACT.Copy).then_inc(o_kept.sem, 1)

            def begin(n):
                rectify(n, range(2))
                weigh_first_head(n)

            def select(n, then, at_last=False):
                rectify(n, range(2, EARLY))
                if then is not None:
                    exponentials(n - 1)
                rectify(n, range(EARLY, UNITS))
                if then is not None:
                    copies(n - 1)
                if not at_last:
                    begin(n + 1)

            def attend(n):
                exponentials(n)
                copies(n)

            begin(0)
            in_turn(act, select, attend)

        @block.vector
        def _(dve):
            dve.sem_inc(added.sem, SUMS)
            dve.sem_inc(finished.sem, 1)

            def select(n, then, at_last=False):
                steps = [0]

                def link(ins):
                    steps[0] += 1
                    ins.then_inc(vdone, 1)
                    dve.wait_ge(vdone, steps[0])

                def restart():
                    dve.sem_clear(vdone)
                    steps[0] = 0

                for k in range(2, UNITS):
                    h, half = divmod(k, 2)
                    part = score[:, half * HALF:(half + 1) * HALF]
                    step = SUMS * n + k - 2
                    dve.wait_ge(rectified.sem, rectified.ready(UNITS * n + k))
                    if h == 1:
                        dve.wait_ge(first_head.sem, first_head.ready(2 * n + half))
                    else:
                        dve.wait_ge(added.sem, added.ready(step - 2))
                    nc.vector.scalar_tensor_tensor(part, relu[:, k, :], weight(n, h), relu[:, half, :] if h == 1 else part,
                                                   ALU.mult, ALU.add).then_inc(added.sem, 1)
                dve.wait_ge(added.sem, added.ready(SUMS * n + SUMS - 1))
                dve.sem_inc(vdone, 1)
                restart()
                for k in range(SPANS):
                    last = nc.vector.max(cand[:, k, :], score[:, :].rearrange("p (j k) -> p k j", k=SPANS)[:, k, :])
                link(last)
                if then is not None:
                    then(n - 1)
                link(nc.vector.tensor_reduce(eighth[:, :], cand[:, :, 7], AX, ALU.max))
                every = cand[:, :, :].rearrange("p g k -> p (g k)")
                for r in range(ROUNDS):
                    link(nc.vector.max(best[:, :], every))
                    link(nc.vector.match_replace(every, best[:, :], every, NONE))
                link(nc.vector.max(after[:, :], every))
                nc.vector.scalar_tensor_tensor(unsure[:, :], after[:, 0:1], eighth[:, :], best[:, 7:8], ALU.max, ALU.is_ge)\
                    .then_inc(flagged.sem, 1)
                if then is not None:
                    dve.wait_ge(prob_t.sem, prob_t.ready(2 * n - 1))
                nc.vector.tensor_scalar(prob[:, :], score[:, :], best[:, 7:8], MASKED, ALU.is_lt, ALU.mult).then_inc(vdone, 1)
                dve.wait_ge(logits.sem, logits.ready(n))
                dve.sem_inc(vdone, 1)
                steps[0] += 2
                dve.wait_ge(vdone, steps[0])
                link(masked_logits(0, NONE))
                dve.wait_ge(flags_in, 16 * n + 16)
                nc.vector.tensor_reduce(again[:, :], unsure_row[:, :], AX, ALU.max).then_inc(vdone, 1)
                masked_logits(1, half_most[:, :]).then_inc(row_max.sem, 1)
                steps[0] += 1
                dve.wait_ge(vdone, steps[0])
                restart()
                with dve.If(dve.value_load(again[0:1, 0:1], min_val=0, max_val=1) != 0):
                    dve.wait_ge(row_max.sem, row_max.ready(n))
                    dve.sem_inc(vdone, 1)
                    restart()
                    for r in range(ROUNDS):
                        link(nc.vector.max(best[:, :], score[:, :]))
                        link(nc.vector.match_replace(score[:, :], best[:, :], score[:, :], NONE))
                    link(nc.vector.tensor_scalar(prob[:, :], score[:, :], NONE / 2, MASKED, ALU.is_gt, ALU.mult))
                    link(masked_logits(0, NONE))
                    link(masked_logits(1, half_most[:, :]))
                    restart()
                dve.wait_ge(row_max.sem, row_max.ready(n))
                nc.vector.tensor_scalar(bias[:, :], most[:, :], -1.0, None, ALU.mult).then_inc(masked.sem, 1)

            def masked_logits(half, most_before):
                part = slice(half * HALF, (half + 1) * HALF)
                return nc.vector.tensor_tensor_reduce(out=prob[:, part], in0=prob[:, part], in1=p_l[:, part], scale=SCALE,
                                                      scalar=most_before, op0=ALU.add, op1=ALU.max,
                                                      accum_out=(most if half else half_most)[:, :])

            def finish_rows(n):
                dve.wait_ge(exped.sem, exped.ready(n))
                nc.vector.reciprocal(inv[:, :], total[:, :]).then_inc(inverted.sem, 1)
                dve.wait_ge(inverted.sem, inverted.ready(n))
                dve.wait_ge(projected.sem, projected.ready(n))
                rows = x[:, bass.ds(n + N * b, 1), :].rearrange("p a d -> p (a d)")
                nc.vector.scalar_tensor_tensor(rows, p_l[:, GROUP:GROUP + D], inv[:, :], rows, ALU.mult, ALU.add)\
                    .then_inc(finished.sem, 1)

            in_turn(dve, select, finish_rows)



PACK0 = dict(wr=E, fw1=FF, fw2=FC * D, fb1=FC, fb2=1)
PACK1 = dict(in_ga=P, in_va=P, in_gr=2 * P, in_vr=2 * P, grow=FF, shrink=2 * P,
             f_aa=P, f_ra=2 * P, f_ar=2 * P, f_rr=P, i_aa=P, i_ra=2 * P, i_ar=2 * P, i_rr=P,
             out_a=P, out_r=2 * P, gamma1=1, gamma2=1, conv_w=8, conv_b=2, b_gates=4, forget_base=2)
PACK2 = dict(qkv=3 * D, out=D, wg=E, b1=E * FC, b2=E, qkv_b=3 * D, out_b=D, ln1_g=D, ln1_b=D, ln2_g=D, ln2_b=D)
PACK3 = dict(qk=4 * D, iqk=(IH + 1) * P, v=D, iw=IH, o=D, qk_b=4, iqk_b=IH + 1, v_b=D, iw_b=IH, o_b=D)


def pack_views(buf, widths, split={}):
    at, views = 0, {}
    for name, n in widths.items():
        view = buf[:, at:at + n]
        if name in split:
            view = view.rearrange("p (c d) -> p c d", c=split[name])
        views[name] = view
        at += n
    return views


def build(nc, io, out):
    with Scope(nc, "g") as g:
        x = g.sb("x", [P, TILES, D])
        pack3 = g.sb("pack3", [P, sum(PACK3.values())])
        g.w3 = pack_views(pack3, PACK3)
        g.w3["qk_iqk"] = pack3[:, 0:(4 + IH + 1) * P]
        g.angles = io["cos"], io["sin"]
        pack2 = g.sb("pack2", [P, sum(PACK2.values())])
        g.w2 = pack_views(pack2, PACK2)
        g.w12_high, g.w12_low = (g.sb(n, [P, E, D], F32R) for n in ("w12_high", "w12_low"))
        g.b12 = g.sb("b12", [P, TPG, D])
        g.carry = g.sb("carry", [P, E * TILES])
        g.stats = g.sb("stats", [P, TILES, 6])
        ident = g.sb("ident", [P, P])
        g.ident = ident[:, :]
        g.upto = g.sb("upto", [P, P], BF16)
        g.ones = g.sb("ones", [P, P], BF16)
        g.one32 = g.sb("one32", [P, TILES])
        g.rank = g.sb("rank", [P, TILES, E])
        g.trash = g.sb("trash", [P, 1])
        g.zeros = g.sb("zeros", [P, D])
        g.pack_in = [g.sem(f"pack_in{k}") for k in range(4)]
        g.cleared = g.sem("cleared")
        g.x_slots = nc.dram_tensor("x_slots", (TRASH + P, D), F32, kind="Internal").ap()
        g.y_slots = nc.dram_tensor("y_slots", (TRASH + P, D), F32, kind="Internal").ap()
        with Scope(nc, "early") as early:
            pack0 = early.sb("pack0", [P, sum(PACK0.values())])
            g.w0 = pack_views(pack0, PACK0, {"fw2": FC})
            g.w0["w1"], g.w0["w2"], g.w0["b12"] = io["w1_top2"], io["w2_top2"], io["b12_top2"]
            pack1 = early.sb("pack1", [P, sum(PACK1.values())])
            g.w1 = pack_views(pack1, PACK1, {n: 2 for n in ("in_gr", "in_vr", "shrink", "f_ra", "f_ar", "i_ra", "i_ar", "out_r")})
            g.w1["in_all"] = pack1[:, 0:6 * P]
            g.decay = early.sb("decay", [P, 2])
            g.tiny = early.sb("tiny", [P, 1])
            setup(nc, g, io, x, (pack0, pack1, pack2, pack3), ident)
            moe_top2(nc, "a", g, x, True, io)
            hawk(nc, "b", g, x)
            moe_top2(nc, "c", g, x, False)
        pair_moe(nc, "d", g, x, False)
        sparse_attention(nc, "e", g, x)
        pair_moe(nc, "k", g, x, True, out)


def setup(nc, g, io, x, packs, ident):
    with Scope(nc, "setup") as s:
        loaded, made, zeroed = (s.sem(n) for n in ("loaded", "made", "zeroed"))
        block = s.block()

        @block.sync
        def _(sp):
            sp.dma_start(x[:, :, :], io["x"].rearrange("b (t p) d -> p (b t) d", p=P)).then_inc(loaded, 16)
            for k, pack in enumerate(packs):
                sp.dma_start(pack[:, :], io[f"pack{k}"]).then_inc(g.pack_in[k], 16)
            sp.wait_ge(loaded, 16)
            sp.wait_ge(g.pack_in[0], 16)

        @block.scalar
        def _(act):
            act.wait_ge(zeroed, 1)
            for e in range(E):
                act.dma_start(g.x_slots[e * CAP0:(e + 1) * CAP0, :].rearrange("(p j) d -> p j d", p=P),
                              g.zeros[:, :].unsqueeze(1).to_broadcast([P, ROWS0, D])).then_inc(g.cleared, 16)
            act.dma_start(g.x_slots[TRASH:TRASH + P, :], g.zeros[:, :]).then_inc(g.cleared, 16)
            act.dma_start(g.y_slots[TRASH:TRASH + P, :], g.zeros[:, :]).then_inc(g.cleared, 16)

        @block.vector
        def _(dve):
            nc.vector.memset(g.zeros[:, :], 0.0).then_inc(zeroed, 1)

        @block.gpsimd
        def _(pool):
            link = Chain(pool, made)
            link(nc.gpsimd.memset(ident[:, :], 0.0))
            link(nc.gpsimd.affine_select(out=ident[:, :], in_=ident[:, :], compare_op=ALU.not_equal, fill=1.0,
                                         base=0, pattern=[[-1, P]], channel_multiplier=1))
            link(nc.gpsimd.memset(g.ones[:, :], 1.0))
            link(nc.gpsimd.memset(g.one32[:, :], 1.0))
            link(nc.gpsimd.affine_select(out=g.upto[:, :], in_=g.ones[:, :], compare_op=ALU.is_ge, fill=0.0,
                                         base=0, pattern=[[1, P]], channel_multiplier=-1))
            link(nc.gpsimd.iota(g.rank[:, :, :], pattern=[[0, TILES], [-1, E]], base=E, channel_multiplier=0,
                                allow_small_or_imprecise_dtypes=True))
            link(nc.gpsimd.memset(g.carry[:, :], 1.0))
            link(nc.gpsimd.memset(g.carry[:, :].rearrange("p (e t) -> p e t", t=TILES)[:, :, 0], 0.0))
            link(nc.gpsimd.iota(g.trash[:, :], pattern=[[0, 1]], base=TRASH, channel_multiplier=1,
                                allow_small_or_imprecise_dtypes=True))


def chunks(a, rows=P):
    return np.concatenate([a[k:k + rows] for k in range(0, a.shape[0], rows)], axis=1)


def lay_out(i):
    cols = lambda v: np.ascontiguousarray(v.reshape(-1, P).T)
    f = {k: np.asarray(v) for k, v in i.items()}
    pack0 = np.concatenate([
        f["L0_ffn_Wr"].T, f["L0_ffn_fw1"], chunks(f["L0_ffn_fw2"]), cols(f["L0_ffn_fb1"]), cols(f["L0_ffn_fb2"])], axis=1)
    rest = lambda a, axis: [np.pad(a, [(0, REST) if k == axis else (0, 0) for k in range(2)]),
                            np.pad(a, [(REST, 0) if k == axis else (0, 0) for k in range(2)])]
    w_in, w_g = f["L0_attn_W_in"].T, f["L0_attn_W_gates"].T
    gate, value = w_in[:, :HID], w_in[:, HID:]
    both = lambda v: np.concatenate([v[:P], v[P:], v[P:]], axis=0).reshape(2, P, -1)
    pair = lambda v: np.concatenate(list(both(v.reshape(HID, -1))), axis=1)
    gates = []
    for m in (w_g[:, :HID], w_g[:, HID:]):
        gates += [m[:P, :P], *rest(m[P:, :P], 0), *rest(m[:P, P:], 1),
                  np.concatenate(rest(m[P:, P:], 1), axis=0)]
    w_out = f["L0_attn_W_out"].T
    pack1 = np.concatenate([
        gate[:, :P], value[:, :P], *rest(gate[:, P:], 1), *rest(value[:, P:], 1), f["L0_attn_W_grow"].T,
        chunks(f["L0_attn_W_shrink"].T), *gates, w_out[:P], *rest(w_out[P:], 0),
        f["L0_attn_gamma1"][:, None], f["L0_attn_gamma2"][:, None], pair(f["L0_attn_conv_w"][:, 0, :]),
        pair(f["L0_attn_conv_b"]), pair(f["L0_attn_b_gates"][:HID]), pair(f["L0_attn_b_gates"][HID:]),
        pair(f["L0_attn_forget_base"])], axis=1)
    rows = lambda v: np.broadcast_to(v[None, :], (P, v.size))
    w1 = f["L1_ffn_w1"]
    pack2 = np.concatenate([
        f["L1_ffn_in_proj_w"].T, f["L1_ffn_out_proj_w"].T, f["L1_ffn_wg"], cols(f["L1_ffn_b1"].reshape(-1)),
        cols(f["L1_ffn_b2"].reshape(-1)), rows(f["L1_ffn_in_proj_b"]), rows(f["L1_ffn_out_proj_b"]),
        rows(f["L1_ffn_ln1_g"]), rows(f["L1_ffn_ln1_b"]), rows(f["L1_ffn_ln2_g"]), rows(f["L1_ffn_ln2_b"])], axis=1)
    q, k, v = np.split(f["L1_attn_w_qkv"], 3)
    q_b, k_b, v_b = np.split(f["L1_attn_b_qkv"], 3)
    swap = lambda a: np.concatenate([a[D // 2:], a[:D // 2]], axis=0)
    twice = lambda a: np.concatenate([a, a], axis=0)
    heads = lambda a: np.concatenate([twice(part) for part in np.split(a, IH)], axis=0)
    pack3 = np.concatenate([
        q.T, swap(q).T, k.T, swap(k).T, heads(f["L1_attn_w_iq"]).T, twice(f["L1_attn_w_ik"]).T, v.T, f["L1_attn_w_iw"].T,
        f["L1_attn_w_o"].T, cols(q_b), cols(swap(q_b)), cols(k_b), cols(swap(k_b)), cols(heads(f["L1_attn_b_iq"])),
        cols(twice(f["L1_attn_b_ik"])), rows(v_b), rows(f["L1_attn_b_iw"]), rows(f["L1_attn_b_o"])], axis=1)
    half = D // 2
    freq = (1.0 / np.float32(10000.0) ** (np.arange(half, dtype=np.float32) / np.float32(half))).astype(np.float32)
    angle = freq[:, None] * np.arange(SEQ, dtype=np.float32)[None, :]
    return {
        "pack3": pack3,
        "cos": twice(np.cos(angle)),
        "sin": np.concatenate([-np.sin(angle), np.sin(angle)], axis=0),
        "pack2": pack2,
        "w1t_top1": chunks(w1.transpose(0, 2, 1).reshape(E * FF, D)),
        "w2_top1": chunks(f["L1_ffn_w2"].reshape(E * FF, D)),
        "pack1": pack1,
        "x": f["L0_attn_x"],
        "pack0": pack0,
        "w1_top2": f["L0_ffn_W1"].reshape(E * D, FF),
        "b12_top2": np.concatenate([np.concatenate([cols(f["L0_ffn_b1"][e]), cols(f["L0_ffn_b2"][e])], axis=1)
                                    for e in range(E)], axis=0),
        "w2_top2": np.concatenate([chunks(f["L0_ffn_W2"][e]) for e in range(E)], axis=0),
    }


def kernel(**inputs):
    import concourse.bacc as bacc
    from concourse.bass_utils import run_bass_kernel_spmd

    nc = bacc.Bacc("TRN2", target_bir_lowering=False, num_devices=1)
    arrays, io = {}, {}
    for name, a in lay_out(inputs).items():
        arrays[name] = np.ascontiguousarray(a)
        io[name] = nc.dram_tensor(name, a.shape, mybir.dt.from_np(a.dtype), kind="ExternalInput").ap()
    out = nc.dram_tensor("out", (BATCH, SEQ, D), F32, kind="ExternalOutput").ap()
    build(nc, io, out)
    r = run_bass_kernel_spmd(nc, [arrays], core_ids=[0])
    return r.results[0]["out"]
```
